# Optimizing a Trainium2 kernel written in Bass

```python
import numpy as np
import jax
import jax.numpy as jnp

def _softmax(x, axis=-1):
    return jax.nn.softmax(x, axis=axis)

def _gelu(x):
    return jax.nn.gelu(x, approximate=True)

def _silu(x):
    return jax.nn.silu(x)

def _sigmoid(x):
    return jax.nn.sigmoid(x)

def _layernorm(x, axis=-1, eps=1e-05):
    m = jnp.mean(x, axis=axis, keepdims=True)
    v = jnp.var(x, axis=axis, keepdims=True)
    return (x - m) / jnp.sqrt(v + eps)

def _scatter_add(tgt, idx, src, axis=0):
    return tgt.at[idx].add(src)

def _segment_sum(src, seg, n):
    return jax.ops.segment_sum(src, seg, n)
kernel_name = 'mk_seq_postln_d2_jaxref_r4_20e1a7'

def setup_inputs(seed: int=0):
    np.random.seed(seed)
    _w = jnp.asarray

    def _L0_attn_setup():
        import jax, jax.numpy as jnp
        import numpy as np
        NUM_HEADS = 8
        D_CONV = 4
        NORMALIZER = 16.0
        LN_EPS = 1e-05

        def _causal_dwconv_silu(x, w):
            xt = jnp.transpose(x, (0, 2, 1))
            y = jax.lax.conv_general_dilated(xt, w[:, None, :], window_strides=(1,), padding=[(w.shape[1] - 1, 0)], feature_group_count=x.shape[-1], dimension_numbers=('NCH', 'OIH', 'NCH'))
            return jnp.transpose(jax.nn.silu(y), (0, 2, 1))

        def _gla(q, k, v, gk, scale):
            B, H, L, Dk = q.shape
            Dv = v.shape[-1]

            def step(S, inp):
                qt, kt, vt, gt = inp
                S = S * jnp.exp(gt)[..., None] + kt[..., None] * vt[..., None, :]
                ot = jnp.einsum('bhk,bhkv->bhv', qt * scale, S)
                return (S, ot)
            mv = lambda a: jnp.moveaxis(a, 2, 0)
            S0 = jnp.zeros((B, H, Dk, Dv), q.dtype)
            _, o = jax.lax.scan(step, S0, (mv(q), mv(k), mv(v), mv(gk)))
            return jnp.moveaxis(o, 0, 2)
        key = jax.random.key(seed)
        ks = jax.random.split(key, 9)
        B, L, E = (4, 512, 256)
        dk = E // 2
        return {'x': jax.random.normal(ks[0], (B, L, E), jnp.float32), 'conv_w': jax.random.normal(ks[1], (E, D_CONV), jnp.float32) * 0.3, 'wq': jax.random.normal(ks[2], (E, dk), jnp.float32) * 0.02, 'wkg': jax.random.normal(ks[3], (E, dk), jnp.float32) * 0.02, 'wv': jax.random.normal(ks[4], (E, E), jnp.float32) * 0.02, 'wg': jax.random.normal(ks[5], (E, E), jnp.float32) * 0.02, 'bg': jax.random.normal(ks[6], (E,), jnp.float32) * 0.02, 'wout': jax.random.normal(ks[7], (E, E), jnp.float32) * 0.02, 'aug_balance': jax.random.normal(ks[8], (dk,), jnp.float32) * 0.1}
    _L0_attn_in = _L0_attn_setup()

    def _L0_ffn_setup():
        import jax, jax.numpy as jnp
        import numpy as np
        TOP_K = 2
        CAP_FACTOR = 1.25
        MIN_CAPACITY = 4
        key = jax.random.key(seed)
        k1, k2, k3, k4 = jax.random.split(key, 4)
        B, T, C, E = (8, 512, 256, 8)
        x = jax.random.normal(k1, (B, T, C), dtype=jnp.float32)
        w_g = jax.random.normal(k2, (E, C), dtype=jnp.float32) * 0.02
        c_fc = jax.random.normal(k3, (E, C, 4 * C), dtype=jnp.float32) * 0.02
        c_proj = jax.random.normal(k4, (E, 4 * C, C), dtype=jnp.float32) * 0.02
        return {'x': x, 'w_g': w_g, 'c_fc': c_fc, 'c_proj': c_proj}
    _L0_ffn_in = _L0_ffn_setup()

    def _L1_attn_setup():
        import jax, jax.numpy as jnp
        import numpy as np
        B, T, D = (4, 512, 256)
        H, Kd = (4, 64)
        Vd = 128
        KEY_DIM, VAL_DIM = (H * Kd, H * Vd)
        CONV = 4
        EPS = 1e-06
        LN_EPS = 1e-05

        def _layernorm(x, g, b):
            m = jnp.mean(x, -1, keepdims=True)
            v = jnp.mean((x - m) ** 2, -1, keepdims=True)
            return (x - m) * jax.lax.rsqrt(v + LN_EPS) * g + b

        def _rmsnorm(x, w):
            return x * jax.lax.rsqrt(jnp.mean(x * x, -1, keepdims=True) + EPS) * w

        def _l2norm(x):
            return x * jax.lax.rsqrt(jnp.sum(x * x, -1, keepdims=True) + EPS)

        def _causal_conv_silu(x, w):
            t = x.shape[1]
            xp = jnp.pad(x, ((0, 0), (CONV - 1, 0), (0, 0)))
            y = xp[:, 0:t, :] * w[:, 0]
            for i in range(1, CONV):
                y = y + xp[:, i:i + t, :] * w[:, i]
            return jax.nn.silu(y)

        def _gated_delta_rule(q, k, v, g, beta):
            qT = jnp.moveaxis(q, 1, 0)
            kT = jnp.moveaxis(k, 1, 0)
            vT = jnp.moveaxis(v, 1, 0)
            gT = jnp.moveaxis(g, 1, 0)
            bT = jnp.moveaxis(beta, 1, 0)
            S0 = jnp.zeros((q.shape[0], H, Kd, Vd), q.dtype)

            def step(S, inp):
                q_t, k_t, v_t, g_t, b_t = inp
                S = S * jnp.exp(g_t)[..., None, None]
                kv = jnp.einsum('bhk,bhkv->bhv', k_t, S)
                delta = (v_t - kv) * b_t[..., None]
                S = S + k_t[..., :, None] * delta[..., None, :]
                o = jnp.einsum('bhk,bhkv->bhv', q_t, S)
                return (S, o)
            _, o = jax.lax.scan(step, S0, (qT, kT, vT, gT, bT))
            return jnp.moveaxis(o, 0, 1)

        def _forward(x, ln1_g, ln1_b, ln2_g, ln2_b, rms_in_w, Wq, Wk, Wv, conv_q_w, conv_k_w, conv_v_w, Wa, dt_bias, A_log, Wb, Wg, o_norm_w, Wo, W2, b2):
            b, t, _ = x.shape
            h = _layernorm(x, ln1_g, ln1_b)
            h = _rmsnorm(h, rms_in_w)
            q = _causal_conv_silu(h @ Wq, conv_q_w).reshape(b, t, H, Kd)
            k = _causal_conv_silu(h @ Wk, conv_k_w).reshape(b, t, H, Kd)
            v = _causal_conv_silu(h @ Wv, conv_v_w).reshape(b, t, H, Vd)
            q = _l2norm(q) * Kd ** (-0.5)
            k = _l2norm(k)
            g = -jnp.exp(A_log) * jax.nn.softplus(h @ Wa + dt_bias)
            beta = jax.nn.sigmoid(h @ Wb)
            o = _gated_delta_rule(q, k, v, g, beta)
            gate = (h @ Wg).reshape(b, t, H, Vd)
            o = _rmsnorm(o, o_norm_w) * jax.nn.silu(gate)
            enc = o.reshape(b, t, VAL_DIM) @ Wo
            x = x + enc
            h2 = _layernorm(x, ln2_g, ln2_b)
            x_out = jax.nn.gelu(h2 @ W2 + b2, approximate=False) + x
            return x_out
        key = jax.random.key(seed)
        ks = jax.random.split(key, 16)
        r = lambda k, shp, s=0.02: jax.random.normal(k, shp, dtype=jnp.float32) * s
        return {'x': jax.random.normal(ks[0], (B, T, D), dtype=jnp.float32), 'ln1_g': jnp.ones((D,), jnp.float32), 'ln1_b': jnp.zeros((D,), jnp.float32), 'ln2_g': jnp.ones((D,), jnp.float32), 'ln2_b': jnp.zeros((D,), jnp.float32), 'rms_in_w': jnp.ones((D,), jnp.float32), 'Wq': r(ks[1], (D, KEY_DIM)), 'Wk': r(ks[2], (D, KEY_DIM)), 'Wv': r(ks[3], (D, VAL_DIM)), 'conv_q_w': r(ks[4], (KEY_DIM, CONV), 0.3), 'conv_k_w': r(ks[5], (KEY_DIM, CONV), 0.3), 'conv_v_w': r(ks[6], (VAL_DIM, CONV), 0.3), 'Wa': r(ks[7], (D, H)), 'dt_bias': r(ks[8], (H,), 0.5), 'A_log': jnp.log(jax.random.uniform(ks[9], (H,), minval=1.0, maxval=16.0)), 'Wb': r(ks[10], (D, H)), 'Wg': r(ks[11], (D, VAL_DIM)), 'o_norm_w': jnp.ones((Vd,), jnp.float32), 'Wo': r(ks[12], (VAL_DIM, D)), 'W2': r(ks[13], (D, D)), 'b2': jnp.zeros((D,), jnp.float32)}
    _L1_attn_in = _L1_attn_setup()

    def _L1_ffn_setup():
        import jax, jax.numpy as jnp
        import numpy as np
        TOP_K = 32
        TEMPERATURE = 1.0
        PARAM_SCALE = 0.02

        def _compose_weight(logits, A, B):
            vals, idx = jax.lax.top_k(logits, TOP_K)
            w = jax.nn.softmax(vals / TEMPERATURE)
            A_sel = A[idx]
            B_sel = B[idx]
            return jnp.einsum('k,kir,kro->io', w, A_sel, B_sel)
        key = jax.random.key(seed)
        ks = jax.random.split(key, 7)
        B, S, D, F, P, R = (2, 256, 256, 1024, 64, 64)
        x = jax.random.normal(ks[0], (B, S, D), dtype=jnp.float32)
        fc1_A = jax.random.normal(ks[1], (P, D, R), dtype=jnp.float32) * PARAM_SCALE
        fc1_B = jax.random.normal(ks[2], (P, R, F), dtype=jnp.float32) * PARAM_SCALE
        fc2_A = jax.random.normal(ks[3], (P, F, R), dtype=jnp.float32) * PARAM_SCALE
        fc2_B = jax.random.normal(ks[4], (P, R, D), dtype=jnp.float32) * PARAM_SCALE
        fc1_logits = jax.random.normal(ks[5], (P,), dtype=jnp.float32)
        fc2_logits = jax.random.normal(ks[6], (P,), dtype=jnp.float32)
        return {'x': x, 'fc1_A': fc1_A, 'fc1_B': fc1_B, 'fc2_A': fc2_A, 'fc2_B': fc2_B, 'fc1_logits': fc1_logits, 'fc2_logits': fc2_logits}
    _L1_ffn_in = _L1_ffn_setup()
    _d = {'L0_attn_x': _L0_attn_in['x'], 'L0_attn_conv_w': _L0_attn_in['conv_w'], 'L0_attn_wq': _L0_attn_in['wq'], 'L0_attn_wkg': _L0_attn_in['wkg'], 'L0_attn_wv': _L0_attn_in['wv'], 'L0_attn_wg': _L0_attn_in['wg'], 'L0_attn_bg': _L0_attn_in['bg'], 'L0_attn_wout': _L0_attn_in['wout'], 'L0_attn_aug_balance': _L0_attn_in['aug_balance'], 'L0_ffn_w_g': _L0_ffn_in['w_g'], 'L0_ffn_c_fc': _L0_ffn_in['c_fc'], 'L0_ffn_c_proj': _L0_ffn_in['c_proj'], 'L1_attn_ln1_g': _L1_attn_in['ln1_g'], 'L1_attn_ln1_b': _L1_attn_in['ln1_b'], 'L1_attn_ln2_g': _L1_attn_in['ln2_g'], 'L1_attn_ln2_b': _L1_attn_in['ln2_b'], 'L1_attn_rms_in_w': _L1_attn_in['rms_in_w'], 'L1_attn_Wq': _L1_attn_in['Wq'], 'L1_attn_Wk': _L1_attn_in['Wk'], 'L1_attn_Wv': _L1_attn_in['Wv'], 'L1_attn_conv_q_w': _L1_attn_in['conv_q_w'], 'L1_attn_conv_k_w': _L1_attn_in['conv_k_w'], 'L1_attn_conv_v_w': _L1_attn_in['conv_v_w'], 'L1_attn_Wa': _L1_attn_in['Wa'], 'L1_attn_dt_bias': _L1_attn_in['dt_bias'], 'L1_attn_A_log': _L1_attn_in['A_log'], 'L1_attn_Wb': _L1_attn_in['Wb'], 'L1_attn_Wg': _L1_attn_in['Wg'], 'L1_attn_o_norm_w': _L1_attn_in['o_norm_w'], 'L1_attn_Wo': _L1_attn_in['Wo'], 'L1_attn_W2': _L1_attn_in['W2'], 'L1_attn_b2': _L1_attn_in['b2'], 'L1_ffn_fc1_A': _L1_ffn_in['fc1_A'], 'L1_ffn_fc1_B': _L1_ffn_in['fc1_B'], 'L1_ffn_fc2_A': _L1_ffn_in['fc2_A'], 'L1_ffn_fc2_B': _L1_ffn_in['fc2_B'], 'L1_ffn_fc1_logits': _L1_ffn_in['fc1_logits'], 'L1_ffn_fc2_logits': _L1_ffn_in['fc2_logits']}
    _x0 = _d['L0_attn_x']
    _d['L0_attn_x'] = jax.random.normal(jax.random.fold_in(jax.random.key(seed), 1), (16, 512, 256), dtype=_x0.dtype)
    del _x0
    return _d

def reference(L0_attn_x, L0_attn_conv_w, L0_attn_wq, L0_attn_wkg, L0_attn_wv, L0_attn_wg, L0_attn_bg, L0_attn_wout, L0_attn_aug_balance, L0_ffn_w_g, L0_ffn_c_fc, L0_ffn_c_proj, L1_attn_ln1_g, L1_attn_ln1_b, L1_attn_ln2_g, L1_attn_ln2_b, L1_attn_rms_in_w, L1_attn_Wq, L1_attn_Wk, L1_attn_Wv, L1_attn_conv_q_w, L1_attn_conv_k_w, L1_attn_conv_v_w, L1_attn_Wa, L1_attn_dt_bias, L1_attn_A_log, L1_attn_Wb, L1_attn_Wg, L1_attn_o_norm_w, L1_attn_Wo, L1_attn_W2, L1_attn_b2, L1_ffn_fc1_A, L1_ffn_fc1_B, L1_ffn_fc2_A, L1_ffn_fc2_B, L1_ffn_fc1_logits, L1_ffn_fc2_logits):

    def _L0_attn_ref(x, conv_w, wq, wkg, wv, wg, bg, wout, aug_balance):
        import jax, jax.numpy as jnp
        import numpy as np
        NUM_HEADS = 8
        D_CONV = 4
        NORMALIZER = 16.0
        LN_EPS = 1e-05

        def _causal_dwconv_silu(x, w):
            xt = jnp.transpose(x, (0, 2, 1))
            y = jax.lax.conv_general_dilated(xt, w[:, None, :], window_strides=(1,), padding=[(w.shape[1] - 1, 0)], feature_group_count=x.shape[-1], dimension_numbers=('NCH', 'OIH', 'NCH'))
            return jnp.transpose(jax.nn.silu(y), (0, 2, 1))

        def _gla(q, k, v, gk, scale):
            B, H, L, Dk = q.shape
            Dv = v.shape[-1]

            def step(S, inp):
                qt, kt, vt, gt = inp
                S = S * jnp.exp(gt)[..., None] + kt[..., None] * vt[..., None, :]
                ot = jnp.einsum('bhk,bhkv->bhv', qt * scale, S)
                return (S, ot)
            mv = lambda a: jnp.moveaxis(a, 2, 0)
            S0 = jnp.zeros((B, H, Dk, Dv), q.dtype)
            _, o = jax.lax.scan(step, S0, (mv(q), mv(k), mv(v), mv(gk)))
            return jnp.moveaxis(o, 0, 2)
        B, L, E = x.shape
        H = NUM_HEADS
        xc = _causal_dwconv_silu(x, conv_w)
        q = xc @ wq
        kg = xc @ wkg
        v = xc @ wv
        g = xc @ wg + bg
        gk = jax.nn.log_sigmoid(kg) / NORMALIZER
        k = 1.0 - jnp.exp(gk)
        dkh = q.shape[-1] // H
        to_heads = lambda t: t.reshape(B, L, H, -1).transpose(0, 2, 1, 3)
        qh, kh, vh, gkh = (to_heads(q), to_heads(k), to_heads(v), to_heads(gk))
        scale = dkh ** (-0.5)
        o = _gla(qh, kh, vh, gkh, scale)
        aug = aug_balance.reshape(H, dkh)
        aug_w = jnp.einsum('bhld,hd,bhld->bhl', qh, aug, kh)
        o = o + jax.nn.sigmoid(aug_w[..., None] * vh)
        mu = o.mean(-1, keepdims=True)
        var = o.var(-1, keepdims=True)
        o = (o - mu) * jax.lax.rsqrt(var + LN_EPS)
        o = o.transpose(0, 2, 1, 3).reshape(B, L, E)
        return jax.nn.silu(g) * o @ wout

    def _L0_ffn_ref(x, w_g, c_fc, c_proj):
        import jax, jax.numpy as jnp
        import numpy as np
        TOP_K = 2
        CAP_FACTOR = 1.25
        MIN_CAPACITY = 4
        B, T, C = x.shape
        E = w_g.shape[0]
        N = B * T
        capacity = max(MIN_CAPACITY, int(CAP_FACTOR * N * TOP_K / E))
        xf = x.reshape(N, C)
        logits = xf @ w_g.T
        top_logits, top_idx = jax.lax.top_k(logits, TOP_K)
        router_probs = jax.nn.softmax(top_logits, axis=-1)
        oh = jax.nn.one_hot(top_idx, E, dtype=jnp.int32)
        oh_t = oh.transpose(1, 0, 2).reshape(TOP_K * N, E)
        pos = jnp.cumsum(oh_t, axis=0).reshape(TOP_K, N, E).transpose(1, 0, 2)
        rank = jnp.sum((pos - 1) * oh, axis=-1)
        valid = rank < capacity
        probs_masked = router_probs * valid.astype(router_probs.dtype)
        rank_c = jnp.clip(rank, 0, capacity - 1)
        contrib = xf[:, None, :] * valid[..., None].astype(xf.dtype)
        buf = jnp.zeros((E, capacity, C), dtype=xf.dtype).at[top_idx, rank_c].add(contrib)
        h = jnp.einsum('ecd,edf->ecf', buf, c_fc)
        h = jnp.square(jax.nn.relu(h))
        expert_out = jnp.einsum('ecf,efd->ecd', h, c_proj)
        gathered = expert_out[top_idx, rank_c]
        out = jnp.sum(gathered * probs_masked[..., None], axis=1)
        return out.reshape(B, T, C)

    def _L1_attn_ref(x, ln1_g, ln1_b, ln2_g, ln2_b, rms_in_w, Wq, Wk, Wv, conv_q_w, conv_k_w, conv_v_w, Wa, dt_bias, A_log, Wb, Wg, o_norm_w, Wo, W2, b2):
        import jax, jax.numpy as jnp
        import numpy as np
        B, T, D = (4, 512, 256)
        H, Kd = (4, 64)
        Vd = 128
        KEY_DIM, VAL_DIM = (H * Kd, H * Vd)
        CONV = 4
        EPS = 1e-06
        LN_EPS = 1e-05

        def _layernorm(x, g, b):
            m = jnp.mean(x, -1, keepdims=True)
            v = jnp.mean((x - m) ** 2, -1, keepdims=True)
            return (x - m) * jax.lax.rsqrt(v + LN_EPS) * g + b

        def _rmsnorm(x, w):
            return x * jax.lax.rsqrt(jnp.mean(x * x, -1, keepdims=True) + EPS) * w

        def _l2norm(x):
            return x * jax.lax.rsqrt(jnp.sum(x * x, -1, keepdims=True) + EPS)

        def _causal_conv_silu(x, w):
            t = x.shape[1]
            xp = jnp.pad(x, ((0, 0), (CONV - 1, 0), (0, 0)))
            y = xp[:, 0:t, :] * w[:, 0]
            for i in range(1, CONV):
                y = y + xp[:, i:i + t, :] * w[:, i]
            return jax.nn.silu(y)

        def _gated_delta_rule(q, k, v, g, beta):
            qT = jnp.moveaxis(q, 1, 0)
            kT = jnp.moveaxis(k, 1, 0)
            vT = jnp.moveaxis(v, 1, 0)
            gT = jnp.moveaxis(g, 1, 0)
            bT = jnp.moveaxis(beta, 1, 0)
            S0 = jnp.zeros((q.shape[0], H, Kd, Vd), q.dtype)

            def step(S, inp):
                q_t, k_t, v_t, g_t, b_t = inp
                S = S * jnp.exp(g_t)[..., None, None]
                kv = jnp.einsum('bhk,bhkv->bhv', k_t, S)
                delta = (v_t - kv) * b_t[..., None]
                S = S + k_t[..., :, None] * delta[..., None, :]
                o = jnp.einsum('bhk,bhkv->bhv', q_t, S)
                return (S, o)
            _, o = jax.lax.scan(step, S0, (qT, kT, vT, gT, bT))
            return jnp.moveaxis(o, 0, 1)

        def _forward(x, ln1_g, ln1_b, ln2_g, ln2_b, rms_in_w, Wq, Wk, Wv, conv_q_w, conv_k_w, conv_v_w, Wa, dt_bias, A_log, Wb, Wg, o_norm_w, Wo, W2, b2):
            b, t, _ = x.shape
            h = _layernorm(x, ln1_g, ln1_b)
            h = _rmsnorm(h, rms_in_w)
            q = _causal_conv_silu(h @ Wq, conv_q_w).reshape(b, t, H, Kd)
            k = _causal_conv_silu(h @ Wk, conv_k_w).reshape(b, t, H, Kd)
            v = _causal_conv_silu(h @ Wv, conv_v_w).reshape(b, t, H, Vd)
            q = _l2norm(q) * Kd ** (-0.5)
            k = _l2norm(k)
            g = -jnp.exp(A_log) * jax.nn.softplus(h @ Wa + dt_bias)
            beta = jax.nn.sigmoid(h @ Wb)
            o = _gated_delta_rule(q, k, v, g, beta)
            gate = (h @ Wg).reshape(b, t, H, Vd)
            o = _rmsnorm(o, o_norm_w) * jax.nn.silu(gate)
            enc = o.reshape(b, t, VAL_DIM) @ Wo
            x = x + enc
            h2 = _layernorm(x, ln2_g, ln2_b)
            x_out = jax.nn.gelu(h2 @ W2 + b2, approximate=False) + x
            return x_out
        return _forward(x, ln1_g, ln1_b, ln2_g, ln2_b, rms_in_w, Wq, Wk, Wv, conv_q_w, conv_k_w, conv_v_w, Wa, dt_bias, A_log, Wb, Wg, o_norm_w, Wo, W2, b2)

    def _L1_ffn_ref(x, fc1_A, fc1_B, fc2_A, fc2_B, fc1_logits, fc2_logits):
        import jax, jax.numpy as jnp
        import numpy as np
        TOP_K = 32
        TEMPERATURE = 1.0
        PARAM_SCALE = 0.02

        def _compose_weight(logits, A, B):
            vals, idx = jax.lax.top_k(logits, TOP_K)
            w = jax.nn.softmax(vals / TEMPERATURE)
            A_sel = A[idx]
            B_sel = B[idx]
            return jnp.einsum('k,kir,kro->io', w, A_sel, B_sel)
        W1 = _compose_weight(fc1_logits, fc1_A, fc1_B)
        W2 = _compose_weight(fc2_logits, fc2_A, fc2_B)
        h = jax.nn.gelu(jnp.einsum('bsd,df->bsf', x, W1))
        return jnp.einsum('bsf,fd->bsd', h, W2)
    x = L0_attn_x
    x = _layernorm(x + _L0_attn_ref(x, L0_attn_conv_w, L0_attn_wq, L0_attn_wkg, L0_attn_wv, L0_attn_wg, L0_attn_bg, L0_attn_wout, L0_attn_aug_balance), axis=-1)
    x = _layernorm(x + _L0_ffn_ref(x, L0_ffn_w_g, L0_ffn_c_fc, L0_ffn_c_proj), axis=-1)
    x = _layernorm(x + _L1_attn_ref(x, L1_attn_ln1_g, L1_attn_ln1_b, L1_attn_ln2_g, L1_attn_ln2_b, L1_attn_rms_in_w, L1_attn_Wq, L1_attn_Wk, L1_attn_Wv, L1_attn_conv_q_w, L1_attn_conv_k_w, L1_attn_conv_v_w, L1_attn_Wa, L1_attn_dt_bias, L1_attn_A_log, L1_attn_Wb, L1_attn_Wg, L1_attn_o_norm_w, L1_attn_Wo, L1_attn_W2, L1_attn_b2), axis=-1)
    x = _layernorm(x + _L1_ffn_ref(x, L1_ffn_fc1_A, L1_ffn_fc1_B, L1_ffn_fc2_A, L1_ffn_fc2_B, L1_ffn_fc1_logits, L1_ffn_fc2_logits), axis=-1)
    return x

_drawn_inputs = setup_inputs


def setup_inputs(seed=0):
    import zlib

    import numpy as np

    out = dict(_drawn_inputs(seed))
    spreads = {'L1_attn_ln1_g': (1.0, 0.6),
     'L1_attn_ln1_b': (0.0, 0.8),
     'L1_attn_ln2_g': (1.0, 0.6),
     'L1_attn_ln2_b': (0.0, 0.8),
     'L1_attn_rms_in_w': (1.0, 0.6),
     'L1_attn_o_norm_w': (1.0, 0.6),
     'L1_attn_b2': (0.0, 0.293)}
    factors = {'L0_attn_conv_w': 4.279,
     'L0_attn_wq': 4.329,
     'L0_attn_wkg': 8.0,
     'L0_attn_wv': 4.261,
     'L0_attn_wg': 4.313,
     'L0_attn_bg': 8.0,
     'L0_attn_wout': 4.265,
     'L0_attn_aug_balance': 8.0,
     'L1_attn_Wq': 2.674,
     'L1_attn_conv_q_w': 2.699,
     'L1_attn_Wa': 8.0,
     'L1_attn_dt_bias': 8.0,
     'L1_attn_A_log': 8.0,
     'L1_attn_Wb': 8.0,
     'L1_attn_Wg': 2.686,
     'L1_ffn_fc1_A': 8.0,
     'L1_ffn_fc1_B': 8.0,
     'L1_ffn_fc2_A': 8.0,
     'L1_ffn_fc2_B': 8.0,
     'L1_ffn_fc1_logits': 8.0,
     'L1_ffn_fc2_logits': 8.0}
    for name, (base, spread) in spreads.items():
        noise = np.random.default_rng([zlib.crc32(name.encode()), seed]).standard_normal(out[name].shape)
        drawn = base * np.exp(spread * noise) if base else spread * noise
        out[name] = jnp.asarray(drawn.astype(out[name].dtype))
    for name, factor in factors.items():
        out[name] = (out[name] * factor).astype(out[name].dtype)
    return out
```

```python
from contextlib import ExitStack

import concourse.bass as bass
from concourse import mybir

F32 = mybir.dt.float32
I32 = mybir.dt.int32
U32 = mybir.dt.uint32
ALU = mybir.AluOpType
ACT = mybir.ActivationFunctionType
AX_X = mybir.AxisListType.X

P = 128
B, L, D = 16, 512, 256
NTOK = B * L
DT = D // P
TT = L // P
LN_EPS = 1e-5
EXPERTS, TOPK, FF = 8, 2, 1024
FT = FF // P
CAP = max(4, int(1.25 * NTOK * TOPK / EXPERTS))
SLOTS = EXPERTS * CAP
BLK = 512
TRASH = SLOTS + BLK
PRIM, RANK, SEL = 64, 64, 32


class Chain:

    def __init__(self, eng, sem, base=0):
        self.eng, self.sem, self.base, self.n = eng, sem, base, 0

    def __call__(self, ins):
        self.n += 1
        ins.then_inc(self.sem, 1)
        self.eng.wait_ge(self.sem, self.base + self.n)


def opener(nc, ctx, tag):
    sems = []

    def close():
        nc.clear_and_free_semaphores(sems)
        nc.all_engine_barrier()

    ctx.callback(close)

    def sb(name, shape, dt=F32):
        return ctx.enter_context(nc.sbuf_tensor(f"{tag}_{name}", shape, dt))

    def ps(name, shape, dt=F32):
        return ctx.enter_context(nc.psum_tensor(f"{tag}_{name}", shape, dt))

    def sem(name):
        sems.append(nc.alloc_semaphore(f"{tag}_{name}"))
        return sems[-1]

    return sb, ps, sem


def identity_tile(nc, pool, tile, zeroed, made):
    nc.gpsimd.memset(tile[:], 0.0).then_inc(zeroed, 1)
    pool.wait_ge(zeroed, 1)
    nc.gpsimd.affine_select(out=tile[:], in_=tile[:], compare_op=ALU.not_equal, fill=1.0, base=0,
                            pattern=[[-1, P]], channel_multiplier=1).then_inc(made, 1)


def row_norm(nc, dve, link, z, out, stats, agg, var, rstd, n, var_ready, rstd_ready, count, hold):
    for t in range(n):
        ins = nc.vector.bn_stats(stats[:, t, :], z[:, t, :])
    link(ins)
    nc.vector.memset(hold[:], 0.0)
    for t in range(n):
        ins = nc.vector.bn_aggr(agg[:, t, :], stats[:, t, :])
    link(ins)
    nc.vector.tensor_scalar(var[:], agg[:, :, 1], LN_EPS, None, ALU.add).then_inc(var_ready, 1)
    dve.wait_ge(rstd_ready, count)
    for t in range(n):
        ins = nc.vector.tensor_scalar(out[:, t, :], z[:, t, :], agg[:, t, 0:1], rstd[:, t:t + 1],
                                      ALU.subtract, ALU.mult)
    return ins


def compose_weights(nc, logits1, a1, b1, logits2, a2, b2, w1_out, w2_out):
    KT = SEL * RANK // P
    ROW2 = 32
    with ExitStack() as ctx:
        sb, ps, sem = opener(nc, ctx, "cw")
        lg = sb("logits", [64, 2, PRIM])
        vals = sb("vals", [64, SEL])
        idx = sb("idx", [64, SEL], U32)
        ew = sb("ew", [64, SEL])
        neg = sb("neg", [64, 1])
        tot = sb("tot", [64, 1])
        rtot = sb("rtot", [64, 1])
        one = sb("one", [64, 64])
        wcol = sb("wcol", [P, 2, KT])
        A1 = [sb(f"A1_{u}", [P, D]) for u in range(2)]
        B1 = [sb(f"B1_{u}", [P, FF]) for u in range(2)]
        A2 = [sb(f"A2_{u}", [P, FF]) for u in range(2)]
        B2 = [sb(f"B2_{u}", [P, D]) for u in range(2)]
        zero = sb("zero", [P, 512])
        acc1 = [ps(f"acc1_{n}", [P, 512]) for n in range(4)]
        acc2 = [ps(f"acc2_{n}", [P, 512]) for n in range(4)]
        loaded, cleared, step, neg_ready, exp_done = (sem(n) for n in ("loaded", "cleared", "step", "neg", "exp"))
        picked, w_ready, w_bcast, w_col = sem("picked"), sem("w_ready"), sem("w_bcast"), sem("w_col")
        in_u = [sem(f"in{u}") for u in range(2)]
        scaled, used, zeroed, acc_done, stored = (sem(n) for n in ("scaled", "used", "zeroed", "acc_done", "stored"))
        out_ready = sem("out_ready")
        w1s = sb("w1s", [P, DT, FF])
        w2s = sb("w2s", [P, FT, D])

        with nc.Block() as block:
            @block.sync
            def _(sp):
                sp.wait_ge(cleared, 1)
                sp.dma_start(lg[0:1, 0, :], logits1.rearrange("(a n) -> a n", a=1)).then_inc(loaded, 16)
                sp.dma_start(lg[ROW2:ROW2 + 1, 0, :], logits2.rearrange("(a n) -> a n", a=1)).then_inc(loaded, 16)
                sp.wait_ge(picked, SEL // 8)
                with sp.Fori(0, KT // 2) as t:
                    for u in range(2):
                        for half in range(2):
                            k1 = sp.value_load(idx[0:1, bass.ds(t * 4 + 2 * u + half, 1)], min_val=0, max_val=PRIM - 1)
                            k2 = sp.value_load(idx[ROW2:ROW2 + 1, bass.ds(t * 4 + 2 * u + half, 1)], min_val=0, max_val=PRIM - 1)
                            rows = slice(half * RANK, (half + 1) * RANK)
                            s1, s2 = bass.ds(k1 * RANK, RANK), bass.ds(k2 * RANK, RANK)
                            srcs = [a1[s1, :], b1[s1, :], a2[s2, :], b2[s2, :]]
                            if half == 0:
                                sp.wait_ge(used, t * 2 + u + 1)
                            for tile, src in zip((A1[u], B1[u], A2[u], B2[u]), srcs):
                                sp.dma_start(tile[rows, :], src).then_inc(in_u[u], 16)
                sp.wait_ge(out_ready, 8)
                sp.dma_start(w1_out.rearrange("(t p) n -> p t n", p=P), w1s[:]).then_inc(stored, 16)
                sp.dma_start(w2_out.rearrange("(t p) n -> p t n", p=P), w2s[:]).then_inc(stored, 16)
                sp.wait_ge(stored, 32)

            @block.vector
            def _(dve):
                link = Chain(dve, step)
                nc.vector.memset(one[:], 1.0)
                nc.vector.memset(zero[:], 0.0).then_inc(zeroed, 1)
                nc.vector.memset(lg[:], 0.0).then_inc(cleared, 1)
                dve.wait_ge(loaded, 32)
                for r in range(SEL // 8):
                    cur, nxt = lg[:, r % 2, :], lg[:, (r + 1) % 2, :]
                    v8 = vals[:, 8 * r:8 * r + 8]
                    link(nc.vector.max(v8, cur))
                    nc.vector.max_index(idx[:, 8 * r:8 * r + 8], v8, cur).then_inc(picked, 1)
                    link(nc.vector.match_replace(nxt, v8, cur, -3.0e38))
                nc.vector.tensor_scalar(neg[:], vals[:, 0:1], -1.0, None, ALU.mult).then_inc(neg_ready, 1)
                dve.wait_ge(exp_done, 1)
                link(nc.vector.reciprocal(rtot[:], tot[:]))
                nc.vector.tensor_scalar(ew[:], ew[:], rtot[:, 0:1], None, ALU.mult).then_inc(w_ready, 1)
                dve.wait_ge(w_bcast, 1)
                for n in range(2):
                    nc.vector.tensor_copy(wcol[:, n, :], acc1[n][:, 0:KT]).then_inc(w_col, 1)
                dve.wait_ge(w_col, 2)
                with dve.Fori(0, KT // 2) as t:
                    for u in range(2):
                        dve.wait_ge(in_u[u], t * 128 + 128)
                        for n, tile in ((0, A1[u]), (1, B2[u])):
                            nc.vector.tensor_scalar(tile[:], tile[:], wcol[:, n, bass.ds(t * 2 + u, 1)], None,
                                                    ALU.mult).then_inc(scaled, 1)
                dve.wait_ge(acc_done, 1)
                for n in range(4):
                    nc.vector.tensor_copy(w1s[:, n // 2, (n % 2) * 512:(n % 2) * 512 + 512], acc1[n][:]).then_inc(out_ready, 1)
                for n in range(4):
                    nc.vector.tensor_copy(w2s[:, 2 * n:2 * n + 2, :].rearrange("p a d -> p (a d)"), acc2[n][:]).then_inc(out_ready, 1)

            @block.scalar
            def _(act):
                act.wait_ge(neg_ready, 1)
                nc.scalar.activation(ew[:], vals[:], ACT.Exp, bias=neg[:, 0:1], accum_out=tot[:]).then_inc(exp_done, 1)

            @block.tensor
            def _(pe):
                pe.nop().then_inc(used, 2)
                pe.wait_ge(w_ready, 1)
                for n, row in ((0, 0), (1, ROW2)):
                    for half in range(2):
                        ins = nc.tensor.matmul(acc1[n][half * 64:half * 64 + 64, 0:KT], one[row:row + 1, :],
                                               ew[row:row + 1, half:SEL:2], start=True, stop=True)
                ins.then_inc(w_bcast, 1)
                pe.wait_ge(w_col, 2)
                pe.wait_ge(zeroed, 1)
                for bank in acc1 + acc2:
                    ins = nc.tensor.matmul(bank[:], zero[:, 0:P], zero[:], start=True, stop=False, skip_group_check=True)
                with pe.Fori(0, KT // 2) as t:
                    for u in range(2):
                        pe.wait_ge(scaled, t * 4 + 2 * u + 2)
                        for n in range(4):
                            nc.tensor.matmul(acc1[n][:], A1[u][:, (n // 2) * P:(n // 2 + 1) * P],
                                             B1[u][:, (n % 2) * 512:(n % 2) * 512 + 512],
                                             start=False, stop=False, skip_group_check=True)
                        for m in range(FT):
                            ins = nc.tensor.matmul(acc2[m // 2][:, (m % 2) * D:(m % 2 + 1) * D], A2[u][:, m * P:(m + 1) * P],
                                                   B2[u][:], start=False, stop=False, skip_group_check=True)
                        ins.then_inc(used, 1)
                for bank in acc1 + acc2:
                    ins = nc.tensor.matmul(bank[:], zero[:, 0:P], zero[:], start=False, stop=True, skip_group_check=True)
                ins.then_inc(acc_done, 1)


NT = NTOK // P
CHOICES = ("first", "second")


def route(nc, logits, put_at, get_at, weight, slots):
    TE = NT * EXPERTS
    with ExitStack() as ctx:
        sb, ps, sem = opener(nc, ctx, "rt")
        lg = sb("lg", [P, NT, EXPERTS])
        ecol = sb("ecol", [P, NT, EXPERTS])
        token = sb("token", [P, NT])
        before = sb("before", [P, P])
        ones = sb("ones", [P, TE])
        nottile0 = sb("nottile0", [P, EXPERTS, NT])
        top = sb("top", [P, 2, NT])
        num = sb("num", [P, 2, NT])
        tmp = sb("tmp", [P, NT, EXPERTS])
        oh = [sb(f"oh{k}", [P, NT, EXPERTS]) for k in range(2)]
        total = sb("total", [P, EXPERTS, NT])
        upto = sb("upto", [P, EXPERTS, NT])
        count1 = sb("count1", [P, EXPERTS])
        rank = sb("rank", [P, NT])
        ok = sb("ok", [P, NT])
        place, aside = sb("place", [P, NT]), sb("aside", [P, NT])
        e2, den = sb("e2", [P, NT]), sb("den", [P, NT])
        ZROWS = 4 * P
        zeros = sb("zeros", [P, ZROWS // P * D])
        zero_set, filled = sem("zero_set"), sem("filled")
        p_before = [ps(f"before{k}", [P, TE]) for k in range(2)]
        p_total = [ps(f"total{k}", [P, TE]) for k in range(2)]
        lg_in, cst, step, picked, counted, e2_in, e2_done = (sem(n) for n in ("lg_in", "cst", "step", "picked", "counted", "e2_in", "e2_done"))
        wide = lambda x: x.unsqueeze(2).broadcast_to([P, NT, EXPERTS])

        with nc.Block() as block:
            @block.sync
            def _(sp):
                sp.dma_start(lg[:], logits.rearrange("(t p) e -> p t e", p=P)).then_inc(lg_in, 16)
                sp.wait_ge(zero_set, 1)
                with sp.Fori(0, TRASH // ZROWS) as n:
                    sp.dma_start(slots[bass.ds(n * ZROWS, ZROWS), :].rearrange("(p r) d -> p (r d)", p=P), zeros[:]).then_inc(filled, 16)
                sp.wait_ge(filled, TRASH // ZROWS * 16)

            @block.gpsimd
            def _(pool):
                link = Chain(pool, cst)
                nc.gpsimd.memset(zeros[:], 0.0).then_inc(zero_set, 1)
                link(nc.gpsimd.iota(ecol[:], pattern=[[0, NT], [1, EXPERTS]], base=0, channel_multiplier=0,
                                    allow_small_or_imprecise_dtypes=True))
                link(nc.gpsimd.iota(token[:], pattern=[[P, NT]], base=0, channel_multiplier=1, allow_small_or_imprecise_dtypes=True))
                link(nc.gpsimd.memset(ones[:], 1.0))
                link(nc.gpsimd.affine_select(out=before[:], in_=ones[:, 0:P], compare_op=ALU.is_gt, fill=0.0, base=0,
                                             pattern=[[1, P]], channel_multiplier=-1))
                link(nc.gpsimd.affine_select(out=nottile0[:], in_=ones[:].rearrange("p (e t) -> p e t", t=NT), compare_op=ALU.is_gt,
                                             fill=0.0, base=0, pattern=[[0, EXPERTS], [1, NT]], channel_multiplier=0))

            @block.scalar
            def _(act):
                act.wait_ge(e2_in, 1)
                nc.scalar.activation(e2[:], e2[:], ACT.Exp).then_inc(e2_done, 1)

            @block.tensor
            def _(pe):
                pe.wait_ge(cst, 5)
                for k in range(2):
                    pe.wait_ge(picked, k + 1)
                    flat = oh[k][:].rearrange("p t e -> p (t e)")
                    nc.tensor.matmul(p_before[k][:], before[:], flat, start=True, stop=True)
                    nc.tensor.matmul(p_total[k][:], ones[:, 0:P], flat, start=True, stop=True).then_inc(counted, 1)

            @block.vector
            def _(dve):
                link = Chain(dve, step)
                tt, v = nc.vector.tensor_tensor, nc.vector
                dve.wait_ge(lg_in, 16)
                dve.wait_ge(cst, 5)
                for k in range(2):
                    link(v.tensor_reduce(top[:, k, :], lg[:], AX_X, ALU.max))
                    link(tt(tmp[:], lg[:], wide(top[:, k, :]), ALU.is_lt))
                    link(v.scalar_tensor_tensor(tmp[:], tmp[:], float(EXPERTS), ecol[:], ALU.mult, ALU.add))
                    link(v.tensor_reduce(num[:, k, :], tmp[:], AX_X, ALU.min))
                    tt(oh[k][:], ecol[:], wide(num[:, k, :]), ALU.is_equal).then_inc(picked, 1)
                    dve.wait_ge(picked, k + 1)
                    if k == 0:
                        link(v.scalar_tensor_tensor(lg[:], oh[0][:], -3.0e38, lg[:], ALU.mult, ALU.add))
                tt(e2[:], top[:, 1, :], top[:, 0, :], ALU.subtract).then_inc(e2_in, 1)
                dve.wait_ge(e2_done, 1)
                link(v.tensor_scalar(den[:], e2[:], 1.0, None, ALU.add))
                link(v.reciprocal(weight[:, 0, :], den[:]))
                link(tt(weight[:, 1, :], e2[:], weight[:, 0, :], ALU.mult))
                for k in range(2):
                    dve.wait_ge(counted, k + 1)
                    link(v.tensor_copy(total[:], p_total[k][:].rearrange("p (t e) -> p e t", e=EXPERTS)))
                    flat = lambda x: x.rearrange("p e t -> p (e t)")
                    link(v.tensor_tensor_scan(flat(upto[:]), flat(nottile0[:]), flat(total[:]), 0.0, ALU.mult, ALU.add))
                    link(tt(total[:], upto[:], total[:], ALU.subtract))
                    if k == 0:
                        link(v.tensor_copy(count1[:], upto[:, :, NT - 1]))
                    else:
                        link(tt(total[:], total[:], count1[:].unsqueeze(2).broadcast_to([P, EXPERTS, NT]), ALU.add))
                    link(tt(tmp[:], p_before[k][:].rearrange("p (t e) -> p t e", e=EXPERTS), total[:].rearrange("p e t -> p t e"), ALU.add))
                    link(tt(tmp[:], tmp[:], oh[k][:], ALU.mult))
                    link(v.tensor_reduce(rank[:], tmp[:], AX_X, ALU.add))
                    link(v.tensor_scalar(ok[:], rank[:], float(CAP), None, ALU.is_lt))
                    link(tt(weight[:, k, :], weight[:, k, :], ok[:], ALU.mult))
                    link(v.tensor_scalar(place[:], rank[:], float(CAP - 1), None, ALU.min))
                    link(v.scalar_tensor_tensor(place[:], num[:, k, :], float(CAP), place[:], ALU.mult, ALU.add))
                    link(v.tensor_copy(get_at[:, k, :], place[:]))
                    link(v.tensor_scalar(aside[:], token[:], float(TRASH + k * NTOK), None, ALU.add))
                    link(tt(place[:], place[:], aside[:], ALU.subtract))
                    link(tt(place[:], place[:], ok[:], ALU.mult))
                    link(tt(place[:], place[:], aside[:], ALU.add))
                    link(v.tensor_copy(put_at[:, k, :], place[:]))


def dispatch(nc, x1_rows, put_at, slots):
    U = 4
    with ExitStack() as ctx:
        sb, ps, sem = opener(nc, ctx, "dp")
        row = [sb(f"row{u}", [P, D]) for u in range(U)]
        ix = [sb(f"ix{u}", [P, 2], U32) for u in range(U)]
        x_in, ix_in = [sem(f"x_in{u}") for u in range(U)], sem("ix_in")
        put, free = [sem(f"put{u}") for u in range(U)], [sem(f"free{u}") for u in range(U)]
        settled = sem("settled")
        with nc.Block() as block:
            @block.sync
            def _(sp):
                with sp.Fori(0, NT // U) as g:
                    for u in range(U):
                        src = x1_rows[bass.ds(g * (U * P) + u * P, P), :]
                        sp.wait_ge(free[u], g + 1)
                        sp.dma_start(row[u][:], src).then_inc(x_in[u], 16)

            @block.vector
            def _(dve):
                with dve.Fori(0, NT // U) as g:
                    for u in range(U):
                        dve.wait_ge(free[u], g + 1)
                        nc.vector.tensor_copy(ix[u][:], put_at[:, :, bass.ds(g * U + u, 1)].rearrange("p k a -> p (k a)")).then_inc(ix_in, 1)

            @block.gpsimd
            def _(pool):
                for u in range(U):
                    pool.nop().then_inc(free[u], 1)
                with pool.Fori(0, NT // U) as g:
                    for u in range(U):
                        pool.wait_ge(x_in[u], g * 16 + 16)
                    pool.wait_ge(ix_in, g * U + U)
                    pool.sem_inc(settled, 1)
                    for u in range(U):
                        for k in range(2):
                            nc.gpsimd.indirect_dma_start(slots, bass.IndirectOffsetOnAxis(ap=ix[u][:, k:k + 1], axis=0),
                                                         row[u][:], None).then_inc(put[u], 16)
                    for u in range(U):
                        pool.wait_ge(put[u], g * 32 + 32)
                        pool.nop().then_inc(free[u], 1)


def combine(nc, x1_rows, slots_out, get_at, weight, x2_rows):
    with ExitStack() as ctx:
        sb, ps, sem = opener(nc, ctx, "cb")
        x1 = sb("x1", [P, TT, D])
        got = [[sb(f"got{u}_{k}", [P, D]) for k in range(2)] for u in range(TT)]
        ix = [sb(f"ix{u}", [P, 2], U32) for u in range(TT)]
        z, x2 = sb("z", [P, TT, D]), sb("x2", [P, TT, D])
        stats, agg = sb("stats", [P, TT, 6]), sb("agg", [P, TT, 2])
        var, rstd, mhalf, hold = sb("var", [P, TT]), sb("rstd", [P, TT]), sb("mhalf", [P, TT]), sb("hold", [P, 1])
        names = "x1_in got_in step z_ready var_ready rstd_ready x2_ready x2_stored x2_free half settled ix_ready"
        s = {n: sem(n) for n in names.split()}
        with nc.Block() as block:
            @block.sync
            def _(sp):
                with sp.Fori(0, B) as g:
                    src = x1_rows[bass.ds(g * L, L), :].rearrange("(t p) d -> p t d", p=P)
                    sp.wait_ge(s["z_ready"], g + 1)
                    sp.dma_start(x1[:], src).then_inc(s["x1_in"], 16)

            @block.vector
            def _(dve):
                dve.nop().then_inc(s["z_ready"], 1)
                with dve.Fori(0, B) as g:
                    link = Chain(dve, s["step"], g * (2 * TT + 1))
                    dve.wait_ge(s["x1_in"], g * 16 + 16)
                    dve.wait_ge(s["got_in"], g * 128 + 128)
                    for u in range(TT):
                        link(nc.vector.scalar_tensor_tensor(z[:, u, :], got[u][0][:], weight[:, 0, bass.ds(g * TT + u, 1)],
                                                            x1[:, u, :], ALU.mult, ALU.add))
                    for u in range(TT):
                        ins = nc.vector.scalar_tensor_tensor(z[:, u, :], got[u][1][:], weight[:, 1, bass.ds(g * TT + u, 1)],
                                                             z[:, u, :], ALU.mult, ALU.add)
                        if u < TT - 1:
                            link(ins)
                    ins.then_inc(s["z_ready"], 1)
                    dve.wait_ge(s["z_ready"], g + 2)
                    dve.wait_ge(s["x2_free"], g + 1)
                    row_norm(nc, dve, link, z, x2, stats, agg, var, rstd, TT, s["var_ready"], s["rstd_ready"], g + 1, hold
                             ).then_inc(s["x2_ready"], 1)
                    dve.wait_ge(s["x2_ready"], g + 1)
                    assert link.n == 2 * TT + 1, link.n

            @block.gpsimd
            def _(pool):
                nc.gpsimd.memset(mhalf[:], -0.5).then_inc(s["half"], 1)
                pool.wait_ge(s["half"], 1)
                pool.nop().then_inc(s["x2_free"], 1)
                with pool.Fori(0, B) as g:
                    dst = x2_rows[bass.ds(g * L, L), :].rearrange("(t p) d -> p t d", p=P)
                    pool.wait_ge(s["z_ready"], g + 1)
                    for u in range(TT):
                        nc.gpsimd.tensor_copy(ix[u][:], get_at[:, :, bass.ds(g * TT + u, 1)].rearrange("p k a -> p (k a)")).then_inc(s["ix_ready"], 1)
                    pool.wait_ge(s["ix_ready"], g * TT + TT)
                    pool.sem_inc(s["settled"], 1)
                    for u in range(TT):
                        for k in range(2):
                            nc.gpsimd.indirect_dma_start(got[u][k][:], None, slots_out,
                                                         bass.IndirectOffsetOnAxis(ap=ix[u][:, k:k + 1], axis=0)).then_inc(s["got_in"], 16)
                    pool.wait_ge(s["var_ready"], g + 1)
                    nc.gpsimd.tensor_tensor(rstd[:], var[:], mhalf[:], ALU.pow).then_inc(s["rstd_ready"], 1)
                    pool.wait_ge(s["x2_ready"], g + 1)
                    pool.dma_start(dst, x2[:]).then_inc(s["x2_stored"], 16)
                    pool.wait_ge(s["x2_stored"], g * 16 + 16)
                    pool.nop().then_inc(s["x2_free"], 1)


def mlp(nc, x_rows, w_in, w_out, out_rows, experts, blocks, gated_norm):
    RT = BLK // P
    with ExitStack() as ctx:
        sb, ps, sem = opener(nc, ctx, "ffn" if gated_norm else "moe")
        ident = sb("ident", [P, P])
        win = sb("win", [P, DT, FF])
        wout = sb("wout", [P, FT, D])
        xin = sb("xin", [P, RT, D])
        xT = sb("xT", [P, DT, BLK])
        hT = sb("hT", [P, FT, BLK])
        rel = sb("rel", [P, 4, BLK])
        osb = sb("osb", [P, RT, D])
        fc_ps = [ps(f"fc{n}", [P, BLK]) for n in range(4)]
        tp_ps = [ps(f"tp{n}", [P, BLK]) for n in range(DT)]
        o_ps = [ps(f"o{n}", [P, 2, D]) for n in range(RT // 2)]
        id0, id1 = sem("id_zeroed"), sem("id_made")
        win_in, wout_in, x_in = sem("win_in"), sem("wout_in"), sem("x_in")
        x_turned, xT_ready, fc_done, relu_done, h_ready = (sem(n) for n in ("x_turned", "xT_ready", "fc_done", "relu_done", "h_ready"))
        o_done, o_ready, o_stored, osb_free = sem("o_done"), sem("o_ready"), sem("o_stored"), sem("osb_free")
        if gated_norm:
            xres = sb("xres", [P, RT, D])
            z = sb("z", [P, RT, D])
            stats = sb("stats", [P, RT, 6])
            agg = sb("agg", [P, RT, 2])
            var = sb("var", [P, RT])
            rstd = sb("rstd", [P, RT])
            mhalf = sb("mhalf", [P, RT])
            hold = sb("hold", [P, 1])
            res_in, step, var_ready, rstd_ready, half_set = (sem(n) for n in ("res_in", "step", "var_ready", "rstd_ready", "half_set"))
            normed = sem("normed")
        n_blocks = experts * blocks

        def rows(n):
            return x_rows[bass.ds(n * BLK, BLK), :].rearrange("(t p) d -> p t d", p=P)

        with nc.Block() as block:
            @block.sync
            def _(sp):
                sp.dma_start(xin[:], rows(0)).then_inc(x_in, 16)
                with sp.Fori(0, experts) as e:
                    w_src = w_in[bass.ds(e * D, D), :].rearrange("(t p) f -> p t f", p=P)
                    if experts > 1:
                        sp.wait_ge(h_ready, e * blocks * FT + 1)
                    sp.dma_start(win[:], w_src).then_inc(win_in, 16)
                    v_src = w_out[bass.ds(e * FF, FF), :].rearrange("(t p) d -> p t d", p=P)
                    if experts > 1:
                        sp.wait_ge(o_done, e * blocks + 1)
                    sp.dma_start(wout[:], v_src).then_inc(wout_in, 16)
                    with sp.Fori(0, blocks) as b:
                        n = e * blocks + b
                        nxt = rows(n + 1)
                        sp.wait_ge(x_turned, n + 1)
                        sp.dma_start(xin[:], nxt).then_inc(x_in, 16)
                        if gated_norm:
                            here = rows(n)
                            sp.wait_ge(o_ready, n * 2 + 2)
                            sp.dma_start(xres[:], here).then_inc(res_in, 16)
                sp.wait_ge(x_in, 16 * (n_blocks + 1))

            @block.gpsimd
            def _(pool):
                identity_tile(nc, pool, ident, id0, id1)
                pool.nop().then_inc(osb_free, 1)
                if gated_norm:
                    nc.gpsimd.memset(mhalf[:], -0.5).then_inc(half_set, 1)
                    pool.wait_ge(half_set, 1)
                with pool.Fori(0, n_blocks) as n:
                    dst = out_rows[bass.ds(n * BLK, BLK), :].rearrange("(t p) d -> p t d", p=P)
                    if gated_norm:
                        pool.wait_ge(var_ready, n + 1)
                        pool.wait_ge(half_set, 1)
                        nc.gpsimd.tensor_tensor(rstd[:], var[:], mhalf[:], ALU.pow).then_inc(rstd_ready, 1)
                        pool.wait_ge(normed, n + 1)
                    else:
                        pool.wait_ge(o_ready, n * 2 + 4)
                    pool.wait_ge(id1, 1)
                    pool.dma_start(dst, osb[:]).then_inc(o_stored, 16)
                    pool.wait_ge(o_stored, n * 16 + 16)
                    pool.nop().then_inc(osb_free, 1)

            @block.tensor
            def _(pe):
                def turn(n):
                    pe.wait_ge(x_in, n * 16 + 16)
                    pe.wait_ge(xT_ready, 2 * n + 1)
                    for c in range(DT):
                        for t in range(RT):
                            ins = nc.tensor.transpose(tp_ps[c][:, t * P:(t + 1) * P], xin[:, t, c * P:(c + 1) * P], ident[:])
                    ins.then_inc(x_turned, 1)

                pe.wait_ge(id1, 1)
                pe.nop().then_inc(xT_ready, 1)
                pe.nop().then_inc(o_done, 1)
                pe.nop().then_inc(h_ready, 1)
                turn(0)
                with pe.Fori(0, experts) as e:
                    with pe.Fori(0, blocks) as b:
                        n = e * blocks + b
                        pe.wait_ge(win_in, e * 16 + 16)
                        pe.wait_ge(xT_ready, n * 2 + 3)
                        for m in range(FT):
                            if m < 4:
                                pe.wait_ge(h_ready, n * FT + 1)
                            else:
                                pe.wait_ge(h_ready, n * FT + m - 2)
                            for c in range(DT):
                                ins = nc.tensor.matmul(fc_ps[m % 4][:], win[:, c, m * P:(m + 1) * P], xT[:, c, :],
                                                       start=(c == 0), stop=(c == DT - 1))
                            ins.then_inc(fc_done, 1)
                        turn(n + 1)
                        pe.wait_ge(wout_in, e * 16 + 16)
                        pe.wait_ge(h_ready, n * FT + FT + 1)
                        for t in range(RT):
                            if t % 2 == 0:
                                pe.wait_ge(o_ready, n * (RT // 2) + t // 2 + 1)
                            for k in range(FT):
                                ins = nc.tensor.matmul(o_ps[t // 2][:, t % 2, :], hT[:, k, t * P:(t + 1) * P], wout[:, k, :],
                                                       start=(k == 0), stop=(k == FT - 1))
                        ins.then_inc(o_done, 1)

            @block.scalar
            def _(act):
                act.nop().then_inc(o_ready, 2)
                act.wait_ge(x_turned, 1)
                for c in range(DT):
                    nc.scalar.copy(xT[:, c, :], tp_ps[c][:]).then_inc(xT_ready, 1)
                with act.Fori(0, n_blocks) as n:
                    for m in range(FT):
                        act.wait_ge(fc_done, n * FT + m + 1)
                        if gated_norm:
                            nc.scalar.activation(hT[:, m, :], fc_ps[m % 4][:], ACT.Gelu_apprx_tanh).then_inc(h_ready, 1)
                        else:
                            if m >= 4:
                                act.wait_ge(h_ready, n * FT + m - 2)
                            else:
                                act.wait_ge(h_ready, n * FT + 1)
                            nc.scalar.activation(rel[:, m % 4, :], fc_ps[m % 4][:], ACT.Relu).then_inc(relu_done, 1)
                    act.wait_ge(x_turned, n + 2)
                    for c in range(DT):
                        nc.scalar.copy(xT[:, c, :], tp_ps[c][:]).then_inc(xT_ready, 1)

            @block.vector
            def _(dve):
                with dve.Fori(0, n_blocks) as n:
                    if gated_norm:
                        link = Chain(dve, step, n * 2)
                        dve.wait_ge(res_in, n * 16 + 16)
                        dve.wait_ge(o_done, n + 2)
                        for h in range(RT // 2):
                            nc.vector.tensor_tensor(z[:, 2 * h:2 * h + 2, :], o_ps[h][:], xres[:, 2 * h:2 * h + 2, :],
                                                    ALU.add).then_inc(o_ready, 1)
                        dve.wait_ge(o_ready, n * 2 + 4)
                        dve.wait_ge(osb_free, n + 1)
                        row_norm(nc, dve, link, z, osb, stats, agg, var, rstd, RT, var_ready, rstd_ready, n + 1, hold
                                 ).then_inc(normed, 1)
                        dve.wait_ge(normed, n + 1)
                    else:
                        for m in range(FT):
                            dve.wait_ge(relu_done, n * FT + m + 1)
                            nc.vector.tensor_tensor(hT[:, m, :], rel[:, m % 4, :], rel[:, m % 4, :], ALU.mult).then_inc(h_ready, 1)
                        dve.wait_ge(o_done, n + 2)
                        dve.wait_ge(osb_free, n + 1)
                        for h in range(RT // 2):
                            nc.vector.tensor_copy(osb[:, 2 * h:2 * h + 2, :], o_ps[h][:]).then_inc(o_ready, 1)


CH, SUB = 64, 8
DK_ALL, GH, DK, DV = 128, 8, 16, 32
NCH, NSUB = L // CH, CH // SUB
VSTEPS = 27
GK_FLOOR = -21.0


def linear_attention(nc, x_rows, xT_rows, conv_w, wq, wkg, wv, wg, bg, wout, aug_bal, w_gate, x1_rows, logits_out):
    with ExitStack() as ctx:
        sb, ps, sem = opener(nc, ctx, "gla")
        ident = sb("ident", [P, P])
        cw = sb("conv_w", [P, DT, 4])
        wq_s, wkg_s = sb("wq", [P, DT, DK_ALL]), sb("wkg", [P, DT, DK_ALL])
        wvg_s = sb("wvg", [P, DT, 2 * D])
        wout_s = sb("wout", [P, DT, D])
        wgate_s = sb("wgate", [P, DT, EXPERTS])
        bg_s = sb("bg", [P, D])
        aug_s = sb("aug", [P, 1])
        headmask = sb("headmask", [P, GH])
        blockmask = sb("blockmask", [P, D])
        causal = sb("causal", [P, 512], I32)
        ones = sb("ones", [P, 512])
        notstart = sb("notstart", [P, NCH, CH])
        mhalf = sb("mhalf", [P, 32])
        hold = sb("hold", [P, 1])
        xp = sb("xp", [P, DT, 3 + L])
        yc = sb("yc", [P, DT, L])
        xc = sb("xc", [P, DT, L])
        ab, g, G = sb("ab", [P, L]), sb("g", [P, L]), sb("G", [P, NCH, CH])
        k_, qs = sb("k", [P, NCH, CH]), sb("q", [P, L])
        eG, eR = sb("eG", [P, NCH, CH]), sb("eR", [P, NCH, CH])
        qt, kt = sb("qt", [P, L]), sb("kt", [P, NCH, NSUB, CH])
        qhat, khat = sb("qhat", [P, L]), sb("khat", [P, NCH, CH])
        qspread = sb("qspread", [P, NCH * NSUB, GH, SUB])
        aw = sb("aw", [P, L])
        S = sb("S", [P, 2, D])
        kvm = sb("kvm", [P, D])
        xres = sb("xres", [P, TT, D])
        vs, gs = sb("v", [P, TT, D]), sb("gate", [P, TT, D])
        kd = sb("kd", [P, TT, P])
        Ab = sb("A", [P, 2, 512])
        o, sg, sq = sb("o", [P, TT, D]), sb("sg", [P, TT, D]), sb("sq", [P, TT, D])
        augw = sb("augw", [P, TT, GH])
        mu, var32, rstd32 = sb("mu", [P, 32]), sb("var32", [P, 32]), sb("rstd32", [P, 32])
        oT = sb("oT", [P, DT, L])
        z, x1 = sb("z", [P, TT, D]), sb("x1", [P, TT, D])
        x1T = sb("x1T", [P, DT, L])
        lg = sb("lg", [P, TT, EXPERTS])
        stats, agg = sb("stats", [P, TT, 6]), sb("agg", [P, TT, 2])
        var, rstd = sb("var", [P, TT]), sb("rstd", [P, TT])
        pA, pB, pV, pW = ps("pA", [P, 512]), ps("pB", [P, 512]), ps("pV", [P, 512]), ps("pW", [P, 512])
        pO, pKV, pKD, pU = ps("pO", [P, 512]), ps("pKV", [P, 512]), ps("pKD", [P, 512]), ps("pU", [P, 512])

        names = ("id0 id1 consts half w_in x_in xres_in masks_a masks_b step act_step pool_step "
                 "conv_done xc_ready qk_ps qk_read e1_ready l1_ready g_ready ek_ready G_ready D_ready E_ready "
                 "small_D small_E q_ready kt_ready qt_ready spread_ready qhat_ready khat_ready kd_ps kd_ready "
                 "vg_ps v_ready gs_ready sg_ready A_ps A_ready kv_ps S_ready o_ps o_read aug_ps augv_ready aug_read sig_ready "
                 "sq_ready var_ready rstd_ready o_final oT_ps oT_ready y_ps z_ready lnvar lnrstd x1_ready x1_stored x1_free "
                 "x1T_ps x1T_ready lg_ps lg_ready aw_ready")
        s = {n: sem(n) for n in names.split()}

        with nc.Block() as block:
            @block.sync
            def _(sp):
                for tile, src in ((cw, conv_w.rearrange("(t p) k -> p t k", p=P)), (wq_s, wq.rearrange("(t p) n -> p t n", p=P)),
                                  (wkg_s, wkg.rearrange("(t p) n -> p t n", p=P)), (wout_s, wout.rearrange("(t p) n -> p t n", p=P)),
                                  (wgate_s, w_gate.rearrange("(t p) n -> p t n", p=P))):
                    sp.dma_start(tile[:], src).then_inc(s["w_in"], 16)
                sp.dma_start(wvg_s[:, :, 0:D], wv.rearrange("(t p) n -> p t n", p=P)).then_inc(s["w_in"], 16)
                sp.dma_start(wvg_s[:, :, D:2 * D], wg.rearrange("(t p) n -> p t n", p=P)).then_inc(s["w_in"], 16)
                sp.dma_start(bg_s[:], bg.rearrange("(a n) -> a n", a=1).broadcast_to([P, D])).then_inc(s["w_in"], 16)
                sp.dma_start(aug_s[:], aug_bal.rearrange("(p a) -> p a", a=1)).then_inc(s["w_in"], 16)
                with sp.Fori(0, B) as b:
                    src = xT_rows[bass.ds(b * D, D), :].rearrange("(t p) l -> p t l", p=P)
                    rsrc = x_rows[bass.ds(b * L, L), :].rearrange("(t p) d -> p t d", p=P)
                    sp.wait_ge(s["conv_done"], b * DT + 1)
                    sp.dma_start(xp[:, :, 3:3 + L], src).then_inc(s["x_in"], 16)
                    sp.wait_ge(s["z_ready"], b * 2 + 1)
                    sp.dma_start(xres[:], rsrc).then_inc(s["xres_in"], 16)

            @block.gpsimd
            def _(pool):
                cst = Chain(pool, s["pool_step"])
                identity_tile(nc, pool, ident, s["id0"], s["id1"])
                cst(nc.gpsimd.memset(mhalf[:], -0.5))
                cst(nc.gpsimd.memset(ones[:], 1.0))
                cst(nc.gpsimd.affine_select(out=headmask[:], in_=ones[:, 0:GH], compare_op=ALU.is_ge, fill=0.0, base=0,
                                            pattern=[[-DK, GH]], channel_multiplier=1))
                cst(nc.gpsimd.affine_select(out=headmask[:], in_=headmask[:], compare_op=ALU.is_ge, fill=0.0, base=DK - 1,
                                            pattern=[[DK, GH]], channel_multiplier=-1))
                cst(nc.gpsimd.tensor_copy(blockmask[:].rearrange("p (h v) -> p h v", v=DV),
                                          headmask[:].unsqueeze(2).broadcast_to([P, GH, DV])))
                cst(nc.gpsimd.memset(causal[:], 1))
                for half in range(2):
                    rows = causal[half * CH:(half + 1) * CH, :].rearrange("p (h i) -> p h i", h=GH)
                    cst(nc.gpsimd.affine_select(out=rows, in_=rows, compare_op=ALU.is_ge, fill=0.0, base=0,
                                                pattern=[[0, GH], [1, CH]], channel_multiplier=-1))
                nc.gpsimd.affine_select(out=notstart[:], in_=ones[:].rearrange("p (c l) -> p c l", l=CH), compare_op=ALU.is_gt,
                                        fill=0.0, base=0, pattern=[[0, NCH], [1, CH]], channel_multiplier=0).then_inc(s["consts"], 1)
                pool.wait_ge(s["consts"], 1)
                pool.nop().then_inc(s["x1_free"], 1)
                with pool.Fori(0, B) as b:
                    dst = x1_rows[bass.ds(b * L, L), :].rearrange("(t p) d -> p t d", p=P)
                    dst2 = logits_out[bass.ds(b * L, L), :].rearrange("(t p) d -> p t d", p=P)
                    for half in range(2):
                        pool.wait_ge(s["qt_ready"], b + 1)
                        pool.wait_ge(s["consts"], 1)
                        n = NCH * NSUB // 2
                        nc.gpsimd.tensor_tensor(
                            qspread[:, half * n:(half + 1) * n, :, :],
                            qt[:, half * L // 2:(half + 1) * L // 2].rearrange("p (n i) -> p n i", i=SUB).unsqueeze(2).broadcast_to([P, n, GH, SUB]),
                            headmask[:].unsqueeze(1).unsqueeze(3).broadcast_to([P, n, GH, SUB]), ALU.mult).then_inc(s["spread_ready"], 1)
                    pool.wait_ge(s["var_ready"], b + 1)
                    pool.wait_ge(s["consts"], 1)
                    nc.gpsimd.tensor_tensor(rstd32[:], var32[:], mhalf[:], ALU.pow).then_inc(s["rstd_ready"], 1)
                    pool.wait_ge(s["lnvar"], b + 1)
                    pool.wait_ge(s["consts"], 1)
                    nc.gpsimd.tensor_tensor(rstd[:], var[:], mhalf[:, 0:TT], ALU.pow).then_inc(s["lnrstd"], 1)
                    pool.wait_ge(s["x1_ready"], b + 1)
                    pool.wait_ge(s["consts"], 1)
                    pool.dma_start(dst, x1[:]).then_inc(s["x1_stored"], 16)
                    pool.wait_ge(s["lg_ready"], b + 1)
                    pool.wait_ge(s["consts"], 1)
                    pool.dma_start(dst2, lg[:]).then_inc(s["x1_stored"], 16)
                    pool.wait_ge(s["x1_stored"], b * 32 + 32)
                    pool.nop().then_inc(s["x1_free"], 1)

            @block.vector
            def _(dve):
                cst = Chain(dve, s["masks_a"])
                dve.nop().then_inc(s["conv_done"], 1)
                dve.nop().then_inc(s["z_ready"], 1)
                cst(nc.vector.memset(xp[:, :, 0:3], 0.0))
                cst(nc.vector.memset(kt[:].rearrange("p c a j -> p (c a j)"), 0.0))
                cst(nc.vector.memset(Ab[:].rearrange("p u n -> p (u n)"), 0.0))
                dve.wait_ge(s["consts"], 1)
                dve.wait_ge(s["w_in"], 9 * 16)
                cst(nc.vector.tensor_scalar(aug_s[:], aug_s[:], 4.0, None, ALU.mult))
                with dve.Fori(0, B) as b:
                    link = Chain(dve, s["step"], b * VSTEPS)

                    def publish(name, ins, count, each=1):
                        ins.then_inc(s[name], 1)
                        dve.wait_ge(s[name], b * each + count)

                    dve.wait_ge(s["x_in"], b * 16 + 16)
                    for c in range(DT):
                        link(nc.vector.tensor_scalar(yc[:, c, :], xp[:, c, 0:L], cw[:, c, 0:1], None, ALU.mult))
                        for k in range(1, 4):
                            ins = nc.vector.scalar_tensor_tensor(yc[:, c, :], xp[:, c, k:k + L], cw[:, c, k:k + 1], yc[:, c, :],
                                                                 ALU.mult, ALU.add)
                            if k < 3:
                                link(ins)
                            else:
                                publish("conv_done", ins, c + 2, 2)
                    for t in range(TT):
                        dve.wait_ge(s["vg_ps"], b * TT + t + 1)
                        publish("gs_ready", nc.vector.tensor_tensor(gs[:, t, :], (pV, pW)[t % 2][:, D:2 * D], bg_s[:], ALU.add), t + 1, TT)
                    dve.wait_ge(s["l1_ready"], b + 1)
                    publish("qk_read", nc.vector.scalar_tensor_tensor(g[:], pB[:], 0.0, ab[:], ALU.min, ALU.subtract), 1)
                    publish("g_ready", nc.vector.tensor_scalar(g[:], g[:], 1.0 / 16.0, GK_FLOOR, ALU.mult, ALU.max), 1)
                    link(nc.vector.tensor_tensor_scan(G[:].rearrange("p c l -> p (c l)"), notstart[:].rearrange("p c l -> p (c l)"),
                                                      g[:], 0.0, ALU.mult, ALU.add))
                    blocks8 = lambda t: t.rearrange("p c (a i) -> p (c a) i", i=SUB)
                    ref8 = blocks8(G[:])[:, :, SUB // 2 - 1:SUB // 2].broadcast_to([P, NCH * NSUB, SUB])
                    link(nc.vector.tensor_tensor(blocks8(eR[:]), blocks8(G[:]), ref8, ALU.subtract))
                    publish("small_D", nc.vector.tensor_tensor(khat[:], G[:, :, CH - 1:CH].broadcast_to([P, NCH, CH]), G[:], ALU.subtract), 1)
                    for a in range(NSUB):
                        n = SUB * (a + 1)
                        r = SUB * a + SUB // 2 - 1
                        publish("D_ready", nc.vector.tensor_tensor(kt[:, :, a, 0:n], G[:, :, r:r + 1].broadcast_to([P, NCH, n]),
                                                                   G[:, :, 0:n], ALU.subtract), a + 1, NSUB)
                    dve.wait_ge(s["ek_ready"], b + 1)
                    link(nc.vector.tensor_scalar(k_[:].rearrange("p c l -> p (c l)"), g[:], -1.0, 1.0, ALU.mult, ALU.add))
                    dve.wait_ge(s["small_E"], b * 3 + 3)
                    publish("qt_ready", nc.vector.tensor_tensor(qt[:], eR[:].rearrange("p c l -> p (c l)"), qs[:], ALU.mult), 1)
                    publish("qhat_ready", nc.vector.tensor_tensor(qhat[:], eG[:].rearrange("p c l -> p (c l)"), qs[:], ALU.mult), 1)
                    publish("khat_ready", nc.vector.tensor_tensor(khat[:], khat[:], k_[:], ALU.mult), 1)
                    link(nc.vector.tensor_tensor(aw[:], qs[:], k_[:].rearrange("p c l -> p (c l)"), ALU.mult))
                    publish("aw_ready", nc.vector.tensor_scalar(aw[:], aw[:], aug_s[:, 0:1], None, ALU.mult), 1)
                    for a in range(NSUB):
                        n = SUB * (a + 1)
                        dve.wait_ge(s["E_ready"], b * NSUB + a + 1)
                        publish("kt_ready", nc.vector.tensor_tensor(kt[:, :, a, 0:n], kt[:, :, a, 0:n], k_[:, :, 0:n], ALU.mult), a + 1, NSUB)
                    publish("S_ready", nc.vector.memset(S[:, 0, :], 0.0), 1, 2 * TT + 1)
                    for t in range(TT):
                        dve.wait_ge(s["A_ps"], b * TT + t + 1)
                        nc.vector.memset(hold[:], 0.0)
                        publish("A_ready", nc.vector.copy_predicated(Ab[:, t % 2, :], causal[:], pU[:]), t + 1, TT)
                        for c in range(2):
                            dve.wait_ge(s["kv_ps"], b * 2 * TT + 2 * t + c + 1)
                            link(nc.vector.tensor_tensor(kvm[:], pKV[:, 0:D], blockmask[:], ALU.mult))
                            publish("S_ready", nc.vector.scalar_tensor_tensor(
                                S[:, (c + 1) % 2, :], S[:, c, :], eG[:, 2 * t + c, CH - 1:CH], kvm[:], ALU.mult, ALU.add),
                                2 * t + c + 2, 2 * TT + 1)
                        dve.wait_ge(s["o_ps"], b * TT + t + 1)
                        publish("o_read", nc.vector.tensor_copy(o[:, t, :], pO[:, 0:D]), t + 1, TT)
                    per_head = lambda x: x.rearrange("p t (h v) -> p (t h) v", v=DV)
                    dve.wait_ge(s["aug_ps"], b + 1)
                    publish("aug_read", nc.vector.tensor_copy(augw[:].rearrange("p t h -> p (t h)"), pKD[:, 0:TT * GH]), 1)
                    dve.wait_ge(s["v_ready"], b * TT + TT)
                    publish("augv_ready", nc.vector.tensor_tensor(
                        per_head(sq[:]), per_head(vs[:]), augw[:].rearrange("p t h -> p (t h)").unsqueeze(2).broadcast_to([P, 32, DV]), ALU.mult), 1)
                    dve.wait_ge(s["sig_ready"], b + 1)
                    link(nc.vector.tensor_tensor(o[:], o[:], sq[:], ALU.add))
                    link(nc.vector.tensor_reduce(mu[:], per_head(o[:]), AX_X, ALU.add))
                    link(nc.vector.tensor_scalar(mu[:], mu[:], 1.0 / DV, None, ALU.mult))
                    spread = lambda x: x.unsqueeze(2).broadcast_to([P, 32, DV])
                    link(nc.vector.tensor_tensor(per_head(o[:]), per_head(o[:]), spread(mu[:]), ALU.subtract))
                    link(nc.vector.tensor_tensor(sq[:], o[:], o[:], ALU.mult))
                    link(nc.vector.tensor_reduce(var32[:], per_head(sq[:]), AX_X, ALU.add))
                    publish("var_ready", nc.vector.tensor_scalar(var32[:], var32[:], 1.0 / DV, LN_EPS, ALU.mult, ALU.add), 1)
                    dve.wait_ge(s["sg_ready"], b + 1)
                    link(nc.vector.tensor_tensor(o[:], o[:], sg[:], ALU.mult))
                    dve.wait_ge(s["rstd_ready"], b + 1)
                    publish("o_final", nc.vector.tensor_tensor(per_head(o[:]), per_head(o[:]), spread(rstd32[:]), ALU.mult), 1)
                    dve.wait_ge(s["xres_in"], b * 16 + 16)
                    for h in range(2):
                        dve.wait_ge(s["y_ps"], b * 2 + h + 1)
                        publish("z_ready", nc.vector.tensor_tensor(z[:, 2 * h:2 * h + 2, :].rearrange("p t d -> p (t d)"), (pV, pW)[h][:],
                                                                   xres[:, 2 * h:2 * h + 2, :].rearrange("p t d -> p (t d)"), ALU.add), h + 2, 2)
                    dve.wait_ge(s["x1_free"], b + 1)
                    row_norm(nc, dve, link, z, x1, stats, agg, var, rstd, TT, s["lnvar"], s["lnrstd"], b + 1, hold
                             ).then_inc(s["x1_ready"], 1)
                    dve.wait_ge(s["x1_ready"], b + 1)
                    dve.wait_ge(s["lg_ps"], b + 1)
                    publish("lg_ready", nc.vector.tensor_copy(lg[:].rearrange("p t e -> p (t e)"), pKD[:, 0:TT * EXPERTS]), 1)
                    assert link.n == VSTEPS, link.n

            @block.scalar
            def _(act):
                with act.Fori(0, B) as b:
                    def publish(name, ins, count, each=1):
                        ins.then_inc(s[name], 1)
                        act.wait_ge(s[name], b * each + count)

                    act.wait_ge(s["conv_done"], b * 2 + 3)
                    publish("xc_ready", nc.scalar.activation(xc[:].rearrange("p c l -> p (c l)"), yc[:].rearrange("p c l -> p (c l)"), ACT.Silu), 1)
                    for t in range(TT):
                        act.wait_ge(s["gs_ready"], b * TT + t + 1)
                        publish("v_ready", nc.scalar.copy(vs[:, t, :], (pV, pW)[t % 2][:, 0:D]), t + 1, TT)
                    publish("sg_ready", nc.scalar.activation(sg[:].rearrange("p t d -> p (t d)"), gs[:].rearrange("p t d -> p (t d)"), ACT.Silu), 1)
                    act.wait_ge(s["qk_ps"], b + 1)
                    publish("act_step", nc.scalar.activation(ab[:], pB[:], ACT.Abs), 1, 2)
                    publish("act_step", nc.scalar.activation(ab[:], ab[:], ACT.Exp, scale=-1.0), 2, 2)
                    publish("l1_ready", nc.scalar.activation(ab[:], ab[:], ACT.Ln, bias=1.0), 1)
                    publish("q_ready", nc.scalar.mul(qs[:], pA[:], float(DK) ** -0.5), 1)
                    act.wait_ge(s["small_D"], b + 1)
                    publish("ek_ready", nc.scalar.activation(g[:], g[:], ACT.Exp), 1)
                    flat = lambda x: x.rearrange("p c l -> p (c l)")
                    publish("small_E", nc.scalar.activation(flat(eR[:]), flat(eR[:]), ACT.Exp), 1, 3)
                    publish("small_E", nc.scalar.activation(flat(eG[:]), flat(G[:]), ACT.Exp), 2, 3)
                    publish("small_E", nc.scalar.activation(flat(khat[:]), flat(khat[:]), ACT.Exp), 3, 3)
                    for a in range(NSUB):
                        n = SUB * (a + 1)
                        act.wait_ge(s["D_ready"], b * NSUB + a + 1)
                        publish("E_ready", nc.scalar.activation(kt[:, :, a, 0:n], kt[:, :, a, 0:n], ACT.Exp), a + 1, NSUB)
                    act.wait_ge(s["kd_ps"], b + 1)
                    publish("kd_ready", nc.scalar.copy(kd[:].rearrange("p t k -> p (t k)"), pKD[:]), 1)
                    act.wait_ge(s["augv_ready"], b + 1)
                    publish("sig_ready", nc.scalar.activation(sq[:].rearrange("p t d -> p (t d)"), sq[:].rearrange("p t d -> p (t d)"), ACT.Sigmoid), 1)
                    act.wait_ge(s["oT_ps"], b + 1)
                    for c in range(DT):
                        publish("oT_ready", nc.scalar.copy(oT[:, c, :], (pA, pB)[c][:]), c + 1, 2)
                    act.wait_ge(s["x1T_ps"], b + 1)
                    for c in range(DT):
                        publish("x1T_ready", nc.scalar.copy(x1T[:, c, :], (pA, pB)[c][:]), c + 1, 2)

            @block.tensor
            def _(pe):
                pe.wait_ge(s["id1"], 1)
                pe.wait_ge(s["w_in"], 9 * 16)
                pe.wait_ge(s["consts"], 1)
                mm = nc.tensor.matmul
                with pe.Fori(0, B) as b:
                    pe.wait_ge(s["xc_ready"], b + 1)
                    for w, bank in ((wq_s, pA), (wkg_s, pB)):
                        for c in range(DT):
                            ins = mm(bank[:], w[:, c, :], xc[:, c, :], start=(c == 0), stop=(c == DT - 1))
                    ins.then_inc(s["qk_ps"], 1)
                    for t in range(TT):
                        if t >= 2:
                            pe.wait_ge(s["v_ready"], b * TT + t - 1)
                        for c in range(DT):
                            ins = mm((pV, pW)[t % 2][:], xc[:, c, t * P:(t + 1) * P], wvg_s[:, c, :], start=(c == 0), stop=(c == DT - 1))
                        ins.then_inc(s["vg_ps"], 1)
                    pe.wait_ge(s["khat_ready"], b + 1)
                    for t in range(TT):
                        ins = nc.tensor.transpose(pKD[:, t * P:(t + 1) * P], khat[:, 2 * t:2 * t + 2, :].rearrange("p c l -> p (c l)"),
                                                  ident[:])
                    ins.then_inc(s["kd_ps"], 1)
                    pe.wait_ge(s["spread_ready"], b * 2 + 2)
                    pe.wait_ge(s["kt_ready"], b * NSUB + NSUB)
                    pe.wait_ge(s["qhat_ready"], b + 1)
                    pe.wait_ge(s["v_ready"], b * TT + TT)
                    for t in range(TT):
                        if t > 0:
                            pe.wait_ge(s["A_ready"], b * TT + t)
                        for c in range(2):
                            for a in range(NSUB):
                                ins = mm(pU[c * CH:(c + 1) * CH, :].rearrange("p (h i) -> p h i", h=GH)[:, :, a * SUB:(a + 1) * SUB], kt[:, 2 * t + c, a, :],
                                         qspread[:, (2 * t + c) * NSUB + a, :, :], start=True, stop=True)
                        ins.then_inc(s["A_ps"], 1)
                        pe.wait_ge(s["kd_ready"], b + 1)
                        if t > 0:
                            pe.wait_ge(s["o_read"], b * TT + t)
                        pe.wait_ge(s["A_ready"], b * TT + t + 1)
                        for c in range(2):
                            rows = slice(c * CH, (c + 1) * CH)
                            pe.wait_ge(s["S_ready"], b * (2 * TT + 1) + 2 * t + c + 1)
                            mm(pKV[:, 0:D], kd[rows, t, :], vs[rows, t, :], start=True, stop=True).then_inc(s["kv_ps"], 1)
                            mm(pO[rows, 0:D], qhat[:, (2 * t + c) * CH:(2 * t + c + 1) * CH], S[:, c, :],
                               start=True, stop=False, skip_group_check=True)
                            for h in range(GH):
                                ins = mm(pO[rows, h * DV:(h + 1) * DV], Ab[rows, t % 2, h * CH:(h + 1) * CH], vs[rows, t, h * DV:(h + 1) * DV],
                                         start=False, stop=(h == GH - 1), skip_group_check=True)
                        ins.then_inc(s["o_ps"], 1)
                    pe.wait_ge(s["aw_ready"], b + 1)
                    for t in range(TT):
                        ins = mm(pKD[:, t * GH:(t + 1) * GH], aw[:, t * P:(t + 1) * P], headmask[:], start=True, stop=True)
                    ins.then_inc(s["aug_ps"], 1)

                    def turn(src, name):
                        for c in range(DT):
                            for t in range(TT):
                                ins = nc.tensor.transpose((pA, pB)[c][:, t * P:(t + 1) * P], src[:, t, c * P:(c + 1) * P], ident[:])
                        ins.then_inc(s[name], 1)

                    pe.wait_ge(s["o_final"], b + 1)
                    turn(o, "oT_ps")
                    pe.wait_ge(s["oT_ready"], b * 2 + 2)
                    for t in range(TT):
                        for c in range(DT):
                            ins = mm((pV, pW)[t // 2][:, (t % 2) * D:(t % 2 + 1) * D], oT[:, c, t * P:(t + 1) * P], wout_s[:, c, :],
                                     start=(c == 0), stop=(c == DT - 1))
                        if t % 2:
                            ins.then_inc(s["y_ps"], 1)
                    pe.wait_ge(s["x1_ready"], b + 1)
                    turn(x1, "x1T_ps")
                    pe.wait_ge(s["x1T_ready"], b * 2 + 2)
                    for t in range(TT):
                        for c in range(DT):
                            ins = mm(pKD[:, t * EXPERTS:(t + 1) * EXPERTS], x1T[:, c, t * P:(t + 1) * P], wgate_s[:, c, :],
                                     start=(c == 0), stop=(c == DT - 1))
                    ins.then_inc(s["lg_ps"], 1)


DH, KD, VD = 4, 64, 128
LEVELS = 7
RMS_EPS = 1e-6
GSTEPS = 67


def tcount(t, lv):
    return (LEVELS - 1) * 2 * (t // 2) + 2 * lv + t % 2 + 1


def zcount(t, lv):
    return LEVELS * 2 * (t // 2) + 2 * lv + t % 2 + 1


def delta_rule(nc, x2_rows, ln1_g, ln1_b, rms_w, wq, wk, wv, conv_q, conv_k, conv_v, wa, dt_bias, a_log, wb, wg,
               o_norm, wo, ln2_g, ln2_b, w2, b2, x3_rows):
    with ExitStack() as ctx:
        sb, ps, sem = opener(nc, ctx, "gdr")
        H2, HV, HK = DH // 2, DH * VD, DH * KD
        NP_ = 2 * H2 + DH
        G = TT * DH
        ident = sb("ident", [P, P])
        id4 = sb("id4", [P, DH, P])
        wqkv = sb("wqkv", [P, DT, 2 * HK + HV])
        wg_s, wo_s, w2_s = sb("wg", [P, DT, HV]), sb("wo", [P, DH, D]), sb("w2", [P, DT, D])
        wab = sb("wab", [P, DT, 2 * DH])
        cw = sb("cw", [P, NP_, 4])
        g1, b1, b2_s = sb("g1", [P, D]), sb("b1", [P, D]), sb("b2", [P, D])
        rw, g2, bb2 = sb("rw", [P, DT]), sb("g2", [P, DT]), sb("bb2", [P, DT])
        onw = sb("onw", [P, 1])
        dtb, nexpA = sb("dtb", [P, DH]), sb("nexpA", [P, DH])
        ones = sb("ones", [P, P])
        last = sb("last", [P, P])
        nottok0 = sb("nottok0", [P, 1])
        level = sb("level", [P, LEVELS, P], I32)
        mhalf, hold = sb("mhalf", [P, 32]), sb("hold", [P, 1])
        x2 = sb("x2", [P, TT, D])
        n1, u_, h_ = sb("n1", [P, TT, D]), sb("u", [P, TT, D]), sb("h", [P, TT, D])
        sq = sb("sq", [P, TT, HV])
        ss = sb("ss", [P, TT])
        hT = sb("hT", [P, DT, L])
        y = sb("y", [P, NP_, L])
        qk = sb("qk", [P, TT, 2, DH, KD])
        kb = sb("kb", [P, TT, DH, KD])
        v_ = sb("v", [P, TT, DH, VD])
        gt = sb("gt", [P, TT, HV])
        XT = sb("XT", [P, 6, L])
        t1, zr, z2, bt, sp_, a_, am = (sb(n, [P, TT, DH]) for n in ("t1", "zr", "z2", "bt", "sp", "a", "am"))
        ssq = sb("ssq", [P, 32])
        DT_, nAT, QD, T, U, Y = ([sb(f"{n}{i}", [P, DH, P]) for i in range(2)] for n in ("DT", "nAT", "QD", "T", "U", "Y"))
        gam, gbn, gC = ([sb(f"{n}{i}", [P, DH]) for i in range(2)] for n in ("gam", "gbn", "gC"))
        kd = [sb(f"kd{i}", [P, DH, KD]) for i in range(2)]
        R, QSe, dl = sb("R", [P, DH, VD]), sb("QSe", [P, DH, VD]), sb("dl", [P, DH, VD])
        S = sb("S", [P, H2, 2, VD])
        ov = sb("ov", [P, G])
        orr = sb("orr", [P, G])
        xa, x3 = sb("xa", [P, TT, D]), sb("x3", [P, TT, D])
        stats, agg = sb("stats", [P, TT, 6]), sb("agg", [P, TT, 2])
        var, rstd = sb("var", [P, TT]), sb("rstd", [P, TT])
        o, og = y[:, 0:TT, :], y[:, TT:2 * TT, :]
        bank = [ps(f"bank{n}", [P, 512]) for n in range(8)]

        per = dict(x_in=1, ln_var=3, ln_rstd=3, u=1, ss=1, ssv=1, ssr=1, h=1, hT_ps=1, hT=2, pj=NP_, tap=NP_, cv=NP_, si=NP_,
                   tk=NP_, te=NP_, gp=TT, gt=TT, ab_ps=1, ab=1, beta=1, abs=2, g_in=1, a=1, am=1, l2v=1, l2r=1, qk=1, vb=1,
                   bk=6, qkT=6, aB=TT, DT=TT, kk=TT, gm=TT, gmr=TT, gc=TT, nat=TT, prep=TT, rst=TT,
                   z=LEVELS * TT, T=(LEVELS - 1) * TT, ut=(LEVELS - 1) * TT, U=(LEVELS - 1) * TT, y=(LEVELS - 1) * TT,
                   Ye=(LEVELS - 1) * TT, Uf=TT, S=TT + 1, ks=TT, R=TT, qse=TT, dl=TT, de=TT, su=TT, op=TT, o=TT, osq=1,
                   ov=1, orr=1, og=1, oT=DH, oTe=DH, en=2, xa=1, n2=1, n2T=1, h2T=2, y2=2, yb=1, ge=1, z3=1, x3=1)
        s = {n: sem("s_" + n) for n in per}
        w_in, x_free, x3_free, stored, step = sem("w_in"), sem("x_free"), sem("x3_free"), sem("stored"), sem("step")
        rst_turn, id0, id1, cst, ready, aprep = sem("rst_turn"), sem("id0"), sem("id1"), sem("cst"), sem("ready"), sem("aprep")

        def waiter(eng, b):
            def wait(name, n):
                assert 1 <= n <= per[name], name
                eng.wait_ge(s[name], b * per[name] + n)

            def done(name, n, ins):
                ins.then_inc(s[name], 1)
                wait(name, n)
            return wait, done

        flat = lambda x: x.rearrange("p a b -> p (a b)")
        heads = lambda x: x.rearrange("p (h n) -> p h n", h=DH)

        with nc.Block() as block:
            @block.sync
            def _(sp):
                chan = lambda w: w.rearrange("(t p) n -> p t n", p=P)
                row = lambda v: v.rearrange("(a n) -> a n", a=1).broadcast_to([P, v.shape[0]])
                col = lambda v: v.rearrange("(t p) -> p t", p=P)
                for dst, src in ((wqkv[:, :, 0:HK], chan(wq)), (wqkv[:, :, HK:2 * HK], chan(wk)), (wqkv[:, :, 2 * HK:], chan(wv)),
                                 (wg_s[:], chan(wg)), (wo_s[:], chan(wo)), (w2_s[:], chan(w2)), (wab[:, :, 0:DH], chan(wa)),
                                 (wab[:, :, DH:], chan(wb)), (cw[:, 0:2, :], chan(conv_q)), (cw[:, 2:4, :], chan(conv_k)),
                                 (cw[:, 4:8, :], chan(conv_v)), (g1[:], row(ln1_g)), (b1[:], row(ln1_b)), (b2_s[:], row(b2)),
                                 (dtb[:], row(dt_bias)), (nexpA[:], row(a_log))):
                    sp.dma_start(dst, src).then_inc(w_in, 16)
                with nc.allow_non_contiguous_dma(reason="a few hundred channel scales"):
                    for dst, src in ((rw[:], col(rms_w)), (g2[:], col(ln2_g)), (bb2[:], col(ln2_b)), (onw[:], col(o_norm))):
                        sp.dma_start(dst, src).then_inc(w_in, 16)
                with sp.Fori(0, B) as b:
                    src = x2_rows[bass.ds(b * L, L), :].rearrange("(t p) d -> p t d", p=P)
                    sp.wait_ge(x_free, b + 1)
                    sp.dma_start(x2[:], src).then_inc(s["x_in"], 16)

            @block.gpsimd
            def _(pool):
                link = Chain(pool, cst)
                identity_tile(nc, pool, ident, id0, id1)
                pool.wait_ge(id1, 1)
                link(nc.gpsimd.memset(mhalf[:], -0.5))
                link(nc.gpsimd.memset(ones[:], 1.0))
                link(nc.gpsimd.affine_select(out=last[:], in_=ones[:], compare_op=ALU.is_ge, fill=0.0, base=1 - P,
                                             pattern=[[0, P]], channel_multiplier=1))
                link(nc.gpsimd.affine_select(out=nottok0[:], in_=ones[:, 0:1], compare_op=ALU.is_gt, fill=0.0, base=0,
                                             pattern=[[0, 1]], channel_multiplier=1))
                link(nc.gpsimd.memset(level[:], 1))
                for lv in range(LEVELS):
                    s_ = 1 << lv
                    m = level[:, lv, :].rearrange("p (m k n) -> p m k n", k=2, n=s_)
                    up = lv == LEVELS - 1
                    if up:
                        link(nc.gpsimd.affine_select(out=m[:, :, 1, :], in_=m[:, :, 1, :], compare_op=ALU.is_gt, fill=0.0, base=s_,
                                                     pattern=[[0, 1], [0, s_]], channel_multiplier=-1))
                        link(nc.gpsimd.memset(m[:, :, 0, :], 0))
                        continue
                    nblk = P // (2 * s_)
                    link(nc.gpsimd.affine_select(out=m[:, :, 0, :], in_=m[:, :, 0, :], compare_op=ALU.is_ge, fill=0.0, base=-s_,
                                                 pattern=[[-2 * s_, nblk], [0, s_]], channel_multiplier=1))
                    link(nc.gpsimd.affine_select(out=m[:, :, 0, :], in_=m[:, :, 0, :], compare_op=ALU.is_gt, fill=0.0, base=2 * s_,
                                                 pattern=[[2 * s_, nblk], [0, s_]], channel_multiplier=-1))
                    link(nc.gpsimd.memset(m[:, :, 1, :], 0))
                nc.gpsimd.tensor_copy(id4[:], ident[:].unsqueeze(1).broadcast_to([P, DH, P])).then_inc(ready, 1)
                pool.nop().then_inc(x3_free, 1)
                with pool.Fori(0, B) as b:
                    wait, done = waiter(pool, b)
                    dst = x3_rows[bass.ds(b * L, L), :].rearrange("(t p) d -> p t d", p=P)

                    def power(src, out, gate, gate_n, name, n, width):
                        wait(gate, gate_n)
                        nc.gpsimd.tensor_tensor(out, src, mhalf[:, 0:width], ALU.pow).then_inc(s[name], 1)

                    power(var[:], rstd[:], "ln_var", 1, "ln_rstd", 1, TT)
                    power(ss[:], ss[:], "ssv", 1, "ssr", 1, TT)
                    power(ssq[:], ssq[:], "l2v", 1, "l2r", 1, 32)
                    for t in range(TT):
                        wait("dl", t - 1) if t >= 2 else wait("l2v", 1)
                        pool.sem_inc(rst_turn, 1)
                        for M in (T[t % 2], U[t % 2]):
                            ins = nc.gpsimd.tensor_copy(M[:], ident[:].unsqueeze(1).broadcast_to([P, DH, P]))
                        ins.then_inc(s["rst"], 1)
                    power(ov[:], orr[:], "ov", 1, "orr", 1, G)
                    power(var[:], rstd[:], "ln_var", 2, "ln_rstd", 2, TT)
                    power(var[:], rstd[:], "ln_var", 3, "ln_rstd", 3, TT)
                    wait("x3", 1)
                    pool.dma_start(dst, x3[:]).then_inc(stored, 16)
                    pool.wait_ge(stored, b * 16 + 16)
                    pool.nop().then_inc(x3_free, 1)

            @block.vector
            def _(dve):
                dve.nop().then_inc(x_free, 1)
                v = nc.vector
                tt, stt, ts = v.tensor_tensor, v.scalar_tensor_tensor, v.tensor_scalar
                dve.wait_ge(w_in, 16 * 20)
                dve.wait_ge(ready, 1)
                wo_link = Chain(dve, aprep, 1)
                dve.wait_ge(aprep, 1)
                wo_link(ts(nexpA[:], nexpA[:], -1.0, None, ALU.mult))
                wo_link(ts(flat(wo_s[:]), flat(wo_s[:]), onw[:, 0:1], None, ALU.mult))
                with dve.Fori(0, B) as b:
                    wait, done = waiter(dve, b)
                    link = Chain(dve, step, b * GSTEPS)
                    token_wide = lambda w: w[:].unsqueeze(1).broadcast_to([P, TT, D])
                    dve.wait_ge(s["x_in"], b * 16 + 16)

                    def norm(src, dst, n, name):
                        ins = row_norm(nc, dve, link, src, dst, stats, agg, var, rstd, TT, s["ln_var"], s["ln_rstd"],
                                       b * 3 + n, hold)
                        link(ins) if name is None else done(name, 1, ins)

                    norm(x2, n1, 1, None)
                    link(tt(u_[:], n1[:], token_wide(g1), ALU.mult))
                    done("u", 1, tt(u_[:], u_[:], token_wide(b1), ALU.add))
                    wait("ss", 1)
                    done("ssv", 1, ts(ss[:], ss[:], 1.0 / D, RMS_EPS, ALU.mult, ALU.add))
                    wait("ssr", 1)
                    for t in range(TT):
                        ins = ts(h_[:, t, :], u_[:, t, :], ss[:, t:t + 1], None, ALU.mult)
                    done("h", 1, ins)
                    for n in range(NP_):
                        wait("tap", n + 1)
                        for d in range(1, 4):
                            ins = stt(y[:, n, d:L], bank[2 + n % 2][:, 0:L - d], cw[:, n, 3 - d:4 - d], y[:, n, d:L], ALU.mult, ALU.add)
                            if d < 3:
                                link(ins)
                        done("cv", n + 1, ins)
                    wait("ab_ps", 1)
                    ab = bank[0][:, 0:TT * 2 * DH].rearrange("p (t n) -> p t n", t=TT)
                    link(tt(t1[:], ab[:, :, 0:DH], dtb[:].unsqueeze(1).broadcast_to([P, TT, DH]), ALU.add))
                    done("ab", 1, v.tensor_copy(bt[:], ab[:, :, DH:2 * DH]))
                    wait("abs", 2)
                    link(ts(zr[:], sp_[:], 2.0, None, ALU.add))
                    link(v.reciprocal(zr[:], zr[:]))
                    link(tt(zr[:], sp_[:], zr[:], ALU.mult))
                    link(tt(z2[:], zr[:], zr[:], ALU.mult))
                    link(ts(sp_[:], z2[:], 1.0 / 13.0, None, ALU.mult))
                    for odd in (11, 9, 7, 5, 3):
                        link(stt(sp_[:], sp_[:], 1.0 / odd, z2[:], ALU.add, ALU.mult))
                    link(stt(sp_[:], sp_[:], 1.0, zr[:], ALU.add, ALU.mult))
                    link(ts(t1[:], t1[:], 0.0, None, ALU.max))
                    link(stt(sp_[:], sp_[:], 2.0, t1[:], ALU.mult, ALU.add))
                    done("g_in", 1, tt(sp_[:], sp_[:], nexpA[:].unsqueeze(1).broadcast_to([P, TT, DH]), ALU.mult))
                    wait("a", 1)
                    done("am", 1, ts(am[:], a_[:], nottok0[:, 0:1], None, ALU.mult))
                    wait("te", NP_)
                    qk3 = qk[:].rearrange("p t a h d -> p t (a h) d")
                    sq3 = sq[:].rearrange("p t (g d) -> p t g d", d=KD)
                    link(tt(sq3, qk3, qk3, ALU.mult))
                    link(v.tensor_reduce(ssq[:].rearrange("p (t g) -> p t g", t=TT), sq3, AX_X, ALU.add))
                    done("l2v", 1, ts(ssq[:], ssq[:], 1.0, RMS_EPS, ALU.mult, ALU.add))
                    wait("l2r", 1)
                    sq4 = ssq[:].rearrange("p (t a h) -> p t a h", t=TT, a=2)
                    link(ts(sq4[:, :, 0, :], sq4[:, :, 0, :], float(KD) ** -0.5, None, ALU.mult))
                    link(tt(qk3, qk3, ssq[:].rearrange("p (t g) -> p t g", t=TT).unsqueeze(3).broadcast_to([P, TT, 2 * DH, KD]), ALU.mult))
                    wait("beta", 1)
                    done("qk", 1, tt(kb[:], qk[:, :, 1, :, :], bt[:].unsqueeze(3).broadcast_to([P, TT, DH, KD]), ALU.mult))
                    done("vb", 1, tt(v_[:], v_[:], bt[:].unsqueeze(3).broadcast_to([P, TT, DH, VD]), ALU.mult))
                    done("S", 1, v.memset(S[:].rearrange("p a b c -> p (a b c)"), 0.0))

                    def prepare(t):
                        i = t % 2
                        wait("aB", t + 1)
                        done("DT", t + 1, v.tensor_tensor_scan(flat(DT_[i][:]), bank[i][:], flat(id4[:]), 0.0, ALU.mult, ALU.add))
                        wait("kk", t + 1)
                        products = [bank[2 + 2 * i + k][:].rearrange("p (w n j) -> p w n j", w=2, n=H2) for k in range(2)]
                        for k in range(2):
                            ins = stt(nAT[i][:, k::2, :], products[k][:, 0, :, :], -1.0, DT_[i][:, k::2, :], ALU.mult, ALU.mult)
                            link(ins) if k == 0 else done("nat", t + 1, ins)
                        wait("gm", t + 1)
                        done("gmr", t + 1, v.tensor_copy(gam[i][:], bank[i][:, 0:DH]))
                        for k in range(2):
                            link(tt(QD[i][:, k::2, :], products[k][:, 1, :, :], DT_[i][:, k::2, :], ALU.mult))
                        link(stt(gbn[i][:], gam[i][:], -1.0, bt[:, t, :], ALU.mult, ALU.mult))
                        link(tt(kd[i][:], qk[:, t, 1, :, :], DT_[i][:, :, P - 1:P].broadcast_to([P, DH, KD]), ALU.mult))
                        wait("gc", t + 1)
                        done("prep", t + 1, v.tensor_copy(gC[i][:], bank[i][:, 8:12]))

                    def grow(t, lv):
                        i = t % 2
                        mask = level[:, lv, :].unsqueeze(1).broadcast_to([P, DH, P])
                        wait("z", zcount(t, lv))
                        if lv == 0:
                            wait("rst", t + 1)
                        v.memset(hold[:], 0.0)
                        if lv < LEVELS - 1:
                            done("T", tcount(t, lv), v.copy_predicated(T[i][:], mask, heads(bank[4 + i][:])))
                        else:
                            done("Uf", t + 1, v.copy_predicated(U[i][:], mask, heads(bank[4 + i][:])))

                    def recur(t):
                        i = t % 2
                        wait("ks", t + 1)
                        for h in range(DH):
                            ins = stt(R[:, h, :], bank[6][:, h * VD:(h + 1) * VD], gbn[i][:, h:h + 1], v_[:, t, h, :], ALU.mult, ALU.add)
                        done("R", t + 1, ins)
                        wait("su", t + 1)
                        for h in range(DH):
                            p, k, r = h // 2, h % 2, slice((h % 2) * KD, (h % 2 + 1) * KD)
                            ins = stt(S[r, p, k, :], S[r, p, k, :], gC[i][r, h:h + 1], bank[6][r, p * VD:(p + 1) * VD], ALU.mult, ALU.add)
                        done("S", t + 2, ins)
                        wait("op", t + 1)
                        done("o", t + 1, tt(heads(o[:, t, :]), heads(bank[7][:]), QSe[:], ALU.add))

                    for pair in range(TT // 2):
                        two = (2 * pair, 2 * pair + 1)
                        for t in two:
                            prepare(t)
                        for lv in range(LEVELS):
                            for t in two:
                                grow(t, lv)
                        for t in two:
                            recur(t)
                    wait("osq", 1)
                    link(v.tensor_reduce(ov[:].rearrange("p (t h) -> p t h", t=TT), sq[:].rearrange("p t (h d) -> p t h d", h=DH), AX_X, ALU.add))
                    done("ov", 1, ts(ov[:], ov[:], 1.0 / VD, RMS_EPS, ALU.mult, ALU.add))
                    wait("orr", 1)
                    for t in range(TT):
                        for h in range(DH):
                            c = slice(h * VD, (h + 1) * VD)
                            ins = stt(og[:, t, c], o[:, t, c], orr[:, t * DH + h:t * DH + h + 1], gt[:, t, c], ALU.mult, ALU.mult)
                    done("og", 1, ins)
                    for p in range(2):
                        wait("en", p + 1)
                        ins = tt(flat(xa[:, 2 * p:2 * p + 2, :]), bank[4 + p][:], flat(x2[:, 2 * p:2 * p + 2, :]), ALU.add)
                        link(ins) if p == 0 else done("xa", 1, ins)
                    norm(xa, n1, 2, "n2")
                    for p in range(2):
                        wait("y2", p + 1)
                        ins = tt(h_[:, 2 * p:2 * p + 2, :], bank[2 + p][:].rearrange("p (t d) -> p t d", t=2),
                                 b2_s[:].unsqueeze(1).broadcast_to([P, 2, D]), ALU.add)
                        link(ins) if p == 0 else done("yb", 1, ins)
                    link(tt(xa[:], xa[:], x2[:], ALU.add))
                    wait("ge", 1)
                    link(tt(u_[:], h_[:], xa[:], ALU.add))
                    dve.sem_inc(x_free, 1)
                    dve.wait_ge(x3_free, b + 1)
                    norm(u_, x3, 3, "x3")
                    assert link.n == GSTEPS, link.n

            @block.scalar
            def _(act):
                act.wait_ge(w_in, 16 * 20)
                nc.scalar.activation(nexpA[:], nexpA[:], ACT.Exp).then_inc(aprep, 1)
                a_op = nc.scalar.activation
                act.wait_ge(aprep, 1)
                with act.Fori(0, B) as b:
                    wait, done = waiter(act, b)
                    wait("u", 1)
                    for t in range(TT):
                        ins = a_op(sq[:, t, 0:D], u_[:, t, :], ACT.Square, accum_out=ss[:, t:t + 1])
                    done("ss", 1, ins)
                    wait("hT_ps", 1)
                    for c in range(DT):
                        done("hT", c + 1, a_op(hT[:, c, :], bank[c][:], ACT.Copy, scale=rw[:, c:c + 1]))
                    for n in range(NP_ + 2):
                        if n < NP_:
                            wait("pj", n + 1)
                            done("tap", n + 1, a_op(y[:, n, :], bank[2 + n % 2][:], ACT.Copy, scale=cw[:, n, 3:4]))
                        if 1 <= n <= NP_:
                            wait("cv", n)
                            done("si", n, a_op(y[:, n - 1, :], y[:, n - 1, :], ACT.Silu))
                        if n >= 2:
                            m = n - 2
                            wait("tk", m + 1)
                            src = bank[4 + m % 2][:].rearrange("p (t c) -> p t c", t=TT)
                            if m < 4:
                                dst = qk[:, :, m // 2, 2 * (m % 2):2 * (m % 2) + 2, :].rearrange("p t h d -> p t (h d)")
                            else:
                                dst = v_[:, :, m - 4, :]
                            done("te", m + 1, nc.scalar.copy(dst, src))
                    for t in range(TT):
                        wait("gp", t + 1)
                        done("gt", t + 1, a_op(gt[:, t, :], bank[6 + t % 2][:], ACT.Silu))
                    wait("ab", 1)
                    done("beta", 1, a_op(bt[:], bt[:], ACT.Sigmoid))
                    done("abs", 1, a_op(sp_[:], t1[:], ACT.Abs))
                    done("abs", 2, a_op(sp_[:], sp_[:], ACT.Exp, scale=-1.0))
                    wait("g_in", 1)
                    done("a", 1, a_op(a_[:], sp_[:], ACT.Exp))
                    for n in range(6):
                        wait("bk", n + 1)
                        done("qkT", n + 1, nc.scalar.copy(XT[:, n, :], bank[2 + n][:]))
                    for pair in range(TT // 2):
                        two = (2 * pair, 2 * pair + 1)
                        for lv in range(LEVELS):
                            for t in two:
                                i = t % 2
                                if lv > 0:
                                    wait("ut", tcount(t, lv - 1))
                                    done("U", tcount(t, lv - 1), nc.scalar.copy(U[i][:], heads(bank[i][:])))
                                    wait("y", tcount(t, lv - 1))
                                    done("Ye", tcount(t, lv - 1), nc.scalar.copy(Y[i][:], heads(bank[2 + i][:])))
                        for t in two:
                            i = t % 2
                            wait("ks", t + 1)
                            for h in range(DH):
                                ins = a_op(QSe[:, h, :], bank[7][:, h * VD:(h + 1) * VD], ACT.Copy, scale=gam[i][:, h:h + 1])
                            done("qse", t + 1, ins)
                            wait("dl", t + 1)
                            done("de", t + 1, nc.scalar.copy(dl[:], heads(bank[6][:])))
                    wait("o", TT)
                    done("osq", 1, a_op(flat(sq[:]), flat(o), ACT.Square))
                    for c in range(DH):
                        wait("oT", c + 1)
                        done("oTe", c + 1, nc.scalar.copy(XT[:, c, :], bank[c][:]))
                    wait("n2T", 1)
                    for c in range(DT):
                        done("h2T", c + 1, a_op(hT[:, c, :], bank[c][:], ACT.Identity, scale=g2[:, c:c + 1], bias=bb2[:, c:c + 1]))
                    wait("yb", 1)
                    done("ge", 1, a_op(flat(h_[:]), flat(h_[:]), ACT.Gelu))

            @block.tensor
            def _(pe):
                pe.wait_ge(w_in, 16 * 20)
                pe.wait_ge(ready, 1)
                pe.wait_ge(aprep, 3)
                mm, tp = nc.tensor.matmul, nc.tensor.transpose
                with pe.Fori(0, B) as b:
                    wait, _ = waiter(pe, b)

                    def mark(name, ins):
                        ins.then_inc(s[name], 1)

                    def turn(src, name):
                        for c in range(DT):
                            for t in range(TT):
                                ins = tp(bank[c][:, t * P:(t + 1) * P], src[:, t, c * P:(c + 1) * P], ident[:])
                        mark(name, ins)

                    wait("h", 1)
                    turn(h_, "hT_ps")
                    wait("hT", 2)
                    for n in range(NP_ + 2):
                        if n < NP_:
                            if n >= 2:
                                wait("cv", n - 1)
                            for c in range(DT):
                                ins = mm(bank[2 + n % 2][:], wqkv[:, c, n * P:(n + 1) * P], hT[:, c, :], start=(c == 0), stop=(c == DT - 1))
                            mark("pj", ins)
                        if n >= 2:
                            m = n - 2
                            wait("si", m + 1)
                            if m >= 2:
                                wait("te", m - 1)
                            for t in range(TT):
                                ins = tp(bank[4 + m % 2][:, t * P:(t + 1) * P], y[:, m, t * P:(t + 1) * P], ident[:])
                            mark("tk", ins)
                    for t in range(TT):
                        for c in range(DT):
                            ins = mm(bank[0][:, t * 2 * DH:(t + 1) * 2 * DH], hT[:, c, t * P:(t + 1) * P], wab[:, c, :],
                                     start=(c == 0), stop=(c == DT - 1))
                    mark("ab_ps", ins)
                    for t in range(TT):
                        if t >= 2:
                            wait("gt", t - 1)
                        for c in range(DT):
                            ins = mm(bank[6 + t % 2][:], hT[:, c, t * P:(t + 1) * P], wg_s[:, c, :], start=(c == 0), stop=(c == DT - 1))
                        mark("gp", ins)
                    wait("gt", TT)
                    wait("qk", 1)
                    for n in range(6):
                        for t in range(TT):
                            src = (kb[:, t, :, :] if n >= 4 else qk[:, t, n // 2, :, :])[:, 2 * (n % 2):2 * (n % 2) + 2, :]
                            ins = tp(bank[2 + n][:, t * P:(t + 1) * P], flat(src), ident[:])
                        mark("bk", ins)

                    def prepare(t):
                        i, tok = t % 2, slice(t * P, (t + 1) * P)
                        wait("am", 1)
                        for h in range(DH):
                            ins = mm(bank[i][:, h * P:(h + 1) * P], am[:, t, h:h + 1].broadcast_to([P, P]), ident[:], start=True, stop=True)
                        mark("aB", ins)
                        wait("qkT", 6)
                        for h in range(DH):
                            r, n, dst = slice((h % 2) * KD, (h % 2 + 1) * KD), h // 2, bank[2 + 2 * i + h % 2]
                            mm(dst[:, n * P:(n + 1) * P], XT[r, 2 + n, tok], XT[r, 4 + n, tok], start=True, stop=True)
                            ins = mm(dst[:, (2 + n) * P:(3 + n) * P], XT[r, 2 + n, tok], XT[r, n, tok], start=True, stop=True)
                        mark("kk", ins)
                        wait("DT", t + 1)
                        for h in range(DH):
                            ins = mm(bank[i][:, h:h + 1], DT_[i][0:1, h, :], a_[0:1, t, h:h + 1], start=True, stop=True)
                        mark("gm", ins)
                        wait("gmr", t + 1)
                        mark("gc", mm(bank[i][:, 8:12], last[:], gam[i][:], start=True, stop=True))

                    def grow_first(t, lv):
                        i = t % 2
                        if lv == 0:
                            wait("nat", t + 1)
                            return
                        wait("T", tcount(t, lv - 1))
                        for h in range(DH):
                            ins = tp(bank[i][:, h * P:(h + 1) * P], T[i][:, h, :], ident[:])
                        mark("ut", ins)
                        for h in range(DH):
                            ins = mm(bank[2 + i][:, h * P:(h + 1) * P], nAT[i][:, h, :], T[i][:, h, :], start=True, stop=True)
                        mark("y", ins)

                    def grow_second(t, lv):
                        i = t % 2
                        if lv == 0:
                            wait("prep", t - i + 2)
                            for h in range(DH):
                                ins = tp(bank[4 + i][:, h * P:(h + 1) * P], nAT[i][:, h, :], ident[:])
                        else:
                            wait("Ye", tcount(t, lv - 1))
                            wait("U", tcount(t, lv - 1))
                            for h in range(DH):
                                lhs, rhs = (U[i], Y[i]) if lv < LEVELS - 1 else (Y[i], U[i])
                                ins = mm(bank[4 + i][:, h * P:(h + 1) * P], lhs[:, h, :], rhs[:, h, :], start=True, stop=True)
                        mark("z", ins)

                    def recur(t):
                        i, tok = t % 2, slice(t * P, (t + 1) * P)
                        wait("S", t + 1)
                        if t > 0:
                            wait("o", t)
                        for dst, n0 in ((bank[6], 2), (bank[7], 0)):
                            for n in range(H2):
                                ins = mm(dst[:, 2 * n * VD:2 * (n + 1) * VD], XT[:, n0 + n, tok], flat(S[:, n, :, :]), start=True, stop=True)
                        mark("ks", ins)
                        wait("R", t + 1)
                        wait("Uf", t + 1)
                        for h in range(DH):
                            ins = mm(bank[6][:, h * VD:(h + 1) * VD], U[i][:, h, :], R[:, h, :], start=True, stop=True)
                        mark("dl", ins)
                        wait("de", t + 1)
                        for h in range(DH):
                            r = slice((h % 2) * KD, (h % 2 + 1) * KD)
                            ins = mm(bank[6][r, (h // 2) * VD:(h // 2 + 1) * VD], kd[i][:, h, :], dl[:, h, :], start=True, stop=True)
                        mark("su", ins)
                        wait("qse", t + 1)
                        for h in range(DH):
                            ins = mm(bank[7][:, h * VD:(h + 1) * VD], QD[i][:, h, :], dl[:, h, :], start=True, stop=True)
                        mark("op", ins)

                    wait("vb", 1)
                    for pair in range(TT // 2):
                        two = (2 * pair, 2 * pair + 1)
                        for t in two:
                            prepare(t)
                        for lv in range(LEVELS):
                            for t in two:
                                grow_first(t, lv)
                            for t in two:
                                grow_second(t, lv)
                        for t in two:
                            recur(t)
                    wait("og", 1)
                    for c in range(DH):
                        for t in range(TT):
                            ins = tp(bank[c][:, t * P:(t + 1) * P], og[:, t, c * P:(c + 1) * P], ident[:])
                        mark("oT", ins)
                    for t in range(TT):
                        for c in range(DH):
                            if t == 0:
                                wait("oTe", c + 1)
                            ins = mm(bank[4 + t // 2][:, (t % 2) * D:(t % 2 + 1) * D], XT[:, c, t * P:(t + 1) * P], wo_s[:, c, :],
                                     start=(c == 0), stop=(c == DH - 1))
                        if t % 2:
                            mark("en", ins)
                    wait("n2", 1)
                    turn(n1, "n2T")
                    wait("h2T", 2)
                    for t in range(TT):
                        for c in range(DT):
                            ins = mm(bank[2 + t // 2][:, (t % 2) * D:(t % 2 + 1) * D], hT[:, c, t * P:(t + 1) * P], w2_s[:, c, :],
                                     start=(c == 0), stop=(c == DT - 1))
                        if t % 2:
                            mark("y2", ins)



INPUTS = dict(
    L0_attn_x=(B, L, D), L0_attn_conv_w=(D, 4), L0_attn_wq=(D, DK_ALL), L0_attn_wkg=(D, DK_ALL), L0_attn_wv=(D, D),
    L0_attn_wg=(D, D), L0_attn_bg=(D,), L0_attn_wout=(D, D), L0_attn_aug_balance=(DK_ALL,),
    L0_ffn_w_g=(EXPERTS, D), L0_ffn_c_fc=(EXPERTS, D, FF), L0_ffn_c_proj=(EXPERTS, FF, D),
    L1_attn_ln1_g=(D,), L1_attn_ln1_b=(D,), L1_attn_ln2_g=(D,), L1_attn_ln2_b=(D,), L1_attn_rms_in_w=(D,),
    L1_attn_Wq=(D, DH * KD), L1_attn_Wk=(D, DH * KD), L1_attn_Wv=(D, DH * VD), L1_attn_conv_q_w=(DH * KD, 4),
    L1_attn_conv_k_w=(DH * KD, 4), L1_attn_conv_v_w=(DH * VD, 4), L1_attn_Wa=(D, DH), L1_attn_dt_bias=(DH,),
    L1_attn_A_log=(DH,), L1_attn_Wb=(D, DH), L1_attn_Wg=(D, DH * VD), L1_attn_o_norm_w=(VD,), L1_attn_Wo=(DH * VD, D),
    L1_attn_W2=(D, D), L1_attn_b2=(D,),
    L1_ffn_fc1_A=(PRIM, D, RANK), L1_ffn_fc1_B=(PRIM, RANK, FF), L1_ffn_fc2_A=(PRIM, FF, RANK),
    L1_ffn_fc2_B=(PRIM, RANK, D), L1_ffn_fc1_logits=(PRIM,), L1_ffn_fc2_logits=(PRIM,))


def build_program(nc, a, out_rows):
    scratch = lambda name, rows, cols: nc.dram_tensor(name, (rows, cols), F32).ap()
    x_late = scratch("x_late", 2 * NTOK, D)
    x3_rows, x2_rows = x_late[0:NTOK, :], x_late[NTOK:2 * NTOK, :]
    x1_rows, logits = scratch("x1_rows", NTOK, D), scratch("router_logits", NTOK, EXPERTS)
    slots, slots_out = scratch("slots", TRASH + TOPK * NTOK, D), scratch("slots_out", SLOTS, D)
    w1, w2 = scratch("ffn_w1", D, FF), scratch("ffn_w2", FF, D)

    linear_attention(nc, a["x_rows"], a["xT_rows"], *[a["L0_attn_" + n] for n in
                     ("conv_w", "wq", "wkg", "wv", "wg", "bg", "wout", "aug_balance")], a["w_gate"], x1_rows, logits)
    with ExitStack() as ctx:
        held = lambda name, dt: ctx.enter_context(nc.sbuf_tensor(name, [P, TOPK, NTOK // P], dt))
        put_at, get_at, weight = held("put_at", U32), held("get_at", U32), held("weight", F32)
        route(nc, logits, put_at, get_at, weight, slots)
        dispatch(nc, x1_rows, put_at, slots)
        mlp(nc, slots, a["moe_w1"], a["moe_w2"], slots_out, EXPERTS, CAP // BLK, False)
        combine(nc, x1_rows, slots_out, get_at, weight, x2_rows)
    delta_rule(nc, x2_rows, *[a["L1_attn_" + n] for n in
               ("ln1_g", "ln1_b", "rms_in_w", "Wq", "Wk", "Wv", "conv_q_w", "conv_k_w", "conv_v_w", "Wa", "dt_bias",
                "A_log", "Wb", "Wg", "o_norm_w", "Wo", "ln2_g", "ln2_b", "W2", "b2")], x3_rows)
    compose_weights(nc, a["L1_ffn_fc1_logits"], a["fc1_aT"], a["fc1_b"], a["L1_ffn_fc2_logits"], a["fc2_aT"], a["fc2_b"],
                    w1, w2)
    mlp(nc, x_late[0:NTOK + BLK, :], w1, w2, out_rows, 1, NTOK // BLK, True)


def kernel(**inputs):
    import concourse.bacc as bacc
    import numpy as np
    from concourse.bass_utils import run_bass_kernel_spmd

    rows = lambda v: np.ascontiguousarray(v).reshape(-1, v.shape[-1])
    given = {name: np.asarray(inputs[name]) for name in INPUTS}
    for name, shape in INPUTS.items():
        assert given[name].shape == shape, name
    take = given.pop
    x = take("L0_attn_x")
    laid = dict(x_rows=rows(x), xT_rows=rows(x.transpose(0, 2, 1)), w_gate=rows(take("L0_ffn_w_g").T),
                moe_w1=rows(take("L0_ffn_c_fc")), moe_w2=rows(take("L0_ffn_c_proj")),
                fc1_aT=rows(take("L1_ffn_fc1_A").transpose(0, 2, 1)), fc1_b=rows(take("L1_ffn_fc1_B")),
                fc2_aT=rows(take("L1_ffn_fc2_A").transpose(0, 2, 1)), fc2_b=rows(take("L1_ffn_fc2_B")))
    laid.update({name: np.ascontiguousarray(v) for name, v in given.items()})

    nc = bacc.Bacc("TRN2", target_bir_lowering=False, num_devices=1)
    aps = {name: nc.dram_tensor(f"in_{name}", v.shape, F32, kind="ExternalInput").ap() for name, v in laid.items()}
    out_rows = nc.dram_tensor("out_rows", (NTOK, D), F32, kind="ExternalOutput").ap()
    build_program(nc, aps, out_rows)
    r = run_bass_kernel_spmd(nc, [{f"in_{name}": v for name, v in laid.items()}], core_ids=[0])
    return r.results[0]["out_rows"].reshape(B, L, D)
```

```python
from contextlib import ExitStack

import concourse.bass as bass
from concourse import mybir

F32 = mybir.dt.float32
I32 = mybir.dt.int32
U32 = mybir.dt.uint32
ALU = mybir.AluOpType
ACT = mybir.ActivationFunctionType
AX_X = mybir.AxisListType.X

P = 128
B, L, D = 16, 512, 256
NTOK = B * L
DT = D // P
TT = L // P
LN_EPS = 1e-5
EXPERTS, TOPK, FF = 8, 2, 1024
FT = FF // P
CAP = max(4, int(1.25 * NTOK * TOPK / EXPERTS))
SLOTS = EXPERTS * CAP
BLK = 512
TRASH = SLOTS + BLK
PRIM, RANK, SEL = 64, 64, 32


class Chain:

    def __init__(self, eng, sem, base=0):
        self.eng, self.sem, self.base, self.n = eng, sem, base, 0

    def __call__(self, ins):
        self.n += 1
        ins.then_inc(self.sem, 1)
        self.eng.wait_ge(self.sem, self.base + self.n)


def opener(nc, ctx, tag):
    sems = []

    def close():
        nc.clear_and_free_semaphores(sems)
        nc.all_engine_barrier()

    ctx.callback(close)

    def sb(name, shape, dt=F32):
        return ctx.enter_context(nc.sbuf_tensor(f"{tag}_{name}", shape, dt))

    def ps(name, shape, dt=F32):
        return ctx.enter_context(nc.psum_tensor(f"{tag}_{name}", shape, dt))

    def sem(name):
        sems.append(nc.alloc_semaphore(f"{tag}_{name}"))
        return sems[-1]

    return sb, ps, sem


def identity_tile(nc, pool, tile, zeroed, made):
    nc.gpsimd.memset(tile[:], 0.0).then_inc(zeroed, 1)
    pool.wait_ge(zeroed, 1)
    nc.gpsimd.affine_select(out=tile[:], in_=tile[:], compare_op=ALU.not_equal, fill=1.0, base=0,
                            pattern=[[-1, P]], channel_multiplier=1).then_inc(made, 1)


def row_spread(nc, link, z, stats, agg, var, n, var_ready, hold):
    for t in range(n):
        ins = nc.vector.bn_stats(stats[:, t, :], z[:, t, :])
    link(ins)
    nc.vector.memset(hold[:], 0.0)
    for t in range(n):
        ins = nc.vector.bn_aggr(agg[:, t, :], stats[:, t, :])
    link(ins)
    nc.vector.tensor_scalar(var[:], agg[:, :, 1], LN_EPS, None, ALU.add).then_inc(var_ready, 1)


def row_scale(nc, z, out, agg, rstd, n):
    for t in range(n):
        ins = nc.vector.tensor_scalar(out[:, t, :], z[:, t, :], agg[:, t, 0:1], rstd[:, t:t + 1],
                                      ALU.subtract, ALU.mult)
    return ins


def row_norm(nc, dve, link, z, out, stats, agg, var, rstd, n, var_ready, rstd_ready, count, hold):
    row_spread(nc, link, z, stats, agg, var, n, var_ready, hold)
    dve.wait_ge(rstd_ready, count)
    return row_scale(nc, z, out, agg, rstd, n)


def compose_weights(nc, ctx, block, logits1, a1, b1, logits2, a2, b2, w1_out, w2_out):
    KT = SEL * RANK // P
    ROW2 = 32
    sb, ps, sem = opener(nc, ctx, "cw")
    lg = sb("logits", [64, 2, PRIM])
    vals = sb("vals", [64, SEL])
    idx = sb("idx", [64, SEL], U32)
    ew = sb("ew", [64, SEL])
    neg = sb("neg", [64, 1])
    tot = sb("tot", [64, 1])
    rtot = sb("rtot", [64, 1])
    one = sb("one", [64, 64])
    wcol = sb("wcol", [P, 2, KT])
    A1 = [sb(f"A1_{u}", [P, D]) for u in range(2)]
    B1 = [sb(f"B1_{u}", [P, FF]) for u in range(2)]
    A2 = [sb(f"A2_{u}", [P, FF]) for u in range(2)]
    B2 = [sb(f"B2_{u}", [P, D]) for u in range(2)]
    zero = sb("zero", [P, 512])
    acc1 = [ps(f"acc1_{n}", [P, 512]) for n in range(4)]
    acc2 = [ps(f"acc2_{n}", [P, 512]) for n in range(4)]
    loaded, cleared, step, neg_ready, exp_done = (sem(n) for n in ("loaded", "cleared", "step", "neg", "exp"))
    picked, w_ready, w_bcast, w_col = sem("picked"), sem("w_ready"), sem("w_bcast"), sem("w_col")
    in_u = [sem(f"in{u}") for u in range(2)]
    scaled, used, zeroed, acc_done, stored = (sem(n) for n in ("scaled", "used", "zeroed", "acc_done", "stored"))
    out_ready = sem("out_ready")
    w1s = sb("w1s", [P, DT, FF])
    w2s = sb("w2s", [P, FT, D])

    @block.sync
    def _(sp):
        sp.wait_ge(cleared, 1)
        sp.dma_start(lg[0:1, 0, :], logits1.rearrange("(a n) -> a n", a=1)).then_inc(loaded, 16)
        sp.dma_start(lg[ROW2:ROW2 + 1, 0, :], logits2.rearrange("(a n) -> a n", a=1)).then_inc(loaded, 16)
        sp.wait_ge(picked, SEL // 8)
        with sp.Fori(0, KT // 2) as t:
            for u in range(2):
                for half in range(2):
                    k1 = sp.value_load(idx[0:1, bass.ds(t * 4 + 2 * u + half, 1)], min_val=0, max_val=PRIM - 1)
                    k2 = sp.value_load(idx[ROW2:ROW2 + 1, bass.ds(t * 4 + 2 * u + half, 1)], min_val=0, max_val=PRIM - 1)
                    rows = slice(half * RANK, (half + 1) * RANK)
                    s1, s2 = bass.ds(k1 * RANK, RANK), bass.ds(k2 * RANK, RANK)
                    srcs = [a1[s1, :], b1[s1, :], a2[s2, :], b2[s2, :]]
                    if half == 0:
                        sp.wait_ge(used, t * 2 + u + 1)
                    for tile, src in zip((A1[u], B1[u], A2[u], B2[u]), srcs):
                        sp.dma_start(tile[rows, :], src).then_inc(in_u[u], 16)
        sp.wait_ge(out_ready, 8)
        sp.dma_start(w1_out.rearrange("(t p) n -> p t n", p=P), w1s[:]).then_inc(stored, 16)
        sp.dma_start(w2_out.rearrange("(t p) n -> p t n", p=P), w2s[:]).then_inc(stored, 16)
        sp.wait_ge(stored, 32)

    @block.vector
    def _(dve):
        link = Chain(dve, step)
        nc.vector.memset(one[:], 1.0)
        nc.vector.memset(zero[:], 0.0).then_inc(zeroed, 1)
        nc.vector.memset(lg[:], 0.0).then_inc(cleared, 1)
        dve.wait_ge(loaded, 32)
        for r in range(SEL // 8):
            cur, nxt = lg[:, r % 2, :], lg[:, (r + 1) % 2, :]
            v8 = vals[:, 8 * r:8 * r + 8]
            link(nc.vector.max(v8, cur))
            nc.vector.max_index(idx[:, 8 * r:8 * r + 8], v8, cur).then_inc(picked, 1)
            link(nc.vector.match_replace(nxt, v8, cur, -3.0e38))
        nc.vector.tensor_scalar(neg[:], vals[:, 0:1], -1.0, None, ALU.mult).then_inc(neg_ready, 1)
        dve.wait_ge(exp_done, 1)
        link(nc.vector.reciprocal(rtot[:], tot[:]))
        nc.vector.tensor_scalar(ew[:], ew[:], rtot[:, 0:1], None, ALU.mult).then_inc(w_ready, 1)
        dve.wait_ge(w_bcast, 1)
        for n in range(2):
            nc.vector.tensor_copy(wcol[:, n, :], acc1[n][:, 0:KT]).then_inc(w_col, 1)
        dve.wait_ge(w_col, 2)
        with dve.Fori(0, KT // 2) as t:
            for u in range(2):
                dve.wait_ge(in_u[u], t * 128 + 128)
                for n, tile in ((0, A1[u]), (1, B2[u])):
                    nc.vector.tensor_scalar(tile[:], tile[:], wcol[:, n, bass.ds(t * 2 + u, 1)], None,
                                            ALU.mult).then_inc(scaled, 1)
        dve.wait_ge(acc_done, 1)
        for n in range(4):
            nc.vector.tensor_copy(w1s[:, n // 2, (n % 2) * 512:(n % 2) * 512 + 512], acc1[n][:]).then_inc(out_ready, 1)
        for n in range(4):
            nc.vector.tensor_copy(w2s[:, 2 * n:2 * n + 2, :].rearrange("p a d -> p (a d)"), acc2[n][:]).then_inc(out_ready, 1)

    @block.scalar
    def _(act):
        act.wait_ge(neg_ready, 1)
        nc.scalar.activation(ew[:], vals[:], ACT.Exp, bias=neg[:, 0:1], accum_out=tot[:]).then_inc(exp_done, 1)

    @block.tensor
    def _(pe):
        pe.nop().then_inc(used, 2)
        pe.wait_ge(w_ready, 1)
        for n, row in ((0, 0), (1, ROW2)):
            for half in range(2):
                ins = nc.tensor.matmul(acc1[n][half * 64:half * 64 + 64, 0:KT], one[row:row + 1, :],
                                       ew[row:row + 1, half:SEL:2], start=True, stop=True)
        ins.then_inc(w_bcast, 1)
        pe.wait_ge(w_col, 2)
        pe.wait_ge(zeroed, 1)
        for bank in acc1 + acc2:
            ins = nc.tensor.matmul(bank[:], zero[:, 0:P], zero[:], start=True, stop=False, skip_group_check=True)
        with pe.Fori(0, KT // 2) as t:
            for u in range(2):
                pe.wait_ge(scaled, t * 4 + 2 * u + 2)
                for n in range(4):
                    nc.tensor.matmul(acc1[n][:], A1[u][:, (n // 2) * P:(n // 2 + 1) * P],
                                     B1[u][:, (n % 2) * 512:(n % 2) * 512 + 512],
                                     start=False, stop=False, skip_group_check=True)
                for m in range(FT):
                    ins = nc.tensor.matmul(acc2[m // 2][:, (m % 2) * D:(m % 2 + 1) * D], A2[u][:, m * P:(m + 1) * P],
                                           B2[u][:], start=False, stop=False, skip_group_check=True)
                ins.then_inc(used, 1)
        for bank in acc1 + acc2:
            ins = nc.tensor.matmul(bank[:], zero[:, 0:P], zero[:], start=False, stop=True, skip_group_check=True)
        ins.then_inc(acc_done, 1)


NT = NTOK // P
CHOICES = ("first", "second")


def route(nc, logits, put_at, get_at, weight, slots):
    TE = NT * EXPERTS
    with ExitStack() as ctx:
        sb, ps, sem = opener(nc, ctx, "rt")
        lg = sb("lg", [P, NT, EXPERTS])
        ecol = sb("ecol", [P, NT, EXPERTS])
        token = sb("token", [P, NT])
        before = sb("before", [P, P])
        ones = sb("ones", [P, TE])
        nottile0 = sb("nottile0", [P, EXPERTS, NT])
        top = sb("top", [P, 2, NT])
        num = sb("num", [P, 2, NT])
        tmp = sb("tmp", [P, NT, EXPERTS])
        oh = [sb(f"oh{k}", [P, NT, EXPERTS]) for k in range(2)]
        total = sb("total", [P, EXPERTS, NT])
        upto = sb("upto", [P, EXPERTS, NT])
        count1 = sb("count1", [P, EXPERTS])
        rank = sb("rank", [P, NT])
        ok = sb("ok", [P, NT])
        place, aside = sb("place", [P, NT]), sb("aside", [P, NT])
        e2, den = sb("e2", [P, NT]), sb("den", [P, NT])
        ZROWS = 4 * P
        zeros = sb("zeros", [P, ZROWS // P * D])
        zero_set, filled = sem("zero_set"), sem("filled")
        p_before = [ps(f"before{k}", [P, TE]) for k in range(2)]
        p_total = [ps(f"total{k}", [P, TE]) for k in range(2)]
        lg_in, cst, step, picked, counted, e2_in, e2_done = (sem(n) for n in ("lg_in", "cst", "step", "picked", "counted", "e2_in", "e2_done"))
        wide = lambda x: x.unsqueeze(2).broadcast_to([P, NT, EXPERTS])

        with nc.Block() as block:
            @block.sync
            def _(sp):
                sp.dma_start(lg[:], logits.rearrange("(t p) e -> p t e", p=P)).then_inc(lg_in, 16)
                sp.wait_ge(zero_set, 1)
                with sp.Fori(0, TRASH // ZROWS) as n:
                    sp.dma_start(slots[bass.ds(n * ZROWS, ZROWS), :].rearrange("(p r) d -> p (r d)", p=P), zeros[:]).then_inc(filled, 16)
                sp.wait_ge(filled, TRASH // ZROWS * 16)

            @block.gpsimd
            def _(pool):
                link = Chain(pool, cst)
                nc.gpsimd.memset(zeros[:], 0.0).then_inc(zero_set, 1)
                link(nc.gpsimd.iota(ecol[:], pattern=[[0, NT], [1, EXPERTS]], base=0, channel_multiplier=0,
                                    allow_small_or_imprecise_dtypes=True))
                link(nc.gpsimd.iota(token[:], pattern=[[P, NT]], base=0, channel_multiplier=1, allow_small_or_imprecise_dtypes=True))
                link(nc.gpsimd.memset(ones[:], 1.0))
                link(nc.gpsimd.affine_select(out=before[:], in_=ones[:, 0:P], compare_op=ALU.is_gt, fill=0.0, base=0,
                                             pattern=[[1, P]], channel_multiplier=-1))
                link(nc.gpsimd.affine_select(out=nottile0[:], in_=ones[:].rearrange("p (e t) -> p e t", t=NT), compare_op=ALU.is_gt,
                                             fill=0.0, base=0, pattern=[[0, EXPERTS], [1, NT]], channel_multiplier=0))

            @block.scalar
            def _(act):
                act.wait_ge(e2_in, 1)
                nc.scalar.activation(e2[:], e2[:], ACT.Exp).then_inc(e2_done, 1)

            @block.tensor
            def _(pe):
                pe.wait_ge(cst, 5)
                for k in range(2):
                    pe.wait_ge(picked, k + 1)
                    flat = oh[k][:].rearrange("p t e -> p (t e)")
                    nc.tensor.matmul(p_before[k][:], before[:], flat, start=True, stop=True)
                    nc.tensor.matmul(p_total[k][:], ones[:, 0:P], flat, start=True, stop=True).then_inc(counted, 1)

            @block.vector
            def _(dve):
                link = Chain(dve, step)
                tt, v = nc.vector.tensor_tensor, nc.vector
                dve.wait_ge(lg_in, 16)
                dve.wait_ge(cst, 5)
                for k in range(2):
                    link(v.tensor_reduce(top[:, k, :], lg[:], AX_X, ALU.max))
                    link(tt(tmp[:], lg[:], wide(top[:, k, :]), ALU.is_lt))
                    link(v.scalar_tensor_tensor(tmp[:], tmp[:], float(EXPERTS), ecol[:], ALU.mult, ALU.add))
                    link(v.tensor_reduce(num[:, k, :], tmp[:], AX_X, ALU.min))
                    tt(oh[k][:], ecol[:], wide(num[:, k, :]), ALU.is_equal).then_inc(picked, 1)
                    dve.wait_ge(picked, k + 1)
                    if k == 0:
                        link(v.scalar_tensor_tensor(lg[:], oh[0][:], -3.0e38, lg[:], ALU.mult, ALU.add))
                tt(e2[:], top[:, 1, :], top[:, 0, :], ALU.subtract).then_inc(e2_in, 1)
                dve.wait_ge(e2_done, 1)
                link(v.tensor_scalar(den[:], e2[:], 1.0, None, ALU.add))
                link(v.reciprocal(weight[:, 0, :], den[:]))
                link(tt(weight[:, 1, :], e2[:], weight[:, 0, :], ALU.mult))
                for k in range(2):
                    dve.wait_ge(counted, k + 1)
                    link(v.tensor_copy(total[:], p_total[k][:].rearrange("p (t e) -> p e t", e=EXPERTS)))
                    flat = lambda x: x.rearrange("p e t -> p (e t)")
                    link(v.tensor_tensor_scan(flat(upto[:]), flat(nottile0[:]), flat(total[:]), 0.0, ALU.mult, ALU.add))
                    link(tt(total[:], upto[:], total[:], ALU.subtract))
                    if k == 0:
                        link(v.tensor_copy(count1[:], upto[:, :, NT - 1]))
                    else:
                        link(tt(total[:], total[:], count1[:].unsqueeze(2).broadcast_to([P, EXPERTS, NT]), ALU.add))
                    link(tt(tmp[:], p_before[k][:].rearrange("p (t e) -> p t e", e=EXPERTS), total[:].rearrange("p e t -> p t e"), ALU.add))
                    link(tt(tmp[:], tmp[:], oh[k][:], ALU.mult))
                    link(v.tensor_reduce(rank[:], tmp[:], AX_X, ALU.add))
                    link(v.tensor_scalar(ok[:], rank[:], float(CAP), None, ALU.is_lt))
                    link(tt(weight[:, k, :], weight[:, k, :], ok[:], ALU.mult))
                    link(v.tensor_scalar(place[:], rank[:], float(CAP - 1), None, ALU.min))
                    link(v.scalar_tensor_tensor(place[:], num[:, k, :], float(CAP), place[:], ALU.mult, ALU.add))
                    link(v.tensor_copy(get_at[:, k, :], place[:]))
                    link(v.tensor_scalar(aside[:], token[:], float(TRASH + k * NTOK), None, ALU.add))
                    link(tt(place[:], place[:], aside[:], ALU.subtract))
                    link(tt(place[:], place[:], ok[:], ALU.mult))
                    link(tt(place[:], place[:], aside[:], ALU.add))
                    link(v.tensor_copy(put_at[:, k, :], place[:]))


def dispatch(nc, ctx, block, x1_rows, put_at, slots):
    U = 16
    sb, ps, sem = opener(nc, ctx, "dp")
    row = [sb(f"row{u}", [P, D]) for u in range(U)]
    ix = [sb(f"ix{u}", [P, 2], U32) for u in range(U)]
    x_in, ix_in = [sem(f"x_in{u}") for u in range(U)], sem("ix_in")
    put, free = [sem(f"put{u}") for u in range(U)], [sem(f"free{u}") for u in range(U)]
    settled = sem("settled")

    @block.scalar
    def _(act):
        with act.Fori(0, NT // U) as g:
            for u in range(U):
                src = x1_rows[bass.ds(g * (U * P) + u * P, P), :]
                act.wait_ge(free[u], g + 1)
                act.dma_start(row[u][:], src).then_inc(x_in[u], 16)

    @block.gpsimd
    def _(pool):
        for u in range(U):
            pool.nop().then_inc(free[u], 1)
        with pool.Fori(0, NT // U) as g:
            for u in range(U):
                nc.gpsimd.tensor_copy(ix[u][:], put_at[:, :, bass.ds(g * U + u, 1)].rearrange("p k a -> p (k a)")).then_inc(ix_in, 1)
            for u in range(U):
                pool.wait_ge(x_in[u], g * 16 + 16)
            pool.wait_ge(ix_in, g * U + U)
            pool.sem_inc(settled, 1)
            for u in range(U):
                for k in range(2):
                    nc.gpsimd.indirect_dma_start(slots, bass.IndirectOffsetOnAxis(ap=ix[u][:, k:k + 1], axis=0),
                                                 row[u][:], None).then_inc(put[u], 16)
            for u in range(U):
                pool.wait_ge(put[u], g * 32 + 32)
                pool.nop().then_inc(free[u], 1)


def mlp(nc, x_rows, w_in, w_out, out_rows, experts, blocks, gated_norm):
    RT = BLK // P
    with ExitStack() as ctx:
        sb, ps, sem = opener(nc, ctx, "ffn" if gated_norm else "moe")
        ident = sb("ident", [P, P])
        win = sb("win", [P, DT, FF])
        wout = sb("wout", [P, FT, D])
        xin = sb("xin", [P, RT, D])
        xT = sb("xT", [P, DT, BLK])
        hT = sb("hT", [P, FT, BLK])
        rel = sb("rel", [P, 4, BLK])
        osb = sb("osb", [P, RT, D])
        fc_ps = [ps(f"fc{n}", [P, BLK]) for n in range(4)]
        tp_ps = [ps(f"tp{n}", [P, BLK]) for n in range(DT)]
        o_ps = [ps(f"o{n}", [P, 2, D]) for n in range(RT // 2)]
        id0, id1 = sem("id_zeroed"), sem("id_made")
        win_in, wout_in, x_in = sem("win_in"), sem("wout_in"), sem("x_in")
        x_turned, xT_ready, fc_done, relu_done, h_ready = (sem(n) for n in ("x_turned", "xT_ready", "fc_done", "relu_done", "h_ready"))
        o_done, o_ready, o_stored, osb_free = sem("o_done"), sem("o_ready"), sem("o_stored"), sem("osb_free")
        if gated_norm:
            xres = sb("xres", [P, RT, D])
            z = sb("z", [P, RT, D])
            stats = sb("stats", [P, RT, 6])
            agg = sb("agg", [P, RT, 2])
            var = sb("var", [P, RT])
            rstd = sb("rstd", [P, RT])
            mhalf = sb("mhalf", [P, RT])
            hold = sb("hold", [P, 1])
            res_in, step, var_ready, rstd_ready, half_set = (sem(n) for n in ("res_in", "step", "var_ready", "rstd_ready", "half_set"))
            normed = sem("normed")
        n_blocks = experts * blocks

        def rows(n):
            return x_rows[bass.ds(n * BLK, BLK), :].rearrange("(t p) d -> p t d", p=P)

        with nc.Block() as block:
            @block.sync
            def _(sp):
                sp.dma_start(xin[:], rows(0)).then_inc(x_in, 16)
                with sp.Fori(0, experts) as e:
                    w_src = w_in[bass.ds(e * D, D), :].rearrange("(t p) f -> p t f", p=P)
                    if experts > 1:
                        sp.wait_ge(h_ready, e * blocks * FT + 1)
                    sp.dma_start(win[:], w_src).then_inc(win_in, 16)
                    v_src = w_out[bass.ds(e * FF, FF), :].rearrange("(t p) d -> p t d", p=P)
                    if experts > 1:
                        sp.wait_ge(o_done, e * blocks + 1)
                    sp.dma_start(wout[:], v_src).then_inc(wout_in, 16)
                    with sp.Fori(0, blocks) as b:
                        n = e * blocks + b
                        nxt = rows(n + 1)
                        sp.wait_ge(x_turned, n + 1)
                        sp.dma_start(xin[:], nxt).then_inc(x_in, 16)
                        if gated_norm:
                            here = rows(n)
                            sp.wait_ge(o_ready, n * 2 + 2)
                            sp.dma_start(xres[:], here).then_inc(res_in, 16)
                sp.wait_ge(x_in, 16 * (n_blocks + 1))

            @block.gpsimd
            def _(pool):
                identity_tile(nc, pool, ident, id0, id1)
                pool.nop().then_inc(osb_free, 1)
                if gated_norm:
                    nc.gpsimd.memset(mhalf[:], -0.5).then_inc(half_set, 1)
                    pool.wait_ge(half_set, 1)
                with pool.Fori(0, n_blocks) as n:
                    dst = out_rows[bass.ds(n * BLK, BLK), :].rearrange("(t p) d -> p t d", p=P)
                    if gated_norm:
                        pool.wait_ge(var_ready, n + 1)
                        pool.wait_ge(half_set, 1)
                        nc.gpsimd.tensor_tensor(rstd[:], var[:], mhalf[:], ALU.pow).then_inc(rstd_ready, 1)
                        pool.wait_ge(normed, n + 1)
                    else:
                        pool.wait_ge(o_ready, n * 2 + 4)
                    pool.wait_ge(id1, 1)
                    pool.dma_start(dst, osb[:]).then_inc(o_stored, 16)
                    pool.wait_ge(o_stored, n * 16 + 16)
                    pool.nop().then_inc(osb_free, 1)

            @block.tensor
            def _(pe):
                def turn(n):
                    pe.wait_ge(x_in, n * 16 + 16)
                    pe.wait_ge(xT_ready, 2 * n + 1)
                    for c in range(DT):
                        for t in range(RT):
                            ins = nc.tensor.transpose(tp_ps[c][:, t * P:(t + 1) * P], xin[:, t, c * P:(c + 1) * P], ident[:])
                    ins.then_inc(x_turned, 1)

                pe.wait_ge(id1, 1)
                pe.nop().then_inc(xT_ready, 1)
                pe.nop().then_inc(o_done, 1)
                pe.nop().then_inc(h_ready, 1)
                turn(0)
                with pe.Fori(0, experts) as e:
                    with pe.Fori(0, blocks) as b:
                        n = e * blocks + b
                        pe.wait_ge(win_in, e * 16 + 16)
                        pe.wait_ge(xT_ready, n * 2 + 3)
                        for m in range(FT):
                            if m < 4:
                                pe.wait_ge(h_ready, n * FT + 1)
                            else:
                                pe.wait_ge(h_ready, n * FT + m - 2)
                            for c in range(DT):
                                ins = nc.tensor.matmul(fc_ps[m % 4][:], win[:, c, m * P:(m + 1) * P], xT[:, c, :],
                                                       start=(c == 0), stop=(c == DT - 1))
                            ins.then_inc(fc_done, 1)
                        turn(n + 1)
                        pe.wait_ge(wout_in, e * 16 + 16)
                        pe.wait_ge(h_ready, n * FT + FT + 1)
                        for t in range(RT):
                            if t % 2 == 0:
                                pe.wait_ge(o_ready, n * (RT // 2) + t // 2 + 1)
                            for k in range(FT):
                                ins = nc.tensor.matmul(o_ps[t // 2][:, t % 2, :], hT[:, k, t * P:(t + 1) * P], wout[:, k, :],
                                                       start=(k == 0), stop=(k == FT - 1))
                        ins.then_inc(o_done, 1)

            @block.scalar
            def _(act):
                act.nop().then_inc(o_ready, 2)
                act.wait_ge(x_turned, 1)
                for c in range(DT):
                    nc.scalar.copy(xT[:, c, :], tp_ps[c][:]).then_inc(xT_ready, 1)
                with act.Fori(0, n_blocks) as n:
                    for m in range(FT):
                        act.wait_ge(fc_done, n * FT + m + 1)
                        if gated_norm:
                            nc.scalar.activation(hT[:, m, :], fc_ps[m % 4][:], ACT.Gelu_apprx_tanh).then_inc(h_ready, 1)
                        else:
                            if m >= 4:
                                act.wait_ge(h_ready, n * FT + m - 2)
                            else:
                                act.wait_ge(h_ready, n * FT + 1)
                            nc.scalar.activation(rel[:, m % 4, :], fc_ps[m % 4][:], ACT.Relu).then_inc(relu_done, 1)
                    act.wait_ge(x_turned, n + 2)
                    for c in range(DT):
                        nc.scalar.copy(xT[:, c, :], tp_ps[c][:]).then_inc(xT_ready, 1)

            @block.vector
            def _(dve):
                with dve.Fori(0, n_blocks) as n:
                    if gated_norm:
                        link = Chain(dve, step, n * 2)
                        dve.wait_ge(res_in, n * 16 + 16)
                        dve.wait_ge(o_done, n + 2)
                        for h in range(RT // 2):
                            nc.vector.tensor_tensor(z[:, 2 * h:2 * h + 2, :], o_ps[h][:], xres[:, 2 * h:2 * h + 2, :],
                                                    ALU.add).then_inc(o_ready, 1)
                        dve.wait_ge(o_ready, n * 2 + 4)
                        dve.wait_ge(osb_free, n + 1)
                        row_norm(nc, dve, link, z, osb, stats, agg, var, rstd, RT, var_ready, rstd_ready, n + 1, hold
                                 ).then_inc(normed, 1)
                        dve.wait_ge(normed, n + 1)
                    else:
                        for m in range(FT):
                            dve.wait_ge(relu_done, n * FT + m + 1)
                            nc.vector.tensor_tensor(hT[:, m, :], rel[:, m % 4, :], rel[:, m % 4, :], ALU.mult).then_inc(h_ready, 1)
                        dve.wait_ge(o_done, n + 2)
                        dve.wait_ge(osb_free, n + 1)
                        for h in range(RT // 2):
                            nc.vector.tensor_copy(osb[:, 2 * h:2 * h + 2, :], o_ps[h][:]).then_inc(o_ready, 1)


CH, SUB = 64, 8
DK_ALL, GH, DK, DV = 128, 8, 16, 32
NCH, NSUB = L // CH, CH // SUB
VSTEPS_FRONT, VSTEPS_EARLY, VSTEPS = 7, 11, 9
GK_FLOOR = -21.0


def linear_attention(nc, x_rows, xT_rows, conv_w, wq, wkg, wv, wg, bg, wout, aug_bal, w_gate, x1_rows, logits_out):
    with ExitStack() as ctx:
        sb, ps, sem = opener(nc, ctx, "gla")
        ident = sb("ident", [P, P])
        cw = sb("conv_w", [P, DT, 4])
        wq_s, wkg_s = sb("wq", [P, DT, DK_ALL]), sb("wkg", [P, DT, DK_ALL])
        wvg_s = sb("wvg", [P, DT, 2 * D])
        wout_s = sb("wout", [P, DT, D])
        wgate_s = sb("wgate", [P, DT, EXPERTS])
        bg_s = sb("bg", [P, D])
        aug_s = sb("aug", [P, 1])
        headmask = sb("headmask", [P, GH])
        blockmask = sb("blockmask", [P, D])
        causal = sb("causal", [P, 512], I32)
        ones = sb("ones", [P, 512])
        notstart = sb("notstart", [P, NCH, CH])
        mhalf = sb("mhalf", [P, 32])
        hold = sb("hold", [P, 1])
        xp = sb("xp", [P, DT, 3 + L])
        yc = sb("yc", [P, DT, L])
        xc = sb("xc", [P, DT, L])
        ab, g, G = sb("ab", [P, L]), sb("g", [P, L]), sb("G", [P, NCH, CH])
        k_, qs = sb("k", [P, NCH, CH]), sb("q", [P, L])
        eG, eR = sb("eG", [P, NCH, CH]), sb("eR", [P, NCH, CH])
        qt, kt = sb("qt", [P, L]), sb("kt", [P, NCH, NSUB, CH])
        qhat, khat = sb("qhat", [P, L]), sb("khat", [P, NCH, CH])
        qspread = sb("qspread", [P, NCH * NSUB, GH, SUB])
        aw = sb("aw", [P, L])
        S = sb("S", [P, 2, D])
        kvm = sb("kvm", [P, D])
        xres = sb("xres", [P, TT, D])
        vn, vs, gs = sb("vn", [P, TT, D]), sb("v", [P, TT, D]), sb("gate", [P, TT, D])
        kd = sb("kd", [P, TT, P])
        Ab = sb("A", [P, 2, 512])
        on = sb("on", [P, TT, D])
        o, sg, sq = sb("o", [P, TT, D]), sb("sg", [P, TT, D]), sb("sq", [P, TT, D])
        augw = sb("augw", [P, TT, GH])
        mu, var32, rstd32 = sb("mu", [P, 32]), sb("var32", [P, 32]), sb("rstd32", [P, 32])
        oT = sb("oT", [P, DT, L])
        z, x1 = sb("z", [P, TT, D]), sb("x1", [P, TT, D])
        x1T = sb("x1T", [P, DT, L])
        lg = sb("lg", [P, TT, EXPERTS])
        stats, agg = sb("stats", [P, TT, 6]), sb("agg", [P, TT, 2])
        var, rstd = sb("var", [P, TT]), sb("rstd", [P, TT])
        pA, pB, pV, pW = ps("pA", [P, 512]), ps("pB", [P, 512]), ps("pV", [P, 512]), ps("pW", [P, 512])
        pO, pKV, pKD, pU = ps("pO", [P, 512]), ps("pKV", [P, 512]), ps("pKD", [P, 512]), ps("pU", [P, 512])

        names = ("id0 id1 consts w_in x_in xres_in masks_a step act_step pool_step "
                 "conv_done xc_ready qk_ps qk_read l1_ready g_ready ek_ready D_ready E_ready "
                 "small_D small_E q_ready kt_ready qt_ready spread_ready qhat_ready khat_ready kd_ps kd_ready "
                 "vg_ps v_ready gs_ready sg_ready A_ps A_ready kv_ps S_ready o_ps o_read aug_ps augv_ready aug_read sig_ready "
                 "var_ready rstd_ready o_final oT_ps oT_ready y_ps z_ready lnvar lnrstd x1_ready x1_stored x1_free "
                 "x1T_ps x1T_ready lg_ps lg_ready aw_ready vn_ready front_step early_step")
        s = {n: sem(n) for n in names.split()}

        with nc.Block() as block:
            @block.sync
            def _(sp):
                for tile, src in ((cw, conv_w.rearrange("(t p) k -> p t k", p=P)), (wq_s, wq.rearrange("(t p) n -> p t n", p=P)),
                                  (wkg_s, wkg.rearrange("(t p) n -> p t n", p=P)), (wout_s, wout.rearrange("(t p) n -> p t n", p=P)),
                                  (wgate_s, w_gate.rearrange("(t p) n -> p t n", p=P))):
                    sp.dma_start(tile[:], src).then_inc(s["w_in"], 16)
                sp.dma_start(wvg_s[:, :, 0:D], wv.rearrange("(t p) n -> p t n", p=P)).then_inc(s["w_in"], 16)
                sp.dma_start(wvg_s[:, :, D:2 * D], wg.rearrange("(t p) n -> p t n", p=P)).then_inc(s["w_in"], 16)
                sp.dma_start(bg_s[:], bg.rearrange("(a n) -> a n", a=1).broadcast_to([P, D])).then_inc(s["w_in"], 16)
                sp.dma_start(aug_s[:], aug_bal.rearrange("(p a) -> p a", a=1)).then_inc(s["w_in"], 16)
                with sp.Fori(0, B) as b:
                    src = xT_rows[bass.ds(b * D, D), :].rearrange("(t p) l -> p t l", p=P)
                    rsrc = x_rows[bass.ds(b * L, L), :].rearrange("(t p) d -> p t d", p=P)
                    sp.wait_ge(s["conv_done"], b * DT + 1)
                    sp.dma_start(xp[:, :, 3:3 + L], src).then_inc(s["x_in"], 16)
                    sp.wait_ge(s["z_ready"], b * 2 + 1)
                    sp.dma_start(xres[:], rsrc).then_inc(s["xres_in"], 16)
                for n in range(2):
                    sp.wait_ge(s["conv_done"], (B + n) * DT + 1)
                    sp.dma_start(xp[:, :, 3:3 + L], xT_rows[0:D, :].rearrange("(t p) l -> p t l", p=P)).then_inc(s["x_in"], 16)

            @block.gpsimd
            def _(pool):
                cst = Chain(pool, s["pool_step"])
                identity_tile(nc, pool, ident, s["id0"], s["id1"])
                cst(nc.gpsimd.memset(mhalf[:], -0.5))
                cst(nc.gpsimd.memset(ones[:], 1.0))
                cst(nc.gpsimd.affine_select(out=headmask[:], in_=ones[:, 0:GH], compare_op=ALU.is_ge, fill=0.0, base=0,
                                            pattern=[[-DK, GH]], channel_multiplier=1))
                cst(nc.gpsimd.affine_select(out=headmask[:], in_=headmask[:], compare_op=ALU.is_ge, fill=0.0, base=DK - 1,
                                            pattern=[[DK, GH]], channel_multiplier=-1))
                cst(nc.gpsimd.tensor_copy(blockmask[:].rearrange("p (h v) -> p h v", v=DV),
                                          headmask[:].unsqueeze(2).broadcast_to([P, GH, DV])))
                cst(nc.gpsimd.memset(causal[:], 1))
                for half in range(2):
                    rows = causal[half * CH:(half + 1) * CH, :].rearrange("p (h i) -> p h i", h=GH)
                    cst(nc.gpsimd.affine_select(out=rows, in_=rows, compare_op=ALU.is_ge, fill=0.0, base=0,
                                                pattern=[[0, GH], [1, CH]], channel_multiplier=-1))
                nc.gpsimd.affine_select(out=notstart[:], in_=ones[:].rearrange("p (c l) -> p c l", l=CH), compare_op=ALU.is_gt,
                                        fill=0.0, base=0, pattern=[[0, NCH], [1, CH]], channel_multiplier=0).then_inc(s["consts"], 1)
                pool.wait_ge(s["consts"], 1)
                pool.nop().then_inc(s["x1_free"], 1)

                def spread_q(b):
                    for half in range(2):
                        pool.wait_ge(s["qt_ready"], b + 1)
                        pool.wait_ge(s["consts"], 1)
                        n = NCH * NSUB // 2
                        nc.gpsimd.tensor_tensor(
                            qspread[:, half * n:(half + 1) * n, :, :],
                            qt[:, half * L // 2:(half + 1) * L // 2].rearrange("p (n i) -> p n i", i=SUB).unsqueeze(2).broadcast_to([P, n, GH, SUB]),
                            headmask[:].unsqueeze(1).unsqueeze(3).broadcast_to([P, n, GH, SUB]), ALU.mult).then_inc(s["spread_ready"], 1)
                spread_q(0)
                with pool.Fori(0, B) as b:
                    dst = x1_rows[bass.ds(b * L, L), :].rearrange("(t p) d -> p t d", p=P)
                    dst2 = logits_out[bass.ds(b * L, L), :].rearrange("(t p) d -> p t d", p=P)
                    pool.wait_ge(s["var_ready"], b + 1)
                    pool.wait_ge(s["consts"], 1)
                    nc.gpsimd.tensor_tensor(rstd32[:], var32[:], mhalf[:], ALU.pow).then_inc(s["rstd_ready"], 1)
                    spread_q(b + 1)
                    pool.wait_ge(s["lnvar"], b + 1)
                    pool.wait_ge(s["consts"], 1)
                    nc.gpsimd.tensor_tensor(rstd[:], var[:], mhalf[:, 0:TT], ALU.pow).then_inc(s["lnrstd"], 1)
                    pool.wait_ge(s["x1_ready"], b + 1)
                    pool.wait_ge(s["consts"], 1)
                    pool.dma_start(dst, x1[:]).then_inc(s["x1_stored"], 16)
                    pool.wait_ge(s["lg_ready"], b + 1)
                    pool.wait_ge(s["consts"], 1)
                    pool.dma_start(dst2, lg[:]).then_inc(s["x1_stored"], 16)
                    pool.wait_ge(s["x1_stored"], b * 32 + 32)
                    pool.nop().then_inc(s["x1_free"], 1)

            @block.vector
            def _(dve):
                cst = Chain(dve, s["masks_a"])
                dve.nop().then_inc(s["conv_done"], 1)
                dve.nop().then_inc(s["z_ready"], 1)
                cst(nc.vector.memset(xp[:, :, 0:3], 0.0))
                cst(nc.vector.memset(kt[:].rearrange("p c a j -> p (c a j)"), 0.0))
                cst(nc.vector.memset(Ab[:].rearrange("p u n -> p (u n)"), 0.0))
                dve.wait_ge(s["consts"], 1)
                dve.wait_ge(s["w_in"], 9 * 16)
                cst(nc.vector.tensor_scalar(aug_s[:], aug_s[:], 4.0, None, ALU.mult))

                def front(slot, b):
                    link = Chain(dve, s["front_step"], b * VSTEPS_FRONT)
                    link.n = 3 * slot

                    def publish(name, ins, count, each=1):
                        ins.then_inc(s[name], 1)
                        dve.wait_ge(s[name], b * each + count)

                    def add_bias(t):
                        dve.wait_ge(s["vg_ps"], b * TT + t + 1)
                        publish("gs_ready", nc.vector.tensor_tensor(gs[:, t, :], (pV, pW)[t % 2][:, D:2 * D], bg_s[:], ALU.add), t + 1, TT)

                    if slot < DT:
                        c = slot
                        if c == 0:
                            dve.wait_ge(s["x_in"], b * 16 + 16)
                        link(nc.vector.tensor_scalar(yc[:, c, :], xp[:, c, 0:L], cw[:, c, 0:1], None, ALU.mult))
                        for k in range(1, 4):
                            ins = nc.vector.scalar_tensor_tensor(yc[:, c, :], xp[:, c, k:k + L], cw[:, c, k:k + 1], yc[:, c, :],
                                                                 ALU.mult, ALU.add)
                            if k < 3:
                                link(ins)
                            else:
                                publish("conv_done", ins, c + 2, 2)
                    else:
                        for t in range(TT):
                            add_bias(t)
                        dve.wait_ge(s["l1_ready"], b + 1)
                        publish("qk_read", nc.vector.scalar_tensor_tensor(g[:], pB[:], 0.0, ab[:], ALU.min, ALU.subtract), 1)
                        publish("g_ready", nc.vector.tensor_scalar(g[:], g[:], 1.0 / 16.0, GK_FLOOR, ALU.mult, ALU.max), 1)
                        link(nc.vector.tensor_tensor_scan(G[:].rearrange("p c l -> p (c l)"), notstart[:].rearrange("p c l -> p (c l)"),
                                                          g[:], 0.0, ALU.mult, ALU.add))

                for slot in range(3):
                    front(slot, 0)
                def exponents(b, link):
                    def publish(name, ins, count, each=1):
                        ins.then_inc(s[name], 1)
                        dve.wait_ge(s[name], b * each + count)

                    blocks8 = lambda t: t.rearrange("p c (a i) -> p (c a) i", i=SUB)
                    ref8 = blocks8(G[:])[:, :, SUB // 2 - 1:SUB // 2].broadcast_to([P, NCH * NSUB, SUB])
                    link(nc.vector.tensor_tensor(blocks8(eR[:]), blocks8(G[:]), ref8, ALU.subtract))
                    publish("small_D", nc.vector.tensor_tensor(khat[:], G[:, :, CH - 1:CH].broadcast_to([P, NCH, CH]), G[:], ALU.subtract), 1)
                    for a in range(NSUB):
                        n = SUB * (a + 1)
                        r = SUB * a + SUB // 2 - 1
                        publish("D_ready", nc.vector.tensor_tensor(kt[:, :, a, 0:n], G[:, :, r:r + 1].broadcast_to([P, NCH, n]),
                                                                   G[:, :, 0:n], ALU.subtract), a + 1, NSUB)
                    dve.wait_ge(s["ek_ready"], b + 1)
                    link(nc.vector.tensor_scalar(k_[:].rearrange("p c l -> p (c l)"), g[:], -1.0, 1.0, ALU.mult, ALU.add))
                    dve.wait_ge(s["small_E"], b * 3 + 3)
                    publish("qt_ready", nc.vector.tensor_tensor(qt[:], eR[:].rearrange("p c l -> p (c l)"), qs[:], ALU.mult), 1)
                    publish("qhat_ready", nc.vector.tensor_tensor(qhat[:], eG[:].rearrange("p c l -> p (c l)"), qs[:], ALU.mult), 1)
                    publish("khat_ready", nc.vector.tensor_tensor(khat[:], khat[:], k_[:], ALU.mult), 1)
                    link(nc.vector.tensor_tensor(aw[:], qs[:], k_[:].rearrange("p c l -> p (c l)"), ALU.mult))
                    publish("aw_ready", nc.vector.tensor_scalar(aw[:], aw[:], aug_s[:, 0:1], None, ALU.mult), 1)
                    for a in range(NSUB):
                        n = SUB * (a + 1)
                        dve.wait_ge(s["E_ready"], b * NSUB + a + 1)
                        publish("kt_ready", nc.vector.tensor_tensor(kt[:, :, a, 0:n], kt[:, :, a, 0:n], k_[:, :, 0:n], ALU.mult), a + 1, NSUB)
                def recur(b, link, aside):
                    def publish(name, ins, count, each=1):
                        ins.then_inc(s[name], 1)
                        dve.wait_ge(s[name], b * each + count)

                    publish("S_ready", nc.vector.memset(S[:, 0, :], 0.0), 1, 2 * TT + 1)
                    for t in range(TT):
                        dve.wait_ge(s["A_ps"], b * TT + t + 1)
                        nc.vector.memset(hold[:], 0.0)
                        publish("A_ready", nc.vector.copy_predicated(Ab[:, t % 2, :], causal[:], pU[:]), t + 1, TT)
                        for c in range(2):
                            dve.wait_ge(s["kv_ps"], b * 2 * TT + 2 * t + c + 1)
                            link(nc.vector.tensor_tensor(kvm[:], pKV[:, 0:D], blockmask[:], ALU.mult))
                            publish("S_ready", nc.vector.scalar_tensor_tensor(
                                S[:, (c + 1) % 2, :], S[:, c, :], eG[:, 2 * t + c, CH - 1:CH], kvm[:], ALU.mult, ALU.add),
                                2 * t + c + 2, 2 * TT + 1)
                            aside(2 * t + c)
                        dve.wait_ge(s["o_ps"], b * TT + t + 1)
                        publish("o_read", nc.vector.tensor_copy(o[:, t, :], pO[:, 0:D]), t + 1, TT)
                def head_norm(b, link):
                    def publish(name, ins, count, each=1):
                        ins.then_inc(s[name], 1)
                        dve.wait_ge(s[name], b * each + count)

                    per_head = lambda x: x.rearrange("p t (h v) -> p (t h) v", v=DV)
                    dve.wait_ge(s["aug_ps"], b + 1)
                    publish("aug_read", nc.vector.tensor_copy(augw[:].rearrange("p t h -> p (t h)"), pKD[:, 0:TT * GH]), 1)
                    dve.wait_ge(s["v_ready"], b + 1)
                    publish("augv_ready", nc.vector.tensor_tensor(
                        per_head(sq[:]), per_head(vs[:]), augw[:].rearrange("p t h -> p (t h)").unsqueeze(2).broadcast_to([P, 32, DV]), ALU.mult), 1)
                    dve.wait_ge(s["sig_ready"], b + 1)
                    link(nc.vector.tensor_tensor(o[:], o[:], sq[:], ALU.add))
                    link(nc.vector.tensor_reduce(mu[:], per_head(o[:]), AX_X, ALU.add))
                    link(nc.vector.tensor_scalar(mu[:], mu[:], 1.0 / DV, None, ALU.mult))
                    spread = lambda x: x.unsqueeze(2).broadcast_to([P, 32, DV])
                    link(nc.vector.tensor_tensor(per_head(o[:]), per_head(o[:]), spread(mu[:]), ALU.subtract))
                    link(nc.vector.tensor_tensor(sq[:], o[:], o[:], ALU.mult))
                    link(nc.vector.tensor_reduce(var32[:], per_head(sq[:]), AX_X, ALU.add))
                    publish("var_ready", nc.vector.tensor_scalar(var32[:], var32[:], 1.0 / DV, LN_EPS, ALU.mult, ALU.add), 1)
                    dve.wait_ge(s["sg_ready"], b + 1)
                    link(nc.vector.tensor_tensor(o[:], o[:], sg[:], ALU.mult))
                    front(2, b + 1)
                    dve.wait_ge(s["rstd_ready"], b + 1)
                    publish("o_final", nc.vector.tensor_tensor(per_head(on[:]), per_head(o[:]), spread(rstd32[:]), ALU.mult), 1)
                def tail(n, b, link):
                    def publish(name, ins, count, each=1):
                        ins.then_inc(s[name], 1)
                        dve.wait_ge(s[name], b * each + count)

                    if n == 2:
                        dve.wait_ge(s["xres_in"], b * 16 + 16)
                        for h in range(2):
                            dve.wait_ge(s["y_ps"], b * 2 + h + 1)
                            publish("z_ready", nc.vector.tensor_tensor(z[:, 2 * h:2 * h + 2, :].rearrange("p t d -> p (t d)"), (pV, pW)[h][:],
                                                                       xres[:, 2 * h:2 * h + 2, :].rearrange("p t d -> p (t d)"), ALU.add), h + 2, 2)
                        row_spread(nc, link, z, stats, agg, var, TT, s["lnvar"], hold)
                    elif n == 3:
                        dve.wait_ge(s["x1_free"], b + 1)
                        dve.wait_ge(s["lnrstd"], b + 1)
                        publish("x1_ready", row_scale(nc, z, x1, agg, rstd, TT), 1)
                    elif n == 5:
                        dve.wait_ge(s["lg_ps"], b + 1)
                        publish("lg_ready", nc.vector.tensor_copy(lg[:].rearrange("p t e -> p (t e)"), pKD[:, 0:TT * EXPERTS]), 1)
                def conv(n, b):
                    if n in (4, 6):
                        front(n // 2 - 2, b)

                link = Chain(dve, s["early_step"], 0)
                exponents(0, link)
                recur(0, link, lambda n: conv(n, 1))
                assert link.n == VSTEPS_EARLY, link.n
                with dve.Fori(0, B) as b:
                    link = Chain(dve, s["step"], b * VSTEPS)
                    head_norm(b, link)
                    early = Chain(dve, s["early_step"], (b + 1) * VSTEPS_EARLY)
                    exponents(b + 1, early)

                    def aside(n):
                        tail(n, b, link)
                        conv(n, b + 2)

                    recur(b + 1, early, aside)
                    assert (link.n, early.n) == (VSTEPS, VSTEPS_EARLY), (link.n, early.n)

            @block.scalar
            def _(act):
                def front(b, part):
                    def publish(name, ins, count, each=1):
                        ins.then_inc(s[name], 1)
                        act.wait_ge(s[name], b * each + count)

                    if part == 0:
                        act.wait_ge(s["conv_done"], b * 2 + 3)
                        publish("xc_ready", nc.scalar.activation(xc[:].rearrange("p c l -> p (c l)"), yc[:].rearrange("p c l -> p (c l)"), ACT.Silu), 1)
                        return
                    act.wait_ge(s["qk_ps"], b + 1)
                    publish("act_step", nc.scalar.activation(ab[:], pB[:], ACT.Abs), 1, 2)
                    publish("act_step", nc.scalar.activation(ab[:], ab[:], ACT.Exp, scale=-1.0), 2, 2)
                    publish("l1_ready", nc.scalar.activation(ab[:], ab[:], ACT.Ln, bias=1.0), 1)
                    publish("q_ready", nc.scalar.mul(qs[:], pA[:], float(DK) ** -0.5), 1)
                    for t in range(TT):
                        act.wait_ge(s["gs_ready"], b * TT + t + 1)
                        publish("vn_ready", nc.scalar.copy(vn[:, t, :], (pV, pW)[t % 2][:, 0:D]), t + 1, TT)

                def exponents(b):
                    def publish(name, ins, count, each=1):
                        ins.then_inc(s[name], 1)
                        act.wait_ge(s[name], b * each + count)

                    act.wait_ge(s["small_D"], b + 1)
                    publish("ek_ready", nc.scalar.activation(g[:], g[:], ACT.Exp), 1)
                    flat = lambda x: x.rearrange("p c l -> p (c l)")
                    publish("small_E", nc.scalar.activation(flat(eR[:]), flat(eR[:]), ACT.Exp), 1, 3)
                    publish("small_E", nc.scalar.activation(flat(eG[:]), flat(G[:]), ACT.Exp), 2, 3)
                    publish("small_E", nc.scalar.activation(flat(khat[:]), flat(khat[:]), ACT.Exp), 3, 3)
                    for a in range(NSUB):
                        n = SUB * (a + 1)
                        act.wait_ge(s["D_ready"], b * NSUB + a + 1)
                        publish("E_ready", nc.scalar.activation(kt[:, :, a, 0:n], kt[:, :, a, 0:n], ACT.Exp), a + 1, NSUB)
                    publish("v_ready", nc.scalar.copy(vs[:].rearrange("p t d -> p (t d)"), vn[:].rearrange("p t d -> p (t d)")), 1)
                    act.wait_ge(s["kd_ps"], b + 1)
                    publish("kd_ready", nc.scalar.copy(kd[:].rearrange("p t k -> p (t k)"), pKD[:]), 1)
                    publish("sg_ready", nc.scalar.activation(sg[:].rearrange("p t d -> p (t d)"), gs[:].rearrange("p t d -> p (t d)"), ACT.Silu), 1)
                def tail(b):
                    def publish(name, ins, count, each=1):
                        ins.then_inc(s[name], 1)
                        act.wait_ge(s[name], b * each + count)

                    act.wait_ge(s["oT_ps"], b + 1)
                    for c in range(DT):
                        publish("oT_ready", nc.scalar.copy(oT[:, c, :], (pA, pB)[c][:]), c + 1, 2)
                    act.wait_ge(s["x1T_ps"], b + 1)
                    for c in range(DT):
                        publish("x1T_ready", nc.scalar.copy(x1T[:, c, :], (pA, pB)[c][:]), c + 1, 2)

                front(0, 0)
                front(0, 1)
                exponents(0)
                act.wait_ge(s["aw_ready"], 1)
                front(1, 0)
                with act.Fori(0, B) as b:
                    def publish(name, ins, count, each=1):
                        ins.then_inc(s[name], 1)
                        act.wait_ge(s[name], b * each + count)

                    act.wait_ge(s["augv_ready"], b + 1)
                    publish("sig_ready", nc.scalar.activation(sq[:].rearrange("p t d -> p (t d)"), sq[:].rearrange("p t d -> p (t d)"), ACT.Sigmoid), 1)
                    front(b + 1, 1)
                    exponents(b + 1)
                    tail(b)
                    front(b + 2, 0)

            @block.tensor
            def _(pe):
                pe.wait_ge(s["id1"], 1)
                pe.wait_ge(s["w_in"], 9 * 16)
                pe.wait_ge(s["consts"], 1)
                mm = nc.tensor.matmul

                def front(b):
                    pe.wait_ge(s["xc_ready"], b + 1)
                    for w, bank in ((wq_s, pA), (wkg_s, pB)):
                        for c in range(DT):
                            ins = mm(bank[:], w[:, c, :], xc[:, c, :], start=(c == 0), stop=(c == DT - 1))
                    ins.then_inc(s["qk_ps"], 1)
                    for t in range(TT):
                        if t >= 2:
                            pe.wait_ge(s["vn_ready"], b * TT + t - 1)
                        for c in range(DT):
                            ins = mm((pV, pW)[t % 2][:], xc[:, c, t * P:(t + 1) * P], wvg_s[:, c, :], start=(c == 0), stop=(c == DT - 1))
                        ins.then_inc(s["vg_ps"], 1)

                def recur(b, aside):
                    pe.wait_ge(s["khat_ready"], b + 1)
                    for t in range(TT):
                        ins = nc.tensor.transpose(pKD[:, t * P:(t + 1) * P], khat[:, 2 * t:2 * t + 2, :].rearrange("p c l -> p (c l)"),
                                                  ident[:])
                    ins.then_inc(s["kd_ps"], 1)
                    pe.wait_ge(s["spread_ready"], b * 2 + 2)
                    pe.wait_ge(s["kt_ready"], b * NSUB + NSUB)
                    pe.wait_ge(s["qhat_ready"], b + 1)
                    pe.wait_ge(s["v_ready"], b + 1)
                    for t in range(TT):
                        if t > 0:
                            pe.wait_ge(s["A_ready"], b * TT + t)
                        for c in range(2):
                            for a in range(NSUB):
                                ins = mm(pU[c * CH:(c + 1) * CH, :].rearrange("p (h i) -> p h i", h=GH)[:, :, a * SUB:(a + 1) * SUB], kt[:, 2 * t + c, a, :],
                                         qspread[:, (2 * t + c) * NSUB + a, :, :], start=True, stop=True)
                        ins.then_inc(s["A_ps"], 1)
                        pe.wait_ge(s["kd_ready"], b + 1)
                        if t > 0:
                            pe.wait_ge(s["o_read"], b * TT + t)
                        pe.wait_ge(s["A_ready"], b * TT + t + 1)
                        for c in range(2):
                            rows = slice(c * CH, (c + 1) * CH)
                            pe.wait_ge(s["S_ready"], b * (2 * TT + 1) + 2 * t + c + 1)
                            mm(pKV[:, 0:D], kd[rows, t, :], vs[rows, t, :], start=True, stop=True).then_inc(s["kv_ps"], 1)
                            mm(pO[rows, 0:D], qhat[:, (2 * t + c) * CH:(2 * t + c + 1) * CH], S[:, c, :],
                               start=True, stop=False, skip_group_check=True)
                            for h in range(GH):
                                ins = mm(pO[rows, h * DV:(h + 1) * DV], Ab[rows, t % 2, h * CH:(h + 1) * CH], vs[rows, t, h * DV:(h + 1) * DV],
                                         start=False, stop=(h == GH - 1), skip_group_check=True)
                            if c == 1:
                                ins.then_inc(s["o_ps"], 1)
                            aside(2 * t + c)

                def own_path(b):
                    pe.wait_ge(s["aw_ready"], b + 1)
                    for t in range(TT):
                        ins = mm(pKD[:, t * GH:(t + 1) * GH], aw[:, t * P:(t + 1) * P], headmask[:], start=True, stop=True)
                    ins.then_inc(s["aug_ps"], 1)

                def turn(src, name):
                    for c in range(DT):
                        for t in range(TT):
                            ins = nc.tensor.transpose((pA, pB)[c][:, t * P:(t + 1) * P], src[:, t, c * P:(c + 1) * P], ident[:])
                    ins.then_inc(s[name], 1)

                def tail(n, b):
                    if n == 0:
                        pe.wait_ge(s["o_final"], b + 1)
                        pe.wait_ge(s["q_ready"], b + 2)
                        pe.wait_ge(s["qk_read"], b + 2)
                        turn(on, "oT_ps")
                    elif n == 1:
                        pe.wait_ge(s["oT_ready"], b * 2 + 2)
                        pe.wait_ge(s["vn_ready"], (b + 1) * TT + TT)
                        for t in range(TT):
                            for c in range(DT):
                                ins = mm((pV, pW)[t // 2][:, (t % 2) * D:(t % 2 + 1) * D], oT[:, c, t * P:(t + 1) * P], wout_s[:, c, :],
                                         start=(c == 0), stop=(c == DT - 1))
                            if t % 2:
                                ins.then_inc(s["y_ps"], 1)
                    elif n == 4:
                        pe.wait_ge(s["x1_ready"], b + 1)
                        turn(x1, "x1T_ps")
                    elif n == 5:
                        pe.wait_ge(s["x1T_ready"], b * 2 + 2)
                        for t in range(TT):
                            for c in range(DT):
                                ins = mm(pKD[:, t * EXPERTS:(t + 1) * EXPERTS], x1T[:, c, t * P:(t + 1) * P], wgate_s[:, c, :],
                                         start=(c == 0), stop=(c == DT - 1))
                        ins.then_inc(s["lg_ps"], 1)

                front(0)
                recur(0, lambda n: None)
                own_path(0)
                with pe.Fori(0, B) as b:
                    front(b + 1)
                    recur(b + 1, lambda n: tail(n, b))
                    pe.wait_ge(s["lg_ready"], b + 1)
                    own_path(b + 1)


DH, KD, VD = 4, 64, 128
LEVELS = 7
RMS_EPS = 1e-6
FSTEPS, TSTEPS, PSTEPS = 43, 10, (3, 2)


def turn_of(t, n, steps=LEVELS - 1):
    return 2 * steps * (t // 2) + 2 * n + t % 2 + 1


CHUNK_PARTS = ((), ((0, 0),), ((0, 1),), ((0, 2), (1, 0)), ((1, 1),), ((1, 2),), ())
FRONT_SLOTS = 2 * (LEVELS + 1) + 4


def slot_of(pair, n):
    return pair * (LEVELS + 1) + n


def delta_rule(nc, x1_rows, slots_out, get_at, weight, ln1_g, ln1_b, rms_w, wq, wk, wv, conv_q, conv_k, conv_v, wa, dt_bias, a_log, wb, wg,
               o_norm, wo, ln2_g, ln2_b, w2, b2, x3_rows):
    with ExitStack() as ctx:
        sb, ps, sem = opener(nc, ctx, "gdr")
        H2, HV, HK = DH // 2, DH * VD, DH * KD
        NP_ = 2 * H2 + DH
        G = TT * DH
        ident = sb("ident", [P, P])
        id4 = sb("id4", [P, DH, P])
        wqkv = sb("wqkv", [P, DT, 2 * HK + HV])
        wg_s, wo_s, w2_s = sb("wg", [P, DT, HV]), sb("wo", [P, DH, D]), sb("w2", [P, DT, D])
        wab = sb("wab", [P, DT, 2 * DH])
        cw = sb("cw", [P, NP_, 4])
        g1, b1, b2_s = sb("g1", [P, D]), sb("b1", [P, D]), sb("b2", [P, D])
        rw, g2, bb2 = sb("rw", [P, DT]), sb("g2", [P, DT]), sb("bb2", [P, DT])
        onw = sb("onw", [P, 1])
        dtb, nexpA = sb("dtb", [P, DH]), sb("nexpA", [P, DH])
        ones = sb("ones", [P, P])
        last = sb("last", [P, P])
        nottok0 = sb("nottok0", [P, 1])
        HP = P // 2
        level = sb("level", [P, LEVELS - 1, HP], I32)
        mhalf, hold = sb("mhalf", [P, 32]), sb("hold", [P, 1])
        x2, x2_next = sb("x2", [P, TT, D]), sb("x2_next", [P, TT, D])
        got = [[sb(f"got{u}_{k}", [P, D]) for k in range(TOPK)] for u in range(TT)]
        ix = [sb(f"ix{u}", [P, TOPK], U32) for u in range(TT)]
        xn, fz, scr = sb("xn", [P, TT, D]), sb("fz", [P, TT, D]), sb("scr", [P, HV])
        n1, h_ = sb("n1", [P, TT, D]), sb("h", [P, TT, D])
        sq = sb("sq", [P, TT, 2 * HK])
        ss = sb("ss", [P, TT])
        hT, h2T = sb("hT", [P, DT, L]), sb("h2T", [P, DT, L])
        y = sb("y", [P, 4, L])
        qk = sb("qk", [P, TT, 2, DH, KD])
        kb = sb("kb", [P, TT, DH, KD])
        vn, v_ = sb("vn", [P, TT, DH, VD]), sb("v", [P, TT, DH, VD])
        gt = sb("gt", [P, TT, HV])
        XT = sb("XT", [P, 6, L])
        t1, zr, z2, bt, sp_, a_, am = (sb(n, [P, TT, DH]) for n in ("t1", "zr", "z2", "bt", "sp", "a", "am"))
        ssq = sb("ssq", [P, 32])
        DT_, nAT, QD, T, U = ([sb(f"{n}{i}", [P, DH, P]) for i in range(k)] for n, k in
                                  (("DT", 2), ("nAT", 2), ("QD", TT), ("T", 2), ("U", TT)))
        Y = [sb(f"Y{i}", [P, DH, HP]) for i in range(2)]
        gam, gbn, gC = ([sb(f"{n}{i}", [P, DH]) for i in range(TT)] for n in ("gam", "gbn", "gC"))
        kd = sb("kd", [P, TT, DH, KD])
        R, QSe, dl = sb("R", [P, DH, VD]), sb("QSe", [P, DH, VD]), sb("dl", [P, DH, VD])
        S = sb("S", [P, H2, 2, VD])
        ov = sb("ov", [P, G])
        orr = sb("orr", [P, G])
        xa, x3 = sb("xa", [P, TT, D]), sb("x3", [P, TT, D])
        stats, agg, var, rstd = ([sb(f"{n}{i}", [P, TT] + w) for i in range(2)]
                                 for n, w in (("stats", [6]), ("agg", [2]), ("var", []), ("rstd", [])))
        o = sb("o", [P, TT, HV])
        bank = [ps(f"bank{n}", [P, 512]) for n in range(8)]

        INV, INV1 = TT * LEVELS, TT * (LEVELS - 1)
        per = dict(ln_var=2, ln_rstd=2, u=1, ss=1, ssv=1, ssr=1, h=1, hT_ps=1, hT=2, pj=NP_, tap=NP_, cv=NP_, si=NP_, tk=NP_,
                   te=NP_, ab_ps=1, ab=1, beta=1, abs=2, g_in=1, a=1, am=1, l2v=1, l2r=1, qk=1, vb=1, bk=6, qkT=6,
                   gp=TT, gt=TT, kcopy=1, aB=TT, DT=TT, kk=TT, qd=TT, gm=TT, gmr=TT, gc=TT, prep=TT, rst=TT,
                   z=INV, T=INV1, ut=INV1, U=INV1, y=INV1, Ye=INV1, Uf=TT, S=TT + 1, ks=TT, R=TT, qse=TT, dl=TT, de=TT, su=TT,
                   op=TT, o=TT, osq=TT, ov=1, orr=1, og=1, oT=DH, oTe=DH, en=2, xa=1, tl_var=2, tl_rstd=2, n2=1, n2T=1,
                   h2T=2, y2=2, yb=1, ge=1, x3=1)
        s = {n: sem("s_" + n) for n in per}
        w_in, x3_free, stored = sem("w_in"), sem("x3_free"), sem("stored")
        front_step, tail_step = sem("front_step"), sem("tail_step")
        pair_step = [sem(f"pair_step{p}") for p in range(2)]
        x1_in, x1_free, got_in, got_used, ix_ready, gather = (sem(n) for n in "x1_in x1_free got_in got_used ix_ready gather".split())
        id0, id1, cst, ready, aprep = sem("id0"), sem("id1"), sem("cst"), sem("ready"), sem("aprep")

        def waiter(eng, b):
            def wait(name, n):
                assert 1 <= n <= per[name], name
                eng.wait_ge(s[name], b * per[name] + n)

            def done(name, n, ins):
                ins.then_inc(s[name], 1)
                wait(name, n)
            return wait, done

        flat = lambda x: x.rearrange("p a b -> p (a b)")
        heads = lambda x: x.rearrange("p (h n) -> p h n", h=DH)

        with nc.Block() as block:
            @block.sync
            def _(sp):
                chan = lambda w: w.rearrange("(t p) n -> p t n", p=P)
                row = lambda v: v.rearrange("(a n) -> a n", a=1).broadcast_to([P, v.shape[0]])
                col = lambda v: v.rearrange("(t p) -> p t", p=P)
                for dst, src in ((wqkv[:, :, 0:HK], chan(wq)), (wqkv[:, :, HK:2 * HK], chan(wk)), (wqkv[:, :, 2 * HK:], chan(wv)),
                                 (wg_s[:], chan(wg)), (wo_s[:], chan(wo)), (w2_s[:], chan(w2)), (wab[:, :, 0:DH], chan(wa)),
                                 (wab[:, :, DH:], chan(wb)), (cw[:, 0:2, :], chan(conv_q)), (cw[:, 2:4, :], chan(conv_k)),
                                 (cw[:, 4:8, :], chan(conv_v)), (g1[:], row(ln1_g)), (b1[:], row(ln1_b)), (b2_s[:], row(b2)),
                                 (dtb[:], row(dt_bias)), (nexpA[:], row(a_log))):
                    sp.dma_start(dst, src).then_inc(w_in, 16)
                with nc.allow_non_contiguous_dma(reason="a few hundred channel scales"):
                    for dst, src in ((rw[:], col(rms_w)), (g2[:], col(ln2_g)), (bb2[:], col(ln2_b)), (onw[:], col(o_norm))):
                        sp.dma_start(dst, src).then_inc(w_in, 16)
                with sp.Fori(0, B) as b:
                    src = x1_rows[bass.ds(b * L, L), :].rearrange("(t p) d -> p t d", p=P)
                    sp.wait_ge(x1_free, b + 1)
                    sp.dma_start(fz[:], src).then_inc(x1_in, 16)
                for n in (1, 2):
                    sp.wait_ge(x1_free, B + n)
                    sp.dma_start(fz[:], x1_rows[0:L, :].rearrange("(t p) d -> p t d", p=P)).then_inc(x1_in, 16)

            @block.gpsimd
            def _(pool):
                link = Chain(pool, cst)
                identity_tile(nc, pool, ident, id0, id1)
                pool.wait_ge(id1, 1)
                link(nc.gpsimd.memset(mhalf[:], -0.5))
                link(nc.gpsimd.memset(ones[:], 1.0))
                link(nc.gpsimd.affine_select(out=last[:], in_=ones[:], compare_op=ALU.is_ge, fill=0.0, base=1 - P,
                                             pattern=[[0, P]], channel_multiplier=1))
                link(nc.gpsimd.affine_select(out=nottok0[:], in_=ones[:, 0:1], compare_op=ALU.is_gt, fill=0.0, base=0,
                                             pattern=[[0, 1]], channel_multiplier=1))
                link(nc.gpsimd.memset(level[:], 1))
                for lv in range(LEVELS - 1):
                    half, blocks = 1 << lv, P // (2 << lv)
                    m = level[:, lv, :].rearrange("p (m n) -> p m n", n=half)
                    link(nc.gpsimd.affine_select(out=m, in_=m, compare_op=ALU.is_ge, fill=0.0, base=-half,
                                                 pattern=[[-2 * half, blocks], [0, half]], channel_multiplier=1))
                    link(nc.gpsimd.affine_select(out=m, in_=m, compare_op=ALU.is_gt, fill=0.0, base=2 * half,
                                                 pattern=[[2 * half, blocks], [0, half]], channel_multiplier=-1))
                link(nc.gpsimd.memset(get_at[:, :, B * TT:], 0))
                link(nc.gpsimd.memset(weight[:, :, B * TT:], 0.0))
                nc.gpsimd.tensor_copy(id4[:], ident[:].unsqueeze(1).broadcast_to([P, DH, P])).then_inc(ready, 1)
                pool.nop().then_inc(x3_free, 1)

                def gather_rows(b):
                    for u in range(TT):
                        nc.gpsimd.tensor_copy(ix[u][:], get_at[:, :, bass.ds(b * TT + u, 1)].rearrange("p k a -> p (k a)")
                                              ).then_inc(ix_ready, 1)
                    pool.wait_ge(ix_ready, b * TT + TT)
                    pool.sem_inc(gather, 1)
                    for u in range(TT):
                        for k in range(TOPK):
                            nc.gpsimd.indirect_dma_start(got[u][k][:], None, slots_out, bass.IndirectOffsetOnAxis(
                                ap=ix[u][:, k:k + 1], axis=0)).then_inc(got_in, 16)

                def power(b, src, out, gate, gate_n, name, width):
                    wait, _ = waiter(pool, b)
                    wait(gate, gate_n)
                    nc.gpsimd.tensor_tensor(out, src, mhalf[:, 0:width], ALU.pow).then_inc(s[name], 1)

                def norms(b):
                    power(b, var[0][:], rstd[0][:], "ln_var", 1, "ln_rstd", TT)
                    power(b, var[0][:], rstd[0][:], "ln_var", 2, "ln_rstd", TT)
                    pool.wait_ge(got_used, b + 1)
                    gather_rows(b + 1)
                    power(b, ss[:], ss[:], "ssv", 1, "ssr", TT)

                def unit_qk(b):
                    power(b, ssq[:], ssq[:], "l2v", 1, "l2r", 32)

                gather_rows(0)
                norms(0)
                unit_qk(0)
                norms(1)
                with pool.Fori(0, B) as b:
                    wait, done = waiter(pool, b)
                    dst = x3_rows[bass.ds(b * L, L), :].rearrange("(t p) d -> p t d", p=P)
                    unit_qk(b + 1)
                    power(b, ov[:], orr[:], "ov", 1, "orr", G)
                    norms(b + 2)
                    power(b, var[1][:], rstd[1][:], "tl_var", 1, "tl_rstd", TT)
                    power(b, var[1][:], rstd[1][:], "tl_var", 2, "tl_rstd", TT)
                    wait("x3", 1)
                    pool.dma_start(dst, x3[:]).then_inc(stored, 16)
                    pool.wait_ge(stored, b * 16 + 16)
                    pool.nop().then_inc(x3_free, 1)
                pool.wait_ge(got_in, (B + 3) * TT * TOPK * 16)

            @block.vector
            def _(dve):
                dve.nop().then_inc(x1_free, 1)
                v = nc.vector
                tt, stt, ts = v.tensor_tensor, v.scalar_tensor_tensor, v.tensor_scalar
                dve.wait_ge(w_in, 16 * 20)
                dve.wait_ge(ready, 1)
                wo_link = Chain(dve, aprep, 1)
                dve.wait_ge(aprep, 1)
                wo_link(ts(nexpA[:], nexpA[:], -1.0, None, ALU.mult))
                wo_link(ts(flat(wo_s[:]), flat(wo_s[:]), onw[:, 0:1], None, ALU.mult))
                token_wide = lambda w: w[:].unsqueeze(1).broadcast_to([P, TT, D])

                def spread(link, src, part):
                    row_spread(nc, link, src, stats[part], agg[part], var[part], TT, s[("ln_var", "tl_var")[part]], hold)

                def norm(b, link, src, dst, part, n, name):
                    _, done = waiter(dve, b)
                    dve.wait_ge(s[("ln_rstd", "tl_rstd")[part]], b * 2 + n)
                    ins = row_scale(nc, src, dst, agg[part], rstd[part], TT)
                    link(ins) if name is None else done(name, 1, ins)

                def front(k, b, link):
                    wait, done = waiter(dve, b)
                    if k == 0:
                        dve.wait_ge(x1_in, b * 16 + 16)
                        dve.wait_ge(got_in, (b + 1) * (TT * TOPK * 16))
                        for k in range(TOPK):
                            for u in range(TT):
                                ins = stt(fz[:, u, :], got[u][k][:], weight[:, k, bass.ds(b * TT + u, 1)],
                                          fz[:, u, :], ALU.mult, ALU.add)
                            link(ins)
                        dve.sem_inc(got_used, 1)
                        spread(link, fz, 0)
                    elif k == 1:
                        norm(b, link, fz, xn, 0, 1, None)
                        spread(link, xn, 0)
                    elif k == 2:
                        norm(b, link, xn, fz, 0, 2, None)
                        link(tt(fz[:], fz[:], token_wide(g1), ALU.mult))
                        done("u", 1, tt(fz[:], fz[:], token_wide(b1), ALU.add))
                    elif k == 4:
                        wait("ss", 1)
                        done("ssv", 1, ts(ss[:], ss[:], 1.0 / D, RMS_EPS, ALU.mult, ALU.add))
                    elif k == 5:
                        wait("ssr", 1)
                        for t in range(TT):
                            ins = ts(fz[:, t, :], fz[:, t, :], ss[:, t:t + 1], None, ALU.mult)
                        done("h", 1, ins)
                    elif 6 <= k < 6 + NP_:
                        n = k - 6
                        wait("tap", n + 1)
                        if n == 0:
                            dve.sem_inc(x1_free, 1)
                        for d in range(1, 4):
                            ins = stt(y[:, n % 4, d:L], bank[6 + n % 2][:, 0:L - d], cw[:, n, 3 - d:4 - d], y[:, n % 4, d:L], ALU.mult, ALU.add)
                            if d < 3:
                                link(ins)
                        done("cv", n + 1, ins)
                    elif k == 15:
                        wait("te", NP_)
                        link(tt(sq3, qk3, qk3, ALU.mult))
                        link(v.tensor_reduce(ssq[:].rearrange("p (t g) -> p t g", t=TT), sq3, AX_X, ALU.add))
                        done("l2v", 1, ts(ssq[:], ssq[:], 1.0, RMS_EPS, ALU.mult, ALU.add))
                        wait("ab_ps", 1)
                        ab = bank[6][:, 0:TT * 2 * DH].rearrange("p (t n) -> p t n", t=TT)
                        link(tt(t1[:], ab[:, :, 0:DH], dtb[:].unsqueeze(1).broadcast_to([P, TT, DH]), ALU.add))
                        done("ab", 1, v.tensor_copy(bt[:], ab[:, :, DH:2 * DH]))
                    elif k == 16:
                        wait("abs", 2)
                        link(ts(zr[:], sp_[:], 2.0, None, ALU.add))
                        link(v.reciprocal(zr[:], zr[:]))
                        link(tt(zr[:], sp_[:], zr[:], ALU.mult))
                        link(tt(z2[:], zr[:], zr[:], ALU.mult))
                        link(ts(sp_[:], z2[:], 1.0 / 13.0, None, ALU.mult))
                        for odd in (11, 9, 7, 5, 3):
                            link(stt(sp_[:], sp_[:], 1.0 / odd, z2[:], ALU.add, ALU.mult))
                        link(stt(sp_[:], sp_[:], 1.0, zr[:], ALU.add, ALU.mult))
                        link(ts(t1[:], t1[:], 0.0, None, ALU.max))
                        link(stt(sp_[:], sp_[:], 2.0, t1[:], ALU.mult, ALU.add))
                        done("g_in", 1, tt(sp_[:], sp_[:], nexpA[:].unsqueeze(1).broadcast_to([P, TT, DH]), ALU.mult))
                    elif k == 18:
                        wait("a", 1)
                        done("am", 1, ts(am[:], a_[:], nottok0[:, 0:1], None, ALU.mult))
                        wait("l2r", 1)
                        sq4 = ssq[:].rearrange("p (t a h) -> p t a h", t=TT, a=2)
                        link(ts(sq4[:, :, 0, :], sq4[:, :, 0, :], float(KD) ** -0.5, None, ALU.mult))
                        link(tt(qk3, qk3, ssq[:].rearrange("p (t g) -> p t g", t=TT).unsqueeze(3).broadcast_to([P, TT, 2 * DH, KD]), ALU.mult))
                        wait("beta", 1)
                        done("qk", 1, tt(kb[:], qk[:, :, 1, :, :], bt[:].unsqueeze(3).broadcast_to([P, TT, DH, KD]), ALU.mult))
                    elif k == FRONT_SLOTS - 1:
                        done("vb", 1, tt(v_[:], vn[:], bt[:].unsqueeze(3).broadcast_to([P, TT, DH, VD]), ALU.mult))

                qk3 = qk[:].rearrange("p t a h d -> p t (a h) d")
                sq3 = sq[:].rearrange("p t (g d) -> p t g d", d=KD)
                first_link = Chain(dve, front_step, 0)
                for k in range(FRONT_SLOTS):
                    front(k, 0, first_link)
                assert first_link.n == FSTEPS, first_link.n
                def chunk(t, part, b):
                    wait, done = waiter(dve, b)
                    if part == 0:
                        wait("ks", t + 1)
                        for h in range(DH):
                            ins = stt(R[:, h, :], bank[4][:, h * VD:(h + 1) * VD], gbn[t][:, h:h + 1], v_[:, t, h, :], ALU.mult, ALU.add)
                        done("R", t + 1, ins)
                    elif part == 2:
                        wait("su", t + 1)
                        for h in range(DH):
                            p, k, r = h // 2, h % 2, slice((h % 2) * KD, (h % 2 + 1) * KD)
                            ins = stt(S[r, p, k, :], S[r, p, k, :], gC[t][r, h:h + 1], bank[4][r, p * VD:(p + 1) * VD], ALU.mult, ALU.add)
                        done("S", t + 2, ins)
                        wait("op", t + 1)
                        done("o", t + 1, tt(heads(o[:, t, :]), heads(bank[5][:]), QSe[:], ALU.add))

                def invert(pair, b, link, aside):
                    wait, done = waiter(dve, b)
                    two = (2 * pair, 2 * pair + 1)
                    for t in two:
                        i = t % 2
                        wait("aB", t + 1)
                        done("DT", t + 1, v.tensor_tensor_scan(flat(DT_[i][:]), bank[4 + i][:], flat(id4[:]), 0.0, ALU.mult, ALU.add))
                    for t in two:
                        i = t % 2
                        wait("kk", t + 1)
                        for k in range(2):
                            products = bank[2 * i + k][:].rearrange("p (w n j) -> p w n j", w=2, n=H2)
                            stt(nAT[i][:, k::2, :], products[:, 0, :, :], -1.0, DT_[i][:, k::2, :], ALU.mult, ALU.mult)
                            ins = tt(QD[t][:, k::2, :], products[:, 1, :, :], DT_[i][:, k::2, :], ALU.mult)
                        done("qd", t + 1, ins)
                    for t in two:
                        i = t % 2
                        wait("gm", t + 1)
                        done("gmr", t + 1, v.tensor_copy(gam[t][:], bank[4 + i][:, 0:DH]))
                        stt(gbn[t][:], gam[t][:], -1.0, bt[:, t, :], ALU.mult, ALU.mult)
                        link(tt(kd[:, t, :, :], kd[:, t, :, :], DT_[i][:, :, P - 1:P].broadcast_to([P, DH, KD]), ALU.mult))
                    for t in two:
                        wait("gc", t + 1)
                        done("prep", t + 1, v.tensor_copy(gC[t][:], bank[4 + t % 2][:, 8:8 + DH]))
                    aside(0)
                    for lv in range(LEVELS):
                        for t in two:
                            i, half = t % 2, 1 << lv
                            wait("z", turn_of(t, lv, LEVELS))
                            z = bank[2 * i + 1][:, DH * HP:].rearrange("p (h c) -> p h c", h=DH)
                            if lv == LEVELS - 1:
                                done("Uf", t + 1, v.tensor_copy(U[t][0:HP, :, HP:P], z[0:HP, :, :]))
                                continue
                            if lv == 0:
                                wait("rst", t + 1)
                            v.memset(hold[:], 0.0)
                            first = T[i][:].rearrange("p h (m k n) -> p h m k n", k=2, n=half)[:, :, :, 0, :]
                            mask = level[:, lv, :].rearrange("p (m n) -> p m n", n=half).unsqueeze(1)
                            done("T", turn_of(t, lv), v.copy_predicated(first, mask.broadcast_to([P, DH, HP // half, half]),
                                                                       z.rearrange("p h (m n) -> p h m n", n=half)))
                        for t, part in CHUNK_PARTS[lv] if pair else ():
                            chunk(t, part, b)
                        aside(1 + lv)

                def begin(b, link):
                    _, done = waiter(dve, b)
                    link(v.tensor_copy(x2_next[:], xn[:]))
                    done("S", 1, v.memset(S[:].rearrange("p a b c -> p (a b c)"), 0.0))
                    done("kcopy", 1, v.tensor_copy(kd[:], qk[:, :, 1, :, :]))

                def tail(n, b, link):
                    wait, done = waiter(dve, b)
                    if n == 0:
                        wait("osq", TT)
                        done("ov", 1, ts(ov[:], ov[:], 1.0 / VD, RMS_EPS, ALU.mult, ALU.add))
                        wait("gt", TT)
                        link(tt(flat(o[:]), flat(o[:]), flat(gt[:]), ALU.mult))
                    elif n == 1:
                        wait("orr", 1)
                        by_head = o[:].rearrange("p t (h d) -> p (t h) d", h=DH)
                        done("og", 1, tt(by_head, by_head, orr[:].unsqueeze(2).broadcast_to([P, G, VD]), ALU.mult))
                    elif n == 5:
                        for p in range(2):
                            wait("en", p + 1)
                            ins = tt(flat(xa[:, 2 * p:2 * p + 2, :]), bank[4 + p][:], flat(x2[:, 2 * p:2 * p + 2, :]), ALU.add)
                            link(ins) if p == 0 else done("xa", 1, ins)
                        spread(link, xa, 1)
                    elif n == 6:
                        norm(b, link, xa, n1, 1, 1, "n2")
                        link(tt(xa[:], xa[:], x2[:], ALU.add))
                        link(v.tensor_copy(x2[:], x2_next[:]))
                    elif n == 7:
                        for p in range(2):
                            wait("y2", p + 1)
                            ins = tt(h_[:, 2 * p:2 * p + 2, :], bank[4 + p][:].rearrange("p (t d) -> p t d", t=2),
                                     b2_s[:].unsqueeze(1).broadcast_to([P, 2, D]), ALU.add)
                            link(ins) if p == 0 else done("yb", 1, ins)
                    elif n == 8:
                        wait("ge", 1)
                        link(tt(n1[:], h_[:], xa[:], ALU.add))
                        spread(link, n1, 1)
                        dve.wait_ge(x3_free, b + 1)
                        norm(b, link, n1, x3, 1, 2, "x3")

                first, second = Chain(dve, pair_step[0], 0), Chain(dve, front_step, FSTEPS)
                begin(0, first)
                wo_link(v.tensor_copy(x2[:], x2_next[:]))
                invert(0, 0, first, lambda n: front(slot_of(0, n), 1, second))
                split = second.n
                assert first.n == PSTEPS[0], first.n
                with dve.Fori(0, B) as b:
                    link = Chain(dve, pair_step[1], b * PSTEPS[1])
                    front_link = Chain(dve, front_step, (b + 1) * FSTEPS)
                    front_link.n = split
                    invert(1, b, link, lambda n: front(slot_of(1, n), b + 1, front_link))
                    for t in (2, 3):
                        for part in range(3):
                            chunk(t, part, b)
                            if t == 2:
                                front(slot_of(2, part), b + 1, front_link)
                    front(FRONT_SLOTS - 1, b + 1, front_link)
                    assert (link.n, front_link.n) == (PSTEPS[1], FSTEPS), (link.n, front_link.n)
                    link = Chain(dve, pair_step[0], (b + 1) * PSTEPS[0])
                    tail_link = Chain(dve, tail_step, b * TSTEPS)
                    front_link = Chain(dve, front_step, (b + 2) * FSTEPS)

                    def aside(n):
                        tail(n, b, tail_link)
                        front(slot_of(0, n), b + 2, front_link)

                    begin(b + 1, link)
                    invert(0, b + 1, link, aside)
                    tail(8, b, tail_link)
                    assert (link.n, tail_link.n) == (PSTEPS[0], TSTEPS), (link.n, tail_link.n)

            @block.scalar
            def _(act):
                act.wait_ge(w_in, 16 * 20)
                nc.scalar.activation(nexpA[:], nexpA[:], ACT.Exp).then_inc(aprep, 1)
                a_op = nc.scalar.activation
                act.wait_ge(aprep, 1)


                def front(k, b):
                    wait, done = waiter(act, b)
                    if k == 3:
                        wait("u", 1)
                        for t in range(TT):
                            ins = a_op(sq[:, t, 0:D], fz[:, t, :], ACT.Square, accum_out=ss[:, t:t + 1])
                        done("ss", 1, ins)
                    elif k == 5:
                        wait("hT_ps", 1)
                        for c in range(DT):
                            done("hT", c + 1, a_op(hT[:, c, :], bank[6 + c][:], ACT.Copy, scale=rw[:, c:c + 1]))
                    elif 6 <= k < 7 + NP_:
                        n = k - 6
                        if n > 0:
                            wait("cv", n)
                            done("si", n, a_op(y[:, (n - 1) % 4, :], y[:, (n - 1) % 4, :], ACT.Silu))
                        if n < NP_:
                            wait("pj", n + 1)
                            done("tap", n + 1, a_op(y[:, n % 4, :], bank[6 + n % 2][:], ACT.Copy, scale=cw[:, n, 3:4]))
                        if n > 0:
                            m = n - 1
                            wait("tk", m + 1)
                            src = bank[6 + m % 2][:].rearrange("p (t c) -> p t c", t=TT)
                            if m < 4:
                                dst = qk[:, :, m // 2, 2 * (m % 2):2 * (m % 2) + 2, :].rearrange("p t h d -> p t (h d)")
                            else:
                                dst = vn[:, :, m - 4, :]
                            done("te", m + 1, nc.scalar.copy(dst, src))
                    elif k == 15:
                        wait("ab", 1)
                        done("beta", 1, a_op(bt[:], bt[:], ACT.Sigmoid))
                        done("abs", 1, a_op(sp_[:], t1[:], ACT.Abs))
                        done("abs", 2, a_op(sp_[:], sp_[:], ACT.Exp, scale=-1.0))
                    elif k == 17:
                        wait("g_in", 1)
                        done("a", 1, a_op(a_[:], sp_[:], ACT.Exp))
                    elif k == FRONT_SLOTS - 1:
                        for n in range(6):
                            wait("bk", n + 1)
                            done("qkT", n + 1, nc.scalar.copy(XT[:, n, :], bank[6 + n % 2][:]))
                    elif k == FRONT_SLOTS:
                        for t in range(TT):
                            wait("gp", t + 1)
                            done("gt", t + 1, a_op(gt[:, t, :], bank[6 + t % 2][:], ACT.Silu))

                for k in range(FRONT_SLOTS + 1):
                    front(k, 0)
                def squares(t, b):
                    _, done = waiter(act, b)
                    for h in range(DH):
                        ins = a_op(scr[:, h * VD:(h + 1) * VD], o[:, t, h * VD:(h + 1) * VD], ACT.Square,
                                   accum_out=ov[:, t * DH + h:t * DH + h + 1])
                    done("osq", t + 1, ins)

                def chunk(t, part, b):
                    wait, done = waiter(act, b)
                    if part == 0:
                        wait("ks", t + 1)
                        if t > 0:
                            wait("o", t)
                        for h in range(DH):
                            ins = a_op(QSe[:, h, :], bank[5][:, h * VD:(h + 1) * VD], ACT.Copy, scale=gam[t][:, h:h + 1])
                        done("qse", t + 1, ins)
                    elif part == 1:
                        wait("dl", t + 1)
                        done("de", t + 1, nc.scalar.copy(dl[:], heads(bank[4][:])))
                        if t > 0:
                            squares(t - 1, b)

                def invert(pair, b, aside):
                    wait, done = waiter(act, b)
                    two = (2 * pair, 2 * pair + 1)
                    for t in two:
                        nc.scalar.copy(T[t % 2][:], id4[:]).then_inc(s["rst"], 1)
                    aside(0)
                    for lv in range(LEVELS):
                        for t in two:
                            i, n = t % 2, turn_of(t, lv - 1)
                            if lv > 0:
                                wait("ut", n)
                                done("U", n, nc.scalar.copy(U[t][:], heads(bank[2 * i][:])))
                                wait("y", n)
                                done("Ye", n, nc.scalar.copy(Y[i][:], bank[2 * i + 1][:, 0:DH * HP].rearrange("p (h c) -> p h c", h=DH)))
                        for t, part in CHUNK_PARTS[lv] if pair else ():
                            chunk(t, part, b)
                        aside(1 + lv)

                def tail(n, b):
                    wait, done = waiter(act, b)
                    if n == 2:
                        wait("og", 1)
                        front(FRONT_SLOTS, b + 1)
                    if n in (2, 3):
                        for c in (2 * n - 4, 2 * n - 3):
                            wait("oT", c + 1)
                            done("oTe", c + 1, nc.scalar.copy(y[:, c, :], bank[4 + c % 2][:]))
                    elif n == 6:
                        wait("n2T", 1)
                        for c in range(DT):
                            done("h2T", c + 1, a_op(h2T[:, c, :], bank[4 + c][:], ACT.Identity, scale=g2[:, c:c + 1], bias=bb2[:, c:c + 1]))
                    elif n == 7:
                        wait("yb", 1)
                        done("ge", 1, a_op(flat(h_[:]), flat(h_[:]), ACT.Gelu))

                invert(0, 0, lambda n: front(slot_of(0, n), 1))
                with act.Fori(0, B) as b:
                    wait, _ = waiter(act, b)
                    invert(1, b, lambda n: front(slot_of(1, n), b + 1))
                    for t in (2, 3):
                        for part in range(3):
                            chunk(t, part, b)
                            if t == 2:
                                front(slot_of(2, part), b + 1)
                    wait("o", TT)
                    squares(TT - 1, b)
                    front(FRONT_SLOTS - 1, b + 1)

                    def aside(n):
                        tail(n, b)
                        front(slot_of(0, n), b + 2)

                    invert(0, b + 1, aside)

            @block.tensor
            def _(pe):
                pe.wait_ge(w_in, 16 * 20)
                pe.wait_ge(ready, 1)
                pe.wait_ge(aprep, 3)
                mm, tp = nc.tensor.matmul, nc.tensor.transpose

                def turn(b, src, at, name):
                    for c in range(DT):
                        for t in range(TT):
                            ins = tp(bank[at + c][:, t * P:(t + 1) * P], src[:, t, c * P:(c + 1) * P], ident[:])
                    ins.then_inc(s[name], 1)

                def front(k, b, first=False):
                    wait, _ = waiter(pe, b)

                    def mark(name, ins):
                        ins.then_inc(s[name], 1)

                    if k == 5:
                        wait("h", 1)
                        if not first:
                            pe.wait_ge(s["gt"], b * TT)
                        turn(b, fz, 6, "hT_ps")
                    elif 6 <= k < 7 + NP_:
                        n = k - 6
                        if n < NP_:
                            wait("hT", 2) if n < 2 else wait("te", n - 1)
                            for c in range(DT):
                                ins = mm(bank[6 + n % 2][:], wqkv[:, c, n * P:(n + 1) * P], hT[:, c, :], start=(c == 0), stop=(c == DT - 1))
                            mark("pj", ins)
                        if n > 0:
                            m = n - 1
                            wait("si", m + 1)
                            for t in range(TT):
                                ins = tp(bank[6 + m % 2][:, t * P:(t + 1) * P], y[:, m % 4, t * P:(t + 1) * P], ident[:])
                            mark("tk", ins)
                    elif k == 15:
                        wait("te", NP_)
                        for t in range(TT):
                            for c in range(DT):
                                ins = mm(bank[6][:, t * 2 * DH:(t + 1) * 2 * DH], hT[:, c, t * P:(t + 1) * P], wab[:, c, :],
                                         start=(c == 0), stop=(c == DT - 1))
                        mark("ab_ps", ins)
                    elif k == FRONT_SLOTS - 1:
                        wait("qk", 1)
                        for n in range(6):
                            if n >= 2:
                                wait("qkT", n - 1)
                            for t in range(TT):
                                src = (kb[:, t, :, :] if n >= 4 else qk[:, t, n // 2, :, :])[:, 2 * (n % 2):2 * (n % 2) + 2, :]
                                ins = tp(bank[6 + n % 2][:, t * P:(t + 1) * P], flat(src), ident[:])
                            mark("bk", ins)

                def gates(half, b):
                    wait, _ = waiter(pe, b)
                    for t in (2 * half, 2 * half + 1):
                        wait("qkT", 5 + t) if t < 2 else wait("gt", t - 1)
                        for c in range(DT):
                            ins = mm(bank[6 + t % 2][:], hT[:, c, t * P:(t + 1) * P], wg_s[:, c, :], start=(c == 0), stop=(c == DT - 1))
                        ins.then_inc(s["gp"], 1)

                for k in range(FRONT_SLOTS):
                    front(k, 0, first=True)
                gates(0, 0)
                gates(1, 0)
                tokens = lambda t: slice(t * P, (t + 1) * P)

                def chunk(t, part, b):
                    wait, _ = waiter(pe, b)

                    def mark(name, ins):
                        ins.then_inc(s[name], 1)

                    if part == 0:
                        wait("S", t + 1)
                        if t == 0:
                            wait("vb", 1)
                        for n in range(H2):
                            mm(bank[4][:, 2 * n * VD:2 * (n + 1) * VD], XT[:, 2 + n, tokens(t)], flat(S[:, n, :, :]), start=True, stop=True)
                        if t > 0:
                            wait("o", t)
                        for n in range(H2):
                            ins = mm(bank[5][:, 2 * n * VD:2 * (n + 1) * VD], XT[:, n, tokens(t)], flat(S[:, n, :, :]), start=True, stop=True)
                        mark("ks", ins)
                    elif part == 1:
                        wait("Uf", t + 1)
                        wait("R", t + 1)
                        for h in range(DH):
                            ins = mm(bank[4][:, h * VD:(h + 1) * VD], U[t][:, h, :], R[:, h, :], start=True, stop=True)
                        mark("dl", ins)
                    else:
                        wait("de", t + 1)
                        for h in range(DH):
                            r = slice((h % 2) * KD, (h % 2 + 1) * KD)
                            ins = mm(bank[4][r, (h // 2) * VD:(h // 2 + 1) * VD], kd[:, t, h, :], dl[:, h, :], start=True, stop=True)
                        mark("su", ins)
                        wait("qse", t + 1)
                        for h in range(DH):
                            ins = mm(bank[5][:, h * VD:(h + 1) * VD], QD[t][:, h, :], dl[:, h, :], start=True, stop=True)
                        mark("op", ins)

                def invert(pair, b, aside):
                    wait, _ = waiter(pe, b)

                    def mark(name, ins):
                        ins.then_inc(s[name], 1)

                    if pair == 0:
                        wait("qkT", 6)
                        wait("kcopy", 1)
                    two = (2 * pair, 2 * pair + 1)
                    for t in two:
                        wait("am", 1)
                        for h in range(DH):
                            ins = mm(bank[4 + t % 2][:, h * P:(h + 1) * P], am[:, t, h:h + 1].broadcast_to([P, P]), ident[:],
                                     start=True, stop=True)
                        mark("aB", ins)
                    for t in two:
                        if pair:
                            wait("Uf", t - 1)
                        for h in range(DH):
                            r, n, dst = slice((h % 2) * KD, (h % 2 + 1) * KD), h // 2, bank[2 * (t % 2) + h % 2]
                            mm(dst[:, n * P:(n + 1) * P], XT[r, 2 + n, tokens(t)], XT[r, 4 + n, tokens(t)], start=True, stop=True)
                            ins = mm(dst[:, (2 + n) * P:(3 + n) * P], XT[r, 2 + n, tokens(t)], XT[r, n, tokens(t)], start=True, stop=True)
                        mark("kk", ins)
                    for t in two:
                        wait("DT", t + 1)
                        for h in range(DH):
                            ins = mm(bank[4 + t % 2][:, h:h + 1], DT_[t % 2][0:1, h, :], a_[0:1, t, h:h + 1], start=True, stop=True)
                        mark("gm", ins)
                    for t in two:
                        wait("gmr", t + 1)
                        mark("gc", mm(bank[4 + t % 2][:, 8:8 + DH], last[:], gam[t][:], start=True, stop=True))
                    aside(0)
                    for lv in range(LEVELS):
                        half = 1 << lv
                        in_blocks = lambda x: x.rearrange("p (m n) -> p m n", n=half)
                        for t in two:
                            i = t % 2
                            if lv == 0:
                                wait("qd", t + 1)
                                for h in range(DH):
                                    ins = mm(bank[2 * i + 1][:, (DH + h) * HP:(DH + h + 1) * HP], nAT[i][:, h, :], ident[:, 0:P:2],
                                             start=True, stop=True)
                                mark("z", ins)
                                continue
                            wait("T", turn_of(t, lv - 1))
                            for h in range(DH):
                                ins = tp(bank[2 * i][:, h * P:(h + 1) * P], T[i][:, h, :], ident[:])
                            mark("ut", ins)
                            for h in range(DH):
                                first = T[i][:, h, :].rearrange("p (m k n) -> p m k n", k=2, n=half)[:, :, 0, :]
                                ins = mm(in_blocks(bank[2 * i + 1][:, h * HP:(h + 1) * HP]), nAT[i][:, h, :], first, start=True, stop=True)
                            mark("y", ins)
                        if lv > 0:
                            for t in two:
                                i = t % 2
                                wait("U", turn_of(t, lv - 1))
                                wait("Ye", turn_of(t, lv - 1))
                                for h in range(DH):
                                    z = slice((DH + h) * HP, (DH + h + 1) * HP)
                                    if lv < LEVELS - 1:
                                        ins = mm(bank[2 * i + 1][:, z], U[t][:, h, :], Y[i][:, h, :], start=True, stop=True)
                                    else:
                                        ins = mm(bank[2 * i + 1][0:HP, z], Y[i][:, h, :], U[t][:, h, HP:P], start=True, stop=True)
                                mark("z", ins)
                        for t, part in CHUNK_PARTS[lv] if pair else ():
                            chunk(t, part, b)
                        aside(1 + lv)

                def tail(n, b):
                    wait, _ = waiter(pe, b)

                    def mark(name, ins):
                        ins.then_inc(s[name], 1)

                    if n in (1, 2):
                        gates(n - 1, b + 1)
                    if n in (2, 3):
                        wait("og", 1)
                        for c in (2 * n - 4, 2 * n - 3):
                            if c >= 2:
                                wait("oTe", c - 1)
                            for t in range(TT):
                                ins = tp(bank[4 + c % 2][:, t * P:(t + 1) * P], o[:, t, c * P:(c + 1) * P], ident[:])
                            mark("oT", ins)
                    elif n == 4:
                        wait("oTe", DH)
                        for t in range(TT):
                            for c in range(DH):
                                ins = mm(bank[4 + t // 2][:, (t % 2) * D:(t % 2 + 1) * D], y[:, c, tokens(t)], wo_s[:, c, :],
                                         start=(c == 0), stop=(c == DH - 1))
                            if t % 2:
                                mark("en", ins)
                    elif n == 6:
                        wait("n2", 1)
                        turn(b, n1, 4, "n2T")
                    elif n == 7:
                        wait("h2T", 2)
                        for t in range(TT):
                            for c in range(DT):
                                ins = mm(bank[4 + t // 2][:, (t % 2) * D:(t % 2 + 1) * D], h2T[:, c, tokens(t)], w2_s[:, c, :],
                                         start=(c == 0), stop=(c == DT - 1))
                            if t % 2:
                                mark("y2", ins)

                invert(0, 0, lambda n: front(slot_of(0, n), 1))
                with pe.Fori(0, B) as b:
                    invert(1, b, lambda n: front(slot_of(1, n), b + 1))
                    for t in (2, 3):
                        for part in range(3):
                            chunk(t, part, b)
                            if t == 2:
                                front(slot_of(2, part), b + 1)
                    front(FRONT_SLOTS - 1, b + 1)

                    def aside(n):
                        tail(n, b)
                        front(slot_of(0, n), b + 2)

                    pe.wait_ge(s["o"], (b + 1) * TT)
                    invert(0, b + 1, aside)
                    pe.wait_ge(s["yb"], b + 1)


INPUTS = dict(
    L0_attn_x=(B, L, D), L0_attn_conv_w=(D, 4), L0_attn_wq=(D, DK_ALL), L0_attn_wkg=(D, DK_ALL), L0_attn_wv=(D, D),
    L0_attn_wg=(D, D), L0_attn_bg=(D,), L0_attn_wout=(D, D), L0_attn_aug_balance=(DK_ALL,),
    L0_ffn_w_g=(EXPERTS, D), L0_ffn_c_fc=(EXPERTS, D, FF), L0_ffn_c_proj=(EXPERTS, FF, D),
    L1_attn_ln1_g=(D,), L1_attn_ln1_b=(D,), L1_attn_ln2_g=(D,), L1_attn_ln2_b=(D,), L1_attn_rms_in_w=(D,),
    L1_attn_Wq=(D, DH * KD), L1_attn_Wk=(D, DH * KD), L1_attn_Wv=(D, DH * VD), L1_attn_conv_q_w=(DH * KD, 4),
    L1_attn_conv_k_w=(DH * KD, 4), L1_attn_conv_v_w=(DH * VD, 4), L1_attn_Wa=(D, DH), L1_attn_dt_bias=(DH,),
    L1_attn_A_log=(DH,), L1_attn_Wb=(D, DH), L1_attn_Wg=(D, DH * VD), L1_attn_o_norm_w=(VD,), L1_attn_Wo=(DH * VD, D),
    L1_attn_W2=(D, D), L1_attn_b2=(D,),
    L1_ffn_fc1_A=(PRIM, D, RANK), L1_ffn_fc1_B=(PRIM, RANK, FF), L1_ffn_fc2_A=(PRIM, FF, RANK),
    L1_ffn_fc2_B=(PRIM, RANK, D), L1_ffn_fc1_logits=(PRIM,), L1_ffn_fc2_logits=(PRIM,))


def build_program(nc, a, out_rows):
    scratch = lambda name, rows, cols: nc.dram_tensor(name, (rows, cols), F32).ap()
    x_rows = scratch("token_rows", 2 * NTOK, D)
    x3_rows, x1_rows = x_rows[0:NTOK, :], x_rows[NTOK:2 * NTOK, :]
    logits = scratch("router_logits", NTOK, EXPERTS)
    slots, slots_out = scratch("slots", TRASH + TOPK * NTOK, D), scratch("slots_out", SLOTS, D)
    w1, w2 = scratch("ffn_w1", D, FF), scratch("ffn_w2", FF, D)

    linear_attention(nc, a["x_rows"], a["xT_rows"], *[a["L0_attn_" + n] for n in
                     ("conv_w", "wq", "wkg", "wv", "wg", "bg", "wout", "aug_balance")], a["w_gate"], x1_rows, logits)
    with ExitStack() as ctx:
        held = lambda name, ahead, dt: ctx.enter_context(nc.sbuf_tensor(name, [P, TOPK, NTOK // P + ahead * TT], dt))
        get_at, weight = held("get_at", 3, U32), held("weight", 2, F32)
        with nc.sbuf_tensor("put_at", [P, TOPK, NTOK // P], U32) as put_at:
            route(nc, logits, put_at, *[t[:, :, 0:NTOK // P] for t in (get_at, weight)], slots)
            with ExitStack() as both, nc.Block() as block:
                compose_weights(nc, both, block, a["L1_ffn_fc1_logits"], a["fc1_aT"], a["fc1_b"],
                                a["L1_ffn_fc2_logits"], a["fc2_aT"], a["fc2_b"], w1, w2)
                dispatch(nc, both, block, x1_rows, put_at, slots)
        mlp(nc, slots, a["moe_w1"], a["moe_w2"], slots_out, EXPERTS, CAP // BLK, False)
        delta_rule(nc, x1_rows, slots_out, get_at, weight, *[a["L1_attn_" + n] for n in
                   ("ln1_g", "ln1_b", "rms_in_w", "Wq", "Wk", "Wv", "conv_q_w", "conv_k_w", "conv_v_w", "Wa", "dt_bias",
                    "A_log", "Wb", "Wg", "o_norm_w", "Wo", "ln2_g", "ln2_b", "W2", "b2")], x3_rows)
    mlp(nc, x_rows[0:NTOK + BLK, :], w1, w2, out_rows, 1, NTOK // BLK, True)


def kernel(**inputs):
    import concourse.bacc as bacc
    import numpy as np
    from concourse.bass_utils import run_bass_kernel_spmd

    rows = lambda v: np.ascontiguousarray(v).reshape(-1, v.shape[-1])
    given = {name: np.asarray(inputs[name]) for name in INPUTS}
    for name, shape in INPUTS.items():
        assert given[name].shape == shape, name
    take = given.pop
    x = take("L0_attn_x")
    laid = dict(x_rows=rows(x), xT_rows=rows(x.transpose(0, 2, 1)), w_gate=rows(take("L0_ffn_w_g").T),
                moe_w1=rows(take("L0_ffn_c_fc")), moe_w2=rows(take("L0_ffn_c_proj")),
                fc1_aT=rows(take("L1_ffn_fc1_A").transpose(0, 2, 1)), fc1_b=rows(take("L1_ffn_fc1_B")),
                fc2_aT=rows(take("L1_ffn_fc2_A").transpose(0, 2, 1)), fc2_b=rows(take("L1_ffn_fc2_B")))
    laid.update({name: np.ascontiguousarray(v) for name, v in given.items()})

    nc = bacc.Bacc("TRN2", target_bir_lowering=False, num_devices=1)
    aps = {name: nc.dram_tensor(f"in_{name}", v.shape, F32, kind="ExternalInput").ap() for name, v in laid.items()}
    out_rows = nc.dram_tensor("out_rows", (NTOK, D), F32, kind="ExternalOutput").ap()
    build_program(nc, aps, out_rows)
    r = run_bass_kernel_spmd(nc, [{f"in_{name}": v for name, v in laid.items()}], core_ids=[0])
    return r.results[0]["out_rows"].reshape(B, L, D)
```
